# Optimizing a Trainium2 kernel written in Bass

```python
import numpy as np
import jax
import jax.numpy as jnp

def _softmax(x, axis=-1):
    return jax.nn.softmax(x, axis=axis)

def _gelu(x):
    return jax.nn.gelu(x, approximate=True)

def _silu(x):
    return jax.nn.silu(x)

def _sigmoid(x):
    return jax.nn.sigmoid(x)

def _layernorm(x, axis=-1, eps=1e-05):
    m = jnp.mean(x, axis=axis, keepdims=True)
    v = jnp.var(x, axis=axis, keepdims=True)
    return (x - m) / jnp.sqrt(v + eps)

def _scatter_add(tgt, idx, src, axis=0):
    return tgt.at[idx].add(src)

def _segment_sum(src, seg, n):
    return jax.ops.segment_sum(src, seg, n)
kernel_name = 'mk_sandwich_d2_jaxref_r8_0c69f5'

def setup_inputs(seed: int=0):
    np.random.seed(seed)
    _w = jnp.asarray

    def _L0_attn_setup():
        import jax, jax.numpy as jnp
        import numpy as np
        D_MODEL = 128
        EXPAND = 2
        D_INNER = EXPAND * D_MODEL
        D_STATE = 64
        NGROUPS = 1
        HEADDIM = 128
        NHEADS = D_INNER // HEADDIM
        D_CONV = 4
        CONV_DIM = D_INNER + 2 * NGROUPS * D_STATE
        D_IN_PROJ = 2 * D_INNER + 2 * NGROUPS * D_STATE + NHEADS
        BATCH = 2
        SEQLEN = 512
        RMS_EPS = 1e-05
        key = jax.random.key(seed)
        ks = jax.random.split(key, 8)
        u = jax.random.normal(ks[0], (BATCH, SEQLEN, D_MODEL), jnp.float32)
        in_proj_w = jax.random.normal(ks[1], (D_IN_PROJ, D_MODEL), jnp.float32) * 0.02
        conv_w = jax.random.normal(ks[2], (CONV_DIM, D_CONV), jnp.float32) * 0.2
        conv_b = jax.random.normal(ks[3], (CONV_DIM,), jnp.float32) * 0.1
        dt_bias = jax.random.normal(ks[4], (NHEADS,), jnp.float32) * 0.5
        A_log = jnp.log(jax.random.uniform(ks[5], (NHEADS,), jnp.float32, 1.0, 16.0))
        D = jnp.ones((NHEADS,), jnp.float32)
        rms_w = jnp.ones((D_INNER,), jnp.float32)
        out_w = jax.random.normal(ks[6], (D_MODEL, D_INNER), jnp.float32) * 0.02
        return {'u': u, 'in_proj_w': in_proj_w, 'conv_w': conv_w, 'conv_b': conv_b, 'dt_bias': dt_bias, 'A_log': A_log, 'D': D, 'rms_w': rms_w, 'out_w': out_w}
    _L0_attn_in = _L0_attn_setup()

    def _L0_ffn_setup():
        import jax, jax.numpy as jnp
        import numpy as np
        D = 128
        H = 512
        E = 12
        K = 3
        B, S = (1, 256)
        key = jax.random.key(seed)
        ks = jax.random.split(key, 6)
        scale = 0.02
        x = jax.random.normal(ks[0], (B, S, D), dtype=jnp.float32)
        Wg = jax.random.normal(ks[1], (D, E), dtype=jnp.float32) * scale
        Wup = jax.random.normal(ks[2], (E, D, H), dtype=jnp.float32) * scale
        bup = jax.random.normal(ks[3], (E, H), dtype=jnp.float32) * scale
        Wdown = jax.random.normal(ks[4], (E, H, D), dtype=jnp.float32) * scale
        bdown = jax.random.normal(ks[5], (E, D), dtype=jnp.float32) * scale
        return {'x': x, 'Wg': Wg, 'Wup': Wup, 'bup': bup, 'Wdown': Wdown, 'bdown': bdown}
    _L0_ffn_in = _L0_ffn_setup()

    def _L1_attn_setup():
        import jax, jax.numpy as jnp
        import numpy as np
        MIN_RAD, MAX_RAD, EPS = (0.9, 0.999, 1e-08)

        def block_diag_linear(x, w, b):
            h, bw, _ = w.shape
            xb = x.reshape(x.shape[0], x.shape[1], h, bw)
            y = jnp.einsum('bthi,hij->bthj', xb, w) + b
            return y.reshape(x.shape)
        key = jax.random.key(seed)
        kx, kw1, kw2, ka = jax.random.split(key, 4)
        B, T, width, num_heads = (8, 512, 128, 8)
        bw = width // num_heads
        std = np.sqrt(1.0 / bw)
        x = jax.random.normal(kx, (B, T, width), dtype=jnp.float32)
        ig_w = std * jax.random.normal(kw1, (num_heads, bw, bw), dtype=jnp.float32)
        ig_b = jnp.zeros((num_heads, bw), dtype=jnp.float32)
        ag_w = std * jax.random.normal(kw2, (num_heads, bw, bw), dtype=jnp.float32)
        ag_b = jnp.zeros((num_heads, bw), dtype=jnp.float32)
        u = jax.random.uniform(ka, (width,), dtype=jnp.float32, minval=MIN_RAD ** 2 + EPS, maxval=MAX_RAD ** 2 + EPS)
        a_param = jnp.log(jnp.exp(-0.5 * jnp.log(u)) - 1.0)
        return {'x': x, 'ig_w': ig_w, 'ig_b': ig_b, 'ag_w': ag_w, 'ag_b': ag_b, 'a_param': a_param}
    _L1_attn_in = _L1_attn_setup()

    def _L1_ffn_setup():
        import math
        import jax, jax.numpy as jnp
        import numpy as np
        B, T, D = (4, 512, 128)
        H = 16
        HD = D // H
        CAP = int(512 * 0.125)
        DFF = int(D * 4 * 2 / 3)
        EPS = 1e-06

        def rmsnorm(x, g):
            return x * jax.lax.rsqrt(jnp.mean(x * x, axis=-1, keepdims=True) + EPS) * g
        key = jax.random.key(seed)
        ks = jax.random.split(key, 9)
        s = lambda k, shape: jax.random.normal(k, shape, jnp.float32) * 0.02
        return {'x': jax.random.normal(ks[0], (B, T, D), jnp.float32), 'w_router': s(ks[1], (D,)), 'W_qkv': s(ks[2], (3 * D, D)), 'W_out': s(ks[3], (D, D)), 'g1': jnp.ones((D,), jnp.float32), 'g2': jnp.ones((D,), jnp.float32), 'W1': s(ks[4], (DFF, D)), 'W2': s(ks[5], (DFF, D)), 'W3': s(ks[6], (D, DFF))}
    _L1_ffn_in = _L1_ffn_setup()
    _d = {'L0_attn_u': _L0_attn_in['u'], 'L0_attn_in_proj_w': _L0_attn_in['in_proj_w'], 'L0_attn_conv_w': _L0_attn_in['conv_w'], 'L0_attn_conv_b': _L0_attn_in['conv_b'], 'L0_attn_dt_bias': _L0_attn_in['dt_bias'], 'L0_attn_A_log': _L0_attn_in['A_log'], 'L0_attn_D': _L0_attn_in['D'], 'L0_attn_rms_w': _L0_attn_in['rms_w'], 'L0_attn_out_w': _L0_attn_in['out_w'], 'L0_ffn_Wg': _L0_ffn_in['Wg'], 'L0_ffn_Wup': _L0_ffn_in['Wup'], 'L0_ffn_bup': _L0_ffn_in['bup'], 'L0_ffn_Wdown': _L0_ffn_in['Wdown'], 'L0_ffn_bdown': _L0_ffn_in['bdown'], 'L1_attn_ig_w': _L1_attn_in['ig_w'], 'L1_attn_ig_b': _L1_attn_in['ig_b'], 'L1_attn_ag_w': _L1_attn_in['ag_w'], 'L1_attn_ag_b': _L1_attn_in['ag_b'], 'L1_attn_a_param': _L1_attn_in['a_param'], 'L1_ffn_w_router': _L1_ffn_in['w_router'], 'L1_ffn_W_qkv': _L1_ffn_in['W_qkv'], 'L1_ffn_W_out': _L1_ffn_in['W_out'], 'L1_ffn_g1': _L1_ffn_in['g1'], 'L1_ffn_g2': _L1_ffn_in['g2'], 'L1_ffn_W1': _L1_ffn_in['W1'], 'L1_ffn_W2': _L1_ffn_in['W2'], 'L1_ffn_W3': _L1_ffn_in['W3']}
    _x0 = _d['L0_attn_u']
    _d['L0_attn_u'] = jax.random.normal(jax.random.fold_in(jax.random.key(seed), 1), (2, 2048, 128), dtype=_x0.dtype)
    del _x0
    return _d

def reference(L0_attn_u, L0_attn_in_proj_w, L0_attn_conv_w, L0_attn_conv_b, L0_attn_dt_bias, L0_attn_A_log, L0_attn_D, L0_attn_rms_w, L0_attn_out_w, L0_ffn_Wg, L0_ffn_Wup, L0_ffn_bup, L0_ffn_Wdown, L0_ffn_bdown, L1_attn_ig_w, L1_attn_ig_b, L1_attn_ag_w, L1_attn_ag_b, L1_attn_a_param, L1_ffn_w_router, L1_ffn_W_qkv, L1_ffn_W_out, L1_ffn_g1, L1_ffn_g2, L1_ffn_W1, L1_ffn_W2, L1_ffn_W3):

    def _L0_attn_ref(u, in_proj_w, conv_w, conv_b, dt_bias, A_log, D, rms_w, out_w):
        import jax, jax.numpy as jnp
        import numpy as np
        D_MODEL = 128
        EXPAND = 2
        D_INNER = EXPAND * D_MODEL
        D_STATE = 64
        NGROUPS = 1
        HEADDIM = 128
        NHEADS = D_INNER // HEADDIM
        D_CONV = 4
        CONV_DIM = D_INNER + 2 * NGROUPS * D_STATE
        D_IN_PROJ = 2 * D_INNER + 2 * NGROUPS * D_STATE + NHEADS
        BATCH = 2
        SEQLEN = 512
        RMS_EPS = 1e-05
        Bsz, L, _ = u.shape
        zxbcdt = jnp.einsum('bld,ed->ble', u, in_proj_w)
        s1 = D_INNER
        s2 = 2 * D_INNER
        s3 = s2 + NGROUPS * D_STATE
        s4 = s3 + NGROUPS * D_STATE
        z = zxbcdt[..., :s1]
        x = zxbcdt[..., s1:s2]
        B_part = zxbcdt[..., s2:s3]
        C_part = zxbcdt[..., s3:s4]
        dt = zxbcdt[..., s4:]
        dt = jax.nn.softplus(dt + dt_bias)
        xBC = jnp.concatenate([x, B_part, C_part], axis=-1)
        xt = xBC.transpose(0, 2, 1)
        kern = conv_w[:, None, :]
        conv = jax.lax.conv_general_dilated(xt, kern, (1,), [(D_CONV - 1, 0)], dimension_numbers=('NCH', 'OIH', 'NCH'), feature_group_count=CONV_DIM)
        xBC = jax.nn.silu((conv + conv_b[None, :, None]).transpose(0, 2, 1))
        x_c = xBC[..., :D_INNER]
        B_c = xBC[..., D_INNER:D_INNER + NGROUPS * D_STATE]
        C_c = xBC[..., D_INNER + NGROUPS * D_STATE:]
        x_s = x_c.reshape(Bsz, L, NHEADS, HEADDIM)
        hpg = NHEADS // NGROUPS
        B_full = jnp.repeat(B_c.reshape(Bsz, L, NGROUPS, D_STATE), hpg, axis=2)
        C_full = jnp.repeat(C_c.reshape(Bsz, L, NGROUPS, D_STATE), hpg, axis=2)
        A = -jnp.exp(A_log)

        def step(state, inp):
            x_t, dt_t, B_t, C_t = inp
            decay = jnp.exp(dt_t * A)[:, :, None, None]
            state = decay * state + B_t[:, :, None, :] * x_t[..., None]
            y_t = jnp.einsum('bhpn,bhn->bhp', state, C_t)
            return (state, y_t)
        init = jnp.zeros((Bsz, NHEADS, HEADDIM, D_STATE), u.dtype)
        xs = (x_s.transpose(1, 0, 2, 3), dt.transpose(1, 0, 2), B_full.transpose(1, 0, 2, 3), C_full.transpose(1, 0, 2, 3))
        _, ys = jax.lax.scan(step, init, xs)
        y = ys.transpose(1, 0, 2, 3) + D[None, None, :, None] * x_s
        y_flat = y.reshape(Bsz, L, D_INNER)
        mu = jnp.mean(y_flat * y_flat, axis=-1, keepdims=True)
        y_flat = y_flat * jax.lax.rsqrt(mu + RMS_EPS) * rms_w
        y_flat = y_flat * jax.nn.sigmoid(z)
        return jnp.einsum('bld,ed->ble', y_flat, out_w)

    def _L0_ffn_ref(x, Wg, Wup, bup, Wdown, bdown):
        import jax, jax.numpy as jnp
        import numpy as np
        D = 128
        H = 512
        E = 12
        K = 3
        B, S = (1, 256)
        gate_logits = jnp.einsum('bsd,de->bse', x, Wg)
        topw, sel = jax.lax.top_k(gate_logits, K)
        topw = jax.nn.softmax(topw.astype(jnp.float32), axis=-1).astype(x.dtype)
        cw = jnp.einsum('bsk,bske->bse', topw, jax.nn.one_hot(sel, E, dtype=x.dtype))
        h = jax.nn.gelu(jnp.einsum('bsd,edh->ebsh', x, Wup) + bup[:, None, None, :], approximate=False)
        y = jnp.einsum('ebsh,ehd->ebsd', h, Wdown) + bdown[:, None, None, :]
        return jnp.einsum('bse,ebsd->bsd', cw, y)

    def _L1_attn_ref(x, ig_w, ig_b, ag_w, ag_b, a_param):
        import jax, jax.numpy as jnp
        import numpy as np
        MIN_RAD, MAX_RAD, EPS = (0.9, 0.999, 1e-08)

        def block_diag_linear(x, w, b):
            h, bw, _ = w.shape
            xb = x.reshape(x.shape[0], x.shape[1], h, bw)
            y = jnp.einsum('bthi,hij->bthj', xb, w) + b
            return y.reshape(x.shape)
        gate_x = jax.nn.sigmoid(block_diag_linear(x, ig_w, ig_b))
        gate_a = jax.nn.sigmoid(block_diag_linear(x, ag_w, ag_b))
        log_a = -8.0 * gate_a * jax.nn.softplus(a_param)
        a = jnp.exp(log_a)
        a2 = jnp.exp(2.0 * log_a)
        gated_x = x * gate_x
        multiplier = jnp.sqrt(jnp.clip(1.0 - a2, 1e-07))
        normed_x = gated_x * multiplier
        B, T, D = x.shape
        p = jnp.cumprod(a, axis=1)
        p_prefix = jnp.concatenate([jnp.ones((B, 1, D), x.dtype), p[:, :-1]], axis=1)
        p_prefix = jnp.clip(p_prefix, 1e-07)
        w = normed_x / p_prefix
        S = jnp.cumsum(w, axis=1)
        h = p_prefix * S
        return h

    def _L1_ffn_ref(x, w_router, W_qkv, W_out, g1, g2, W1, W2, W3):
        import math
        import jax, jax.numpy as jnp
        import numpy as np
        B, T, D = (4, 512, 128)
        H = 16
        HD = D // H
        CAP = int(512 * 0.125)
        DFF = int(D * 4 * 2 / 3)
        EPS = 1e-06

        def rmsnorm(x, g):
            return x * jax.lax.rsqrt(jnp.mean(x * x, axis=-1, keepdims=True) + EPS) * g
        Bq, Tq, Dq = x.shape
        scores = x @ w_router
        _, idx = jax.lax.top_k(scores, CAP)
        x_sel = jnp.take_along_axis(x, idx[:, :, None], axis=1)
        h = rmsnorm(x_sel, g1)
        qkv = (h @ W_qkv.T).reshape(Bq, CAP, 3, H, HD)
        q, k, v = jnp.moveaxis(qkv, 2, 0)
        att = jnp.einsum('bqhd,bkhd->bhqk', q, k) / math.sqrt(HD)
        mask = jnp.triu(jnp.ones((CAP, CAP), bool), 1)
        att = jnp.where(mask, -jnp.inf, att)
        att = jax.nn.softmax(att, axis=-1)
        o = jnp.einsum('bhqk,bkhd->bqhd', att, v).reshape(Bq, CAP, Dq)
        x_attn = o @ W_out.T
        h2 = rmsnorm(x_sel + x_attn, g2)
        x_ff = jax.nn.silu(h2 @ W1.T) * (h2 @ W2.T) @ W3.T
        x_proc = x_sel + x_attn + x_ff
        out = x.at[jnp.arange(Bq)[:, None], idx].set(x_proc)
        return out
    x = L0_attn_u
    x = x + _layernorm(_L0_attn_ref(_layernorm(x, axis=-1), L0_attn_in_proj_w, L0_attn_conv_w, L0_attn_conv_b, L0_attn_dt_bias, L0_attn_A_log, L0_attn_D, L0_attn_rms_w, L0_attn_out_w), axis=-1)
    x = x + _layernorm(_L0_ffn_ref(_layernorm(x, axis=-1), L0_ffn_Wg, L0_ffn_Wup, L0_ffn_bup, L0_ffn_Wdown, L0_ffn_bdown), axis=-1)
    x = x + _layernorm(_L1_attn_ref(_layernorm(x, axis=-1), L1_attn_ig_w, L1_attn_ig_b, L1_attn_ag_w, L1_attn_ag_b, L1_attn_a_param), axis=-1)
    x = x + _layernorm(_L1_ffn_ref(_layernorm(x, axis=-1), L1_ffn_w_router, L1_ffn_W_qkv, L1_ffn_W_out, L1_ffn_g1, L1_ffn_g2, L1_ffn_W1, L1_ffn_W2, L1_ffn_W3), axis=-1)
    return x

_drawn_inputs = setup_inputs


def setup_inputs(seed=0):
    import zlib

    import numpy as np

    out = dict(_drawn_inputs(seed))
    spreads = {'L0_attn_D': (1.0, 0.2),
     'L0_attn_rms_w': (1.0, 0.2),
     'L1_attn_ig_b': (0.0, 0.471),
     'L1_attn_ag_b': (0.0, 0.617),
     'L1_ffn_g1': (1.0, 0.6),
     'L1_ffn_g2': (1.0, 0.6)}
    factors = {'L0_attn_dt_bias': 8.0,
     'L0_attn_A_log': 8.0,
     'L1_ffn_w_router': 8.0,
     'L1_ffn_W_qkv': 8.0,
     'L1_ffn_W_out': 8.0,
     'L1_ffn_W1': 8.0,
     'L1_ffn_W2': 8.0,
     'L1_ffn_W3': 8.0}
    for name, (base, spread) in spreads.items():
        noise = np.random.default_rng([zlib.crc32(name.encode()), seed]).standard_normal(out[name].shape)
        drawn = base * np.exp(spread * noise) if base else spread * noise
        out[name] = jnp.asarray(drawn.astype(out[name].dtype))
    for name, factor in factors.items():
        out[name] = (out[name] * factor).astype(out[name].dtype)
    return out
```

```python
from contextlib import ExitStack

import concourse.bass as bass
from concourse import mybir

F32 = mybir.dt.float32
U32 = mybir.dt.uint32
ALU = mybir.AluOpType
ACT = mybir.ActivationFunctionType
AX = mybir.AxisListType

P = 128
BATCH, SEQ, D = 2, 2048, 128
TOKENS = BATCH * SEQ
TILES = TOKENS // P
BT = SEQ // P
GT = 4
GW = GT * P
GROUPS = TILES // GT
BG = BT // GT
HEADS, NS, DI = 2, 64, 256
TAPS = 4
E, HID, TOPK = 12, 512, 3
HC = HID // P
CAP, AH, HD = 64, 16, 8
DFF = 341
FC = [128, 128, 85]
LN_EPS, RMS_EPS, FF_EPS = 1e-5, 1e-5, 1e-6

MIXER_COLS = [("win", 642), ("wout", 256), ("conv_w", 12), ("conv_b", 3), ("rms_w", 2),
              ("dt_bias", 2), ("a_log", 2), ("d_skip", 2), ("a_param", 1)]
LATER_COLS = [("gate", E), ("bup", E * HC), ("bdown", D), ("ig", P), ("ag", P), ("ig_b", 1), ("ag_b", 1),
              ("router", D), ("wqkv", 3 * D), ("wo", D), ("g1", 1), ("g2", 1), ("w1", DFF), ("w2", DFF),
              ("w3", 3 * D)]


def columns(cols):
    at, out = 0, {}
    for name, n in cols:
        out[name] = (at, at + n)
        at += n
    return out, at


MIXER_AT, MIXER_N = columns(MIXER_COLS)
LATER_AT, LATER_N = columns(LATER_COLS)


def build(nc, u, mixer_w, later_w, wup, wdown, out):
    with ExitStack() as ctx:
        def sb(name, shape, dt=F32):
            return ctx.enter_context(nc.sbuf_tensor(name, shape, dt))

        def sem(name):
            return ctx.enter_context(nc.semaphore(name))

        X = sb("X", [P, TILES * D])
        A = sb("A", [P, TILES * D])
        T = sb("T", [P, TOKENS])
        F = sb("F", [P, 5 * TOKENS + 64])
        NX = F[:, 0:TOKENS]
        WM = sb("WM", [P, MIXER_N])
        WL = sb("WL", [P, LATER_N])
        ident = sb("ident", [P, P])
        ones = sb("ones", [P, P])
        zeros = sb("zeros", [P, 1])
        st6 = sb("st6", [P, TILES * 6])
        MN = sb("MN", [P, TILES])
        DF = sb("DF", [P, TILES])
        VR = sb("VR", [P, TILES])
        SD = sb("SD", [P, TILES])
        RS = sb("RS", [P, TILES])
        NT = 2 * TILES + 1
        dt0 = sb("dt0", [P, NT])
        dt1 = sb("dt1", [P, NT])
        dt2 = sb("dt2", [P, NT])
        dt3 = sb("dt3", [P, NT])
        decay = sb("decay", [P, 2 * TILES])
        negA = sb("negA", [P, 2])
        lru_c = sb("lru_c", [P, 1])
        lru_c2 = sb("lru_c2", [P, 1])
        ssq = sb("ssq", [P, TILES])

        def wm(name, lo=0, hi=None, rows=P):
            a, b = MIXER_AT[name]
            return WM[0:rows, a + lo:(a + hi if hi is not None else b)]

        def wl(name, lo=0, hi=None, rows=P):
            a, b = LATER_AT[name]
            return WL[0:rows, a + lo:(a + hi if hi is not None else b)]

        at = [0]

        def carve(n):
            at[0] += n
            assert at[0] <= 5 * TOKENS + 64
            return F[:, at[0] - n:at[0]]

        XW = SEQ + TAPS - 1
        xin = [carve(XW) for _ in range(3)]
        cv = [[carve(GW) for _ in range(3)] for _ in range(2)]
        sg = [carve(GW) for _ in range(2)]
        xc = [[carve(GW) for _ in range(3)] for _ in range(2)]
        sigz = [[carve(GW) for _ in range(2)] for _ in range(2)]
        Y = [carve(GW) for _ in range(2)]
        YSQ = [carve(GW) for _ in range(2)]
        YF = [carve(GW) for _ in range(2)]
        C0 = [sb(f"C0_{i}", [NS, GW]) for i in range(2)]
        diag = [sb(f"diag{i}", [P, HEADS, P]) for i in range(2)]
        LB = [sb(f"LB{i}", [P, HEADS, P]) for i in range(2)]
        EB = [sb(f"EB{i}", [NS, HEADS, P]) for i in range(2)]
        MB = [sb(f"MB{i}", [P, HEADS, P]) for i in range(2)]
        BW = [sb(f"BW{i}", [P, HEADS, NS]) for i in range(2)]
        CE = [sb(f"CE{i}", [NS, HEADS, P]) for i in range(2)]
        XT = [sb(f"XT{i}", [P, DI]) for i in range(2)]
        ST = [sb(f"ST{i}", [NS, DI]) for i in range(2)]

        cwT = F[0:E, TOKENS:2 * TOKENS]
        HB = [F[:, (2 + i) * TOKENS // 2 + TOKENS:(3 + i) * TOKENS // 2 + TOKENS] for i in range(2)]
        wu = [sb(f"wu{i}", [P, HID]) for i in range(2)]
        wd = [sb(f"wd{i}", [P, HC * D]) for i in range(2)]
        LG = sb("LG", [P, TILES * E])
        top8 = sb("top8", [P, TILES * 8])
        sel8 = sb("sel8", [P, TILES * 8], U32)
        self_ = sb("sel_f", [P, TILES * 8])
        tw = sb("tw", [P, TILES * TOPK])
        tsum = sb("tsum", [P, TILES])
        iotaE = sb("iotaE", [P, E])
        oh = [sb(f"oh{i}", [P, TILES * E]) for i in range(TOPK)]
        CW = sb("CW", [P, TILES * E])

        G = [F[:, i * TOKENS:(i + 1) * TOKENS] for i in range(4)]
        PW = SEQ + 1
        CP = F[:, 4 * TOKENS:4 * TOKENS + BATCH * PW]

        sc = sb("sc", [P, TILES])
        sc32 = sb("sc32", [TILES, P])
        row = sb("row", [BATCH, SEQ])
        v8 = sb("v8", [BATCH, CAP])
        i8 = sb("i8", [BATCH, CAP], U32)
        rowoff = sb("rowoff", [BATCH, 1])
        i8g = sb("i8g", [BATCH, CAP], U32)
        idx = sb("idx", [P, 1], U32)
        hmask = sb("hmask", [P, AH])
        amask = sb("amask", [P, P])
        XS = sb("XS", [P, D])
        XN = sb("XN", [P, D])
        SQ = sb("SQ", [P, D])
        HN = sb("HN", [P, D])
        hT = sb("hT", [P, P])
        qT = sb("qT", [P, P])
        kT = sb("kT", [P, P])
        vv = sb("vv", [P, P])
        kM = F[:, 0:AH * P]
        SM = F[:, AH * P:2 * AH * P]
        PT = F[:, 2 * AH * P:3 * AH * P]
        mx = sb("mx", [P, AH])
        sm = sb("sm", [P, AH])
        O = sb("O", [P, D])
        OT = sb("OT", [P, P])
        XA = sb("XA", [P, D])
        u1 = [sb(f"u1_{i}", [P, P]) for i in range(3)]
        gg = [sb(f"gg_{i}", [P, P]) for i in range(3)]
        PR = sb("PR", [P, D])
        c1 = [sb(f"c1_{i}", [P, 8]) for i in range(2)]

        PB = [ctx.enter_context(nc.psum_tensor(f"PB{i}", [P, 512], F32)) for i in range(8)]

        IN, XP, SP, OP = PB[0], PB[1], PB[4], PB[7]
        FR = [PB[2], PB[3]]
        YP = [PB[5], PB[6]]

        x3_dram = nc.dram_tensor("x3_scratch", [TOKENS, D], F32, kind="Internal").ap()

        s_apart = sem("s_apart")
        s_u = sem("s_u")
        s_wm = sem("s_wm")
        s_wl = sem("s_wl")
        s_const = sem("s_const")
        s_cstep = sem("s_cstep")
        s_stat = sem("s_stat")
        s_dve = sem("s_dve")
        s_var = sem("s_var")
        s_sd = sem("s_sd")
        s_xn = sem("s_xn")
        s_tr = sem("s_tr")
        s_T = sem("s_T")
        s_dtp = sem("s_dtp")
        s_sp = sem("s_sp")
        s_spa = sem("s_spa")
        s_decay = sem("s_decay")
        s_zero = sem("s_zero")
        s_in = sem("s_in")
        s_ev = sem("s_ev")
        s_conv = sem("s_conv")
        s_sig = sem("s_sig")
        s_xc = sem("s_xc")
        s_c0 = sem("s_c0")
        s_diag = sem("s_diag")
        s_dec = sem("s_dec")
        s_tp = sem("s_tp")
        s_g = sem("s_g")
        s_xt = sem("s_xt")
        s_L = sem("s_L")
        s_E = sem("s_E")
        s_M = sem("s_M")
        s_Bw = sem("s_Bw")
        s_CE = sem("s_CE")
        s_S = sem("s_S")
        s_upd = sem("s_upd")
        s_post = sem("s_post")
        s_ysq = sem("s_ysq")
        s_yf = sem("s_yf")
        s_out = sem("s_out")
        s_oev = sem("s_oev")
        s_res = sem("s_res")
        s_X = sem("s_X")
        s_lg = sem("s_lg")
        s_top = sem("s_top")
        s_ex = sem("s_ex")
        s_exd = sem("s_exd")
        s_cw = sem("s_cw")
        s_cwt = sem("s_cwt")
        s_cwe = sem("s_cwe")
        s_bd = sem("s_bd")
        s_bde = sem("s_bde")
        s_we = [sem(f"s_we{i}") for i in range(2)]
        s_up = sem("s_up")
        s_gl = sem("s_gl")
        s_dn = sem("s_dn")
        s_acc = sem("s_acc")
        s_gt = sem("s_gt")
        s_gs = sem("s_gs")
        s_aa = sem("s_aa")
        s_1a = sem("s_1a")
        s_mu = sem("s_mu")
        s_xg = sem("s_xg")
        s_h = sem("s_h")
        s_ht = sem("s_ht")
        s_he = sem("s_he")
        s_wx = sem("s_wx")
        s_sc = sem("s_sc")
        s_sct = sem("s_sct")
        s_sce = sem("s_sce")
        s_row = sem("s_row")
        s_tk = sem("s_tk")
        s_idx = sem("s_idx")
        s_fin = sem("s_fin")
        s_st = sem("s_st")
        s_x3 = sem("s_x3")
        s_gat = sem("s_gat")
        s_sca = sem("s_sca")
        s_pd = sem("s_pd")
        s_vd = sem("s_vd")
        s_ad = sem("s_ad")

        s_rows = sem("s_rows")

        block = ctx.enter_context(nc.Block())

        def row_begins(eng, b):
            eng.wait_ge(s_rows, b * 5 + 5)
            eng.sem_inc(s_apart, 1)

        def cols(t, start, n):
            return t[:, bass.ds(start, n)]

        FILL = [[(1, 1)], [(1, 2)], [(1, 3)], [(1, 4), (2, 0)]]
        N_NORM = 3

        @block.sync
        def _(sp):
            uv = u.rearrange("(g t p) d -> g p t d", t=GT, p=P)
            for g in range(GROUPS):
                sp.dma_start(X[:, g * GW:(g + 1) * GW].rearrange("p (t d) -> p t d", t=GT), uv[g]).then_inc(s_u, 16)
                if g == 3:
                    sp.dma_start(WM[:, :], mixer_w).then_inc(s_wm, 16)
            sp.dma_start(WL[:, :], later_w).then_inc(s_wl, 16)

            def load_expert(e, i):
                sp.dma_start(wu[i][:, :], wup[bass.ds(e, 1)].rearrange("e p n -> (e p) n")).then_inc(s_we[i], 16)
                sp.dma_start(wd[i][:, :], wdown[bass.ds(e, 1)].rearrange("e p n -> (e p) n")).then_inc(s_we[i], 16)

            load_expert(0, 0)
            sp.sem_inc(s_rows, 1)
            with sp.Fori(0, BATCH) as b:
                row_begins(sp, b)
                for g in range(BG):
                    sp.wait_ge(s_xc, b * 12 + 3 * g + 3)
                    sp.sem_inc(s_apart, 1)
                    if g >= 2:
                        sp.wait_ge(s_CE, b * 16 + GT * (g - 1))
                        sp.sem_inc(s_apart, 1)
                        sp.wait_ge(s_g, b * 16 + GT * (g - 1))
                        sp.sem_inc(s_apart, 1)
                    if g >= 1:
                        sp.wait_ge(s_c0, b * 64 + 16 * g)
                        sp.sem_inc(s_apart, 1)
                    sp.dma_start(C0[g % 2][:, :], xc[g % 2][2][NS:2 * NS, :]).then_inc(s_c0, 16)
                sp.wait_ge(s_c0, b * 64 + 16 * BG)
                sp.sem_inc(s_rows, 1)
            with sp.Fori(0, E // 2 - 1) as j:
                for i in range(2):
                    sp.wait_ge(s_dn, j * 64 + 32 * i + 1)
                    sp.sem_inc(s_apart, 1)
                    load_expert(j * 2 + i + 1, 1 - i)
            sp.wait_ge(s_dn, (E - 2) * 32 + 1)
            load_expert(E - 1, 1)
            sp.wait_ge(s_X, 8 * 3)
            sp.dma_start(x3_dram.rearrange("(t p) d -> p t d", p=P), X[:, :].rearrange("p (t d) -> p t d", t=TILES)).then_inc(s_x3, 16)
            sp.wait_ge(s_sce, 1)
            sp.dma_start(row[:, :].rearrange("b (t p) -> b t p", p=P), sc32[:, :]).then_inc(s_row, 16)
            ov = out.rearrange("(g t p) d -> g p t d", t=GT, p=P)
            for g in range(GROUPS):
                sp.wait_ge(s_fin, g + 1)
                sp.dma_start(ov[g], A[:, g * GW:(g + 1) * GW].rearrange("p (t d) -> p t d", t=GT)).then_inc(s_st, 16)
            sp.wait_ge(s_tk, 25)
            sp.dma_start(idx[:, :], i8g[:, :]).then_inc(s_idx, 16)
            sp.wait_ge(s_st, 16 * GROUPS)
            sp.wait_ge(s_sca, 16)

        @block.gpsimd
        def _(pool):
            pool.memset(ident[:, :], 0.0).then_inc(s_cstep, 1)
            pool.memset(ones[:, :], 1.0).then_inc(s_const, 1)
            pool.memset(zeros[:, :], 0.0).then_inc(s_const, 1)
            pool.memset(hmask[:, :], 1.0).then_inc(s_cstep, 1)
            pool.memset(amask[:, :], 0.0).then_inc(s_cstep, 1)
            pool.wait_ge(s_cstep, 3)
            pool.affine_select(out=ident[:, :], in_=ident[:, :], compare_op=ALU.not_equal, fill=1.0, base=0,
                               pattern=[[-1, P]], channel_multiplier=1).then_inc(s_const, 1)
            pool.affine_select(out=hmask[:, :], in_=hmask[:, :], compare_op=ALU.is_ge, fill=0.0, base=0,
                               pattern=[[-HD, AH]], channel_multiplier=1).then_inc(s_cstep, 1)
            pool.affine_select(out=amask[:, :], in_=amask[:, :], compare_op=ALU.is_ge, fill=-1e30, base=0,
                               pattern=[[-1, P]], channel_multiplier=1).then_inc(s_cstep, 1)
            pool.wait_ge(s_cstep, 5)
            pool.affine_select(out=hmask[:, :], in_=hmask[:, :], compare_op=ALU.is_ge, fill=0.0, base=HD - 1,
                               pattern=[[HD, AH]], channel_multiplier=-1).then_inc(s_const, 1)
            pool.wait_ge(s_const, 4)
            pool.memset(amask[CAP:P, 0:CAP], -1e30).then_inc(s_const, 1)
            pool.wait_ge(s_const, 5)
            pool.iota(iotaE[:, :], pattern=[[1, E]], base=0, channel_multiplier=0,
                      allow_small_or_imprecise_dtypes=True).then_inc(s_const, 1)
            pool.iota(rowoff[:, :], pattern=[[1, 1]], base=0, channel_multiplier=SEQ,
                      allow_small_or_imprecise_dtypes=True).then_inc(s_const, 1)
            pool.wait_ge(s_T, GROUPS)
            for j in range(3):
                pool.memset(xin[j][:, 0:TAPS - 1], 0.0).then_inc(s_zero, 1)
            pool.wait_ge(s_const, 7)
            pool.wait_ge(s_decay, 1)

            pool.sem_inc(s_rows, 1)
            with pool.Fori(0, BATCH) as b:
                def make_diag(k):
                    if k >= 2:
                        pool.wait_ge(s_dec, b * 16 + k - 1)
                    dk = decay[:, bass.ds(b * 32 + 2 * k, 2)]
                    pool.tensor_tensor(diag[k % 2][:, :, :], ident[:, :].unsqueeze(1).broadcast_to([P, HEADS, P]),
                                       dk.unsqueeze(2).broadcast_to([P, HEADS, P]), ALU.mult).then_inc(s_diag, 1)

                def silu(g, j):
                    n = 3 * g + j
                    pool.wait_ge(s_sig, b * 12 + n + 1)
                    if g >= 2:
                        pool.wait_ge(s_post, b * 8 + 2 * (g - 1))
                        pool.wait_ge(s_c0, b * 64 + 16 * (g - 1))
                    pool.tensor_tensor(xc[g % 2][j], cv[g % 2][j], sg[n % 2], ALU.mult).then_inc(s_xc, 1)

                def decayed_c(k):
                    g = k // GT
                    pool.wait_ge(s_c0, b * 64 + 16 * (g + 1))
                    pool.wait_ge(s_E, b * 32 + 2 * (k + 1))
                    if k >= 2:
                        pool.wait_ge(s_S, b * 16 + k - 1)
                    c = C0[g % 2][:, (k % GT) * P:(k % GT + 1) * P]
                    pool.tensor_tensor(CE[k % 2][:, :, :], c.unsqueeze(1).broadcast_to([NS, HEADS, P]),
                                       EB[k % 2][:, :, :], ALU.mult).then_inc(s_CE, 1)

                row_begins(pool, b)
                make_diag(0)
                make_diag(1)
                for j in range(3):
                    silu(0, j)
                decayed_c(0)
                for k in range(BT):
                    g, c = divmod(k, GT)
                    if k + 2 < BT:
                        make_diag(k + 2)
                    if k + 1 < BT:
                        decayed_c(k + 1)
                    if c < 3 and g + 1 < BG:
                        silu(g + 1, c)
                pool.wait_ge(s_CE, b * 16 + BT)
                pool.sem_inc(s_rows, 1)
            for b in range(BATCH):
                pool.wait_ge(s_gs, 8 * (b + 1))
                a, z = b * SEQ, (b + 1) * SEQ
                pool.tensor_tensor(G[0][:, a:z], T[:, a:z], G[0][:, a:z], ALU.mult).then_inc(s_xg, 1)
            rw = wl("router").unsqueeze(1).broadcast_to([P, BT, D])
            for b in range(BATCH):
                pool.wait_ge(s_xn, 8 * N_NORM + 4 * (b + 1))
                a, z = b * SEQ, (b + 1) * SEQ
                pool.tensor_tensor(G[1][:, a:z].rearrange("p (t d) -> p t d", d=D),
                                   NX[:, a:z].rearrange("p (t d) -> p t d", d=D), rw, ALU.mult).then_inc(s_wx, 1)
            pool.wait_ge(s_idx, 16)
            pool.wait_ge(s_x3, 16)
            pool.indirect_dma_start(XS[:, :], None, x3_dram, bass.IndirectOffsetOnAxis(idx[:, :], 0)).then_inc(s_gat, 16)
            pool.wait_ge(s_vd, 9)
            pool.wait_ge(s_st, 16 * GROUPS)
            pool.indirect_dma_start(out, bass.IndirectOffsetOnAxis(idx[:, :], 0), PR[:, :], None).then_inc(s_sca, 16)

        @block.vector
        def _(v):
            link = [0]
            nstat = [0]
            nvar = [0]

            def step(ins):
                ins.then_inc(s_dve, 1)
                link[0] += 1

            def settle():
                v.wait_ge(s_dve, link[0])

            def root(src, dst):
                nvar[0] += 1
                v.wait_ge(s_sd, nvar[0])
                step(v.reciprocal(dst, src))
                settle()

            def stats(src, eps):
                with v.Fori(0, GROUPS) as g:
                    for t in range(GT):
                        v.bn_stats(st6[:, bass.ds(g * GT * 6 + t * 6, 6)], cols(src, g * GW + t * D, D)).then_inc(s_stat, 1)
                nstat[0] += TILES
                v.wait_ge(s_stat, nstat[0])
                s6 = st6[:, :].rearrange("p (t s) -> p t s", s=6)
                step(v.tensor_tensor(MN[:, :], s6[:, :, 1], s6[:, :, 4], ALU.add))
                step(v.tensor_tensor(DF[:, :], s6[:, :, 1], s6[:, :, 4], ALU.subtract))
                step(v.tensor_tensor(VR[:, :], s6[:, :, 2], s6[:, :, 5], ALU.add))
                settle()
                step(v.tensor_scalar(MN[:, :], MN[:, :], 0.5, None, ALU.mult))
                step(v.scalar_tensor_tensor(DF[:, :], DF[:, :], 0.25, DF[:, :], ALU.mult, ALU.mult))
                step(v.tensor_scalar(VR[:, :], VR[:, :], 1.0 / D, eps, ALU.mult, ALU.add))
                settle()

            def to_root():
                v.tensor_tensor(VR[:, :], VR[:, :], DF[:, :], ALU.add).then_inc(s_var, 1)

            def norm(r):
                stats(X, LN_EPS)
                to_root()
                root(SD[:, :], RS[:, :])
                with v.Fori(0, GROUPS) as g:
                    for t in range(GT):
                        i = v.tensor_scalar(NX[:, bass.ds(g * GW + t * D, D)], cols(X, g * GW + t * D, D),
                                            MN[:, bass.ds(g * GT + t, 1)], RS[:, bass.ds(g * GT + t, 1)],
                                            ALU.subtract, ALU.mult)
                        if t == GT - 1:
                            i.then_inc(s_xn, 1)
                v.wait_ge(s_xn, GROUPS * (r + 1))

            def residual(e):
                with v.Fori(0, GROUPS) as g:
                    for t in range(GT):
                        a = cols(A, g * GW + t * D, D)
                        v.tensor_scalar(a, a, MN[:, bass.ds(g * GT + t, 1)], RS[:, bass.ds(g * GT + t, 1)],
                                        ALU.subtract, ALU.mult).then_inc(s_res, 1)
                v.wait_ge(s_res, TILES * (e + 1))
                with v.Fori(0, GROUPS) as g:
                    x = cols(X, g * GW, GW)
                    v.tensor_tensor(x, x, cols(A, g * GW, GW), ALU.add).then_inc(s_X, 1)
                v.wait_ge(s_X, GROUPS * (e + 1))

            v.wait_ge(s_u, 16 * GROUPS)
            norm(0)

            v.wait_ge(s_wm, 16)
            v.wait_ge(s_dtp, 1)
            N2 = 2 * TILES
            step(v.tensor_tensor(dt0[:, 0:N2].rearrange("p (t h) -> p t h", h=2),
                                 PB[2][:, 0:N2].rearrange("p (t h) -> p t h", h=2),
                                 wm("dt_bias").unsqueeze(1).broadcast_to([P, TILES, 2]), ALU.add))
            step(v.tensor_copy(dt0[:, N2:NT], wm("a_param")))
            settle()
            step(v.tensor_scalar(dt1[:, :], dt0[:, :], -1.0, None, ALU.mult))
            settle()
            v.tensor_tensor(dt1[:, :], dt1[:, :], dt0[:, :], ALU.min).then_inc(s_sp, 1)
            v.wait_ge(s_spa, 1)
            v.tensor_scalar(dt2[:, :], dt1[:, :], 1.0, None, ALU.add).then_inc(s_sp, 1)
            v.wait_ge(s_sp, 2)
            step(v.tensor_scalar(dt3[:, :], dt2[:, :], -1.0, None, ALU.add))
            settle()
            step(v.tensor_tensor(dt3[:, :], dt1[:, :], dt3[:, :], ALU.subtract))
            v.wait_ge(s_spa, 2)
            settle()
            step(v.reciprocal(dt1[:, :], dt2[:, :]))
            settle()
            step(v.tensor_tensor(dt3[:, :], dt3[:, :], dt1[:, :], ALU.mult))
            step(v.tensor_scalar(dt0[:, :], dt0[:, :], 0.0, None, ALU.max))
            settle()
            step(v.tensor_tensor(dt3[:, :], dt3[:, :], LG[:, 0:NT], ALU.add))
            settle()
            step(v.tensor_tensor(dt3[:, :], dt3[:, :], dt0[:, :], ALU.add))
            v.wait_ge(s_spa, 3)
            settle()
            step(v.tensor_scalar(lru_c[:, :], dt3[:, N2:NT], -8.0, None, ALU.mult))
            step(v.tensor_scalar(lru_c2[:, :], dt3[:, N2:NT], -16.0, None, ALU.mult))
            v.scalar_tensor_tensor(dt2[:, 0:N2].rearrange("p (t h) -> p t h", h=2),
                                   dt3[:, 0:N2].rearrange("p (t h) -> p t h", h=2), -1.0,
                                   negA[:, :].unsqueeze(1).broadcast_to([P, TILES, 2]), ALU.mult, ALU.mult).then_inc(s_sp, 1)
            v.wait_ge(s_zero, 3)
            v.wait_ge(s_const, 7)

            v.sem_inc(s_rows, 1)
            with v.Fori(0, BATCH) as b:
                def conv(g, j):
                    n = 3 * g + j
                    v.wait_ge(s_ev, b * 20 + 5 * g + j + 1)
                    if g >= 2:
                        v.wait_ge(s_xc, b * 12 + n - 5)
                    o = cv[g % 2][j]
                    for k in range(TAPS):
                        i = xin[j][:, g * GW + k:g * GW + k + GW]
                        w = wm("conv_w", 4 * j + k, 4 * j + k + 1)
                        if k == 0:
                            v.tensor_scalar(o, i, w, wm("conv_b", j, j + 1), ALU.mult, ALU.add).then_inc(s_conv, 1)
                        else:
                            v.wait_ge(s_conv, b * 48 + 4 * n + k)
                            v.scalar_tensor_tensor(o, i, w, o, ALU.mult, ALU.add).then_inc(s_conv, 1)

                def front(k):
                    q = k % 2
                    dec = FR[q][:, 0:256].rearrange("p (h t) -> p h t", h=2)
                    v.wait_ge(s_g, b * 16 + k + 1)
                    if k >= 2:
                        v.wait_ge(s_Bw, b * 16 + k - 1)
                    for h in range(HEADS):
                        v.tensor_tensor_scan(LB[q][:, h, :], dec[:, h, :], ident[:, :], 0.0, ALU.mult, ALU.add).then_inc(s_L, 1)
                    if k >= 2:
                        v.wait_ge(s_CE, b * 16 + k - 1)
                        v.wait_ge(s_upd, b * 34 + 2 * k)
                    for h in range(HEADS):
                        v.tensor_tensor_scan(EB[q][:, h, :], dec[0:NS, h, :], zeros[0:NS, :].broadcast_to([NS, P]),
                                             1.0, ALU.mult, ALU.add).then_inc(s_E, 1)
                    v.wait_ge(s_L, b * 32 + 2 * k + 2)
                    if k >= 2:
                        v.wait_ge(s_S, b * 16 + k - 1)
                    gp = FR[q][:, 256:256 + NS + P]
                    v.tensor_tensor(MB[q][:, :, :], LB[q][:, :, :], gp[:, NS:NS + P].unsqueeze(1).broadcast_to([P, HEADS, P]),
                                    ALU.mult).then_inc(s_M, 1)
                    v.tensor_tensor(BW[q][:, :, :], LB[q][:, :, P - 1:P].broadcast_to([P, HEADS, NS]),
                                    gp[:, 0:NS].unsqueeze(1).broadcast_to([P, HEADS, NS]), ALU.mult).then_inc(s_Bw, 1)

                def back(k):
                    q = k % 2
                    v.wait_ge(s_S, b * 16 + k + 1)
                    v.wait_ge(s_E, b * 32 + 2 * k + 2)
                    v.wait_ge(s_upd, b * 34 + 2 * k + 2)
                    for h in range(HEADS):
                        a, z = h * P, (h + 1) * P
                        v.scalar_tensor_tensor(ST[1 - q][:, a:z], ST[q][:, a:z], EB[q][:, h, P - 1:P],
                                               SP[0:NS, a:z], ALU.mult, ALU.add).then_inc(s_upd, 1)

                def post(g):
                    for h in range(HEADS):
                        if g >= 1:
                            v.wait_ge(s_ysq, b * 8 + 2 * g)
                            v.wait_ge(s_yf, b * 8 + 2 * g)
                        v.scalar_tensor_tensor(Y[h], xc[g % 2][h], wm("d_skip", h, h + 1), YP[h][:, :],
                                               ALU.mult, ALU.add).then_inc(s_post, 1)
                    v.wait_ge(s_post, b * 8 + 2 * g + 2)
                    v.wait_ge(s_ev, b * 20 + 5 * g + 5)
                    if g >= 1:
                        v.wait_ge(s_out, b * 16 + GT * g)
                    for h in range(HEADS):
                        v.scalar_tensor_tensor(YF[h], Y[h], wm("rms_w", h, h + 1), sigz[g % 2][h],
                                               ALU.mult, ALU.mult).then_inc(s_yf, 1)

                row_begins(v, b)
                v.memset(ST[0][:, 0:P], 0.0).then_inc(s_upd, 1)
                v.memset(ST[0][:, P:DI], 0.0).then_inc(s_upd, 1)
                for j in range(3):
                    conv(0, j)
                front(0)
                for k in range(BT):
                    g, c = divmod(k, GT)
                    if k + 1 < BT:
                        front(k + 1)
                    if c < 3 and g + 1 < BG:
                        conv(g + 1, c)
                    back(k)
                    if c == GT - 1:
                        post(g)
                v.wait_ge(s_yf, b * 8 + 8)
                v.wait_ge(s_upd, b * 34 + 34)
                v.sem_inc(s_rows, 1)

            v.wait_ge(s_oev, TILES)
            v.tensor_scalar(ssq[:, :], ssq[:, :], 1.0 / DI, RMS_EPS, ALU.mult, ALU.add).then_inc(s_var, 1)
            root(SD[:, :], ssq[:, :])
            stats(A, 0.0)
            step(v.tensor_tensor(VR[:, :], VR[:, :], DF[:, :], ALU.add))
            settle()
            step(v.tensor_tensor(VR[:, :], VR[:, :], ssq[:, :], ALU.mult))
            settle()
            step(v.tensor_tensor(VR[:, :], VR[:, :], ssq[:, :], ALU.mult))
            settle()
            v.tensor_scalar(VR[:, :], VR[:, :], LN_EPS, None, ALU.add).then_inc(s_var, 1)
            root(SD[:, :], RS[:, :])
            step(v.tensor_tensor(RS[:, :], RS[:, :], ssq[:, :], ALU.mult))
            settle()
            residual(0)
            norm(1)

            v.wait_ge(s_lg, 1)
            step(v.tensor_copy(LG[:, :], PB[2][:, 0:TILES * E]))
            settle()
            for t in range(TILES):
                step(v.max(top8[:, 8 * t:8 * t + 8], LG[:, E * t:E * t + E]))
            settle()
            for t in range(TILES):
                step(v.max_index(sel8[:, 8 * t:8 * t + 8], top8[:, 8 * t:8 * t + 8], LG[:, E * t:E * t + E]))
            t8 = top8[:, :].rearrange("p (t k) -> p t k", k=8)
            tw3 = tw[:, :].rearrange("p (t k) -> p t k", k=TOPK)
            v.tensor_tensor(tw3, t8[:, :, 0:TOPK], t8[:, :, 0:1].broadcast_to([P, TILES, TOPK]), ALU.subtract).then_inc(s_ex, 1)
            settle()
            step(v.tensor_copy(self_[:, :], sel8[:, :]))
            v.wait_ge(s_exd, 1)
            step(v.tensor_reduce(tsum[:, :], tw3, AX.X, ALU.add))
            settle()
            step(v.reciprocal(tsum[:, :], tsum[:, :]))
            settle()
            step(v.tensor_tensor(tw3, tw3, tsum[:, :].unsqueeze(2).broadcast_to([P, TILES, TOPK]), ALU.mult))
            s8 = self_[:, :].rearrange("p (t k) -> p t k", k=8)
            for k in range(TOPK):
                step(v.tensor_tensor(oh[k][:, :].rearrange("p (t e) -> p t e", e=E),
                                     iotaE[:, :].unsqueeze(1).broadcast_to([P, TILES, E]),
                                     s8[:, :, k:k + 1].broadcast_to([P, TILES, E]), ALU.is_equal))
            settle()
            for k in range(TOPK):
                o3 = oh[k][:, :].rearrange("p (t e) -> p t e", e=E)
                step(v.tensor_tensor(o3, o3, tw3[:, :, k:k + 1].broadcast_to([P, TILES, E]), ALU.mult))
            settle()
            step(v.tensor_tensor(CW[:, :], oh[0][:, :], oh[1][:, :], ALU.add))
            settle()
            v.tensor_tensor(CW[:, :], CW[:, :], oh[2][:, :], ALU.add).then_inc(s_cw, 1)
            v.wait_ge(s_cw, 1)
            v.wait_ge(s_bde, GROUPS)
            v.sem_inc(s_acc, 1)
            with v.Fori(0, E) as e:
                with v.Fori(0, GROUPS) as g:
                    for t in range(GT):
                        v.wait_ge(s_dn, e * 32 + g * 4 + t + 2)
                        v.wait_ge(s_acc, e * 32 + 1)
                        a = cols(A, g * GW + t * D, D)
                        v.scalar_tensor_tensor(a, PB[4 + t][:, 0:D], CW[:, bass.ds(g * (GT * E) + t * E + e, 1)],
                                               a, ALU.mult, ALU.add).then_inc(s_acc, 1)
            v.wait_ge(s_acc, E * TILES + 1)
            stats(A, LN_EPS)
            to_root()
            root(SD[:, :], RS[:, :])
            residual(1)
            norm(2)

            v.wait_ge(s_T, 3 * GROUPS)
            for b in range(BATCH):
                a, z = b * SEQ, (b + 1) * SEQ
                pa, pz = b * PW, b * PW + SEQ
                step(v.memset(CP[:, pa:pa + 1], 1.0))
                v.wait_ge(s_aa, 2 * b + 1)
                step(v.tensor_tensor_scan(CP[:, pa + 1:pz + 1], G[2][:, a:z], zeros[:, :].broadcast_to([P, SEQ]),
                                          1.0, ALU.mult, ALU.add))
                v.wait_ge(s_aa, 2 * b + 2)
                step(v.tensor_scalar(G[3][:, a:z], G[3][:, a:z], -1.0, 1.0, ALU.mult, ALU.add))
                settle()
                v.tensor_scalar(G[3][:, a:z], G[3][:, a:z], 1e-7, None, ALU.max).then_inc(s_1a, 1)
                step(v.tensor_scalar(G[1][:, a:z], CP[:, pa:pz], 1e-7, None, ALU.max))
                settle()
                step(v.reciprocal(G[2][:, a:z], G[1][:, a:z]))
                v.wait_ge(s_mu, b + 1)
                v.wait_ge(s_xg, b + 1)
                step(v.tensor_tensor(G[0][:, a:z], G[0][:, a:z], G[3][:, a:z], ALU.mult))
                settle()
                step(v.tensor_tensor(G[0][:, a:z], G[0][:, a:z], G[2][:, a:z], ALU.mult))
                settle()
                step(v.tensor_tensor_scan(G[3][:, a:z], G[0][:, a:z], zeros[:, :].broadcast_to([P, SEQ]),
                                          0.0, ALU.add, ALU.add))
                settle()
                v.tensor_tensor(CP[:, pa:pz], G[1][:, a:z], G[3][:, a:z], ALU.mult).then_inc(s_h, 1)
            v.wait_ge(s_he, GROUPS)
            stats(A, LN_EPS)
            to_root()
            root(SD[:, :], RS[:, :])
            residual(2)
            norm(3)

            for b in range(BATCH):
                a, z = b * SEQ, (b + 1) * SEQ
                v.wait_ge(s_wx, b + 1)
                step(v.tensor_reduce(sc[:, b * BT:(b + 1) * BT], G[1][:, a:z].rearrange("p (t d) -> p t d", d=D), AX.X, ALU.add))
            v.wait_ge(s_dve, link[0])
            v.sem_inc(s_sc, 1)
            v.wait_ge(s_xn, GROUPS * 4)
            stats(NX, LN_EPS)
            to_root()
            root(SD[:, :], RS[:, :])
            for g in range(GROUPS):
                for t in range(GT):
                    i = g * GT + t
                    step(v.tensor_scalar(A[:, i * D:(i + 1) * D], NX[:, i * D:(i + 1) * D], MN[:, i:i + 1], RS[:, i:i + 1],
                                         ALU.subtract, ALU.mult))
                settle()
                a = A[:, g * GW:(g + 1) * GW]
                v.tensor_tensor(a, a, X[:, g * GW:(g + 1) * GW], ALU.add).then_inc(s_fin, 1)

            v.wait_ge(s_row, 16)
            for r in range(CAP // 8):
                k8 = slice(8 * r, 8 * r + 8)
                v.max(v8[:, k8], row[:, :]).then_inc(s_tk, 1)
                v.wait_ge(s_tk, 3 * r + 1)
                v.max_index(i8[:, k8], v8[:, k8], row[:, :]).then_inc(s_tk, 1)
                v.wait_ge(s_tk, 3 * r + 2)
                v.match_replace(row[:, :], v8[:, k8], row[:, :], -3.0e38).then_inc(s_tk, 1)
                v.wait_ge(s_tk, 3 * r + 3)
            v.tensor_scalar(i8g[:, :], i8[:, :], rowoff[:, 0:1], None, ALU.add).then_inc(s_tk, 1)

            vd = [0]

            def vstep(ins):
                ins.then_inc(s_vd, 1)
                vd[0] += 1

            def vsettle():
                v.wait_ge(s_vd, vd[0])

            def row_stats(src, eps):
                step(v.bn_stats(st6[:, 0:6], src))
                settle()
                step(v.bn_aggr(c1[0][:, 0:2], st6[:, 0:6]))
                settle()
                v.tensor_scalar(c1[0][:, 1:2], c1[0][:, 1:2], eps, None, ALU.add).then_inc(s_var, 1)
                root(c1[1][:, 1:2], c1[1][:, 2:3])

            def row_norm(dst, src, eps):
                row_stats(src, eps)
                step(v.tensor_scalar(dst, src, c1[0][:, 0:1], c1[1][:, 2:3], ALU.subtract, ALU.mult))
                settle()

            def rms(dst, src):
                step(v.tensor_tensor(SQ[:, :], src, src, ALU.mult))
                settle()
                step(v.tensor_reduce(c1[0][:, 4:5], SQ[:, :], AX.X, ALU.add))
                settle()
                v.tensor_scalar(c1[0][:, 5:6], c1[0][:, 4:5], 1.0 / D, FF_EPS, ALU.mult, ALU.add).then_inc(s_var, 1)
                root(c1[1][:, 1:2], c1[1][:, 3:4])
                vstep(v.tensor_scalar(dst, src, c1[1][:, 3:4], None, ALU.mult))

            v.wait_ge(s_gat, 16)
            row_norm(XN[:, :], XS[:, :], LN_EPS)
            rms(HN[:, :], XN[:, :])
            v.wait_ge(s_ad, 3)
            kM3 = kM.rearrange("p (h k) -> p h k", h=AH)
            vstep(v.tensor_tensor(kM3, kT[:, :].unsqueeze(1).broadcast_to([P, AH, P]),
                                  hmask[:, :].unsqueeze(2).broadcast_to([P, AH, P]), ALU.mult))
            for i in range(4):
                v.wait_ge(s_pd, 4 + i + 1)
                step(v.tensor_tensor(SM[:, i * 512:(i + 1) * 512].rearrange("p (h k) -> p h k", h=4),
                                     PB[i][:, :].rearrange("p (h k) -> p h k", h=4),
                                     amask[:, :].unsqueeze(1).broadcast_to([P, 4, P]), ALU.add))
            settle()
            SM3 = SM.rearrange("p (h k) -> p h k", h=AH)
            step(v.tensor_reduce(mx[:, :], SM3, AX.X, ALU.max))
            settle()
            vstep(v.tensor_tensor(SM3, SM3, mx[:, :].unsqueeze(2).broadcast_to([P, AH, P]), ALU.subtract))
            v.wait_ge(s_ad, 5)
            step(v.tensor_reduce(sm[:, :], SM3, AX.X, ALU.add))
            settle()
            step(v.reciprocal(sm[:, :], sm[:, :]))
            settle()
            v.wait_ge(s_pd, 13)
            vstep(v.tensor_tensor(O[:, :].rearrange("p (h d) -> p h d", h=AH),
                                  PB[4][:, 0:D].rearrange("p (h d) -> p h d", h=AH),
                                  sm[:, :].unsqueeze(2).broadcast_to([P, AH, HD]), ALU.mult))
            v.wait_ge(s_pd, 15)
            step(v.tensor_tensor(XA[:, :], XN[:, :], PB[5][:, 0:D], ALU.add))
            settle()
            rms(HN[:, :], XA[:, :])
            for i in range(3):
                v.wait_ge(s_ad, 12 + i)
                vstep(v.tensor_tensor(gg[i][0:FC[i], :], u1[i][0:FC[i], :], PB[4][0:FC[i], i * P:(i + 1) * P], ALU.mult))
            v.wait_ge(s_pd, 18)
            step(v.tensor_tensor(PR[:, :], XA[:, :], PB[5][:, 0:D], ALU.add))
            settle()
            row_norm(PR[:, :], PR[:, :], LN_EPS)
            vstep(v.tensor_tensor(PR[:, :], PR[:, :], XS[:, :], ALU.add))
            assert vd[0] == 9, vd

        @block.scalar
        def _(act):
            nvar = [0]

            def sqrt(dst, src):
                nvar[0] += 1
                act.wait_ge(s_var, nvar[0])
                act.activation(dst, src, ACT.Sqrt).then_inc(s_sd, 1)

            def evict_T(r):
                for g in range(GROUPS):
                    act.wait_ge(s_tr, r * GROUPS + g + 1)
                    act.copy(T[:, g * GW:(g + 1) * GW], PB[g % 2][:, :]).then_inc(s_T, 1)

            sqrt(SD[:, :], VR[:, :])
            evict_T(0)
            act.wait_ge(s_sp, 1)
            act.activation(dt1[:, :], dt1[:, :], ACT.Exp).then_inc(s_spa, 1)
            act.wait_ge(s_sp, 2)
            act.activation(LG[:, 0:NT], dt2[:, :], ACT.Ln).then_inc(s_spa, 1)
            act.wait_ge(s_wm, 16)
            act.activation(negA[:, :], wm("a_log"), ACT.Exp).then_inc(s_spa, 1)
            act.wait_ge(s_sp, 3)
            act.activation(decay[:, :], dt2[:, 0:2 * TILES], ACT.Exp).then_inc(s_decay, 1)

            act.sem_inc(s_rows, 1)
            with act.Fori(0, BATCH) as b:
                def evict_in(g, j):
                    n = 5 * g + j
                    act.wait_ge(s_in, b * 20 + n + 1)
                    src = IN[:, :]
                    if j < 3:
                        act.copy(xin[j][:, TAPS - 1 + g * GW:TAPS - 1 + (g + 1) * GW], src).then_inc(s_ev, 1)
                    else:
                        if g >= 2:
                            act.wait_ge(s_yf, b * 8 + 2 * (g - 1))
                        act.activation(sigz[g % 2][j - 3], src, ACT.Sigmoid).then_inc(s_ev, 1)

                def conv_sigmoid(g, j):
                    n = 3 * g + j
                    act.wait_ge(s_conv, b * 48 + 4 * n + 4)
                    if n >= 2:
                        act.wait_ge(s_xc, b * 12 + n - 1)
                    act.activation(sg[n % 2], cv[g % 2][j], ACT.Sigmoid).then_inc(s_sig, 1)

                def evict_x(k):
                    q = k % 2
                    act.wait_ge(s_tp, b * 16 + k + 1)
                    if k >= 2:
                        act.wait_ge(s_S, b * 16 + k - 1)
                    act.copy(XT[q][:, :], XP[:, 0:DI]).then_inc(s_xt, 1)

                def evict_out(g, c):
                    k = g * GT + c
                    act.wait_ge(s_out, b * 16 + k + 1)
                    act.sem_inc(s_apart, 1)
                    act.copy(A[:, bass.ds(b * SEQ + k * D, D)], OP[:, 0:D])
                    act.copy(ssq[:, bass.ds(b * BT + k, 1)], OP[:, D:D + 1]).then_inc(s_oev, 1)

                row_begins(act, b)
                for j in range(3):
                    evict_in(0, j)
                    conv_sigmoid(0, j)
                evict_in(0, 3)
                evict_in(0, 4)
                evict_in(1, 0)
                evict_x(0)
                for k in range(BT):
                    g, c = divmod(k, GT)
                    if k + 1 < BT:
                        evict_x(k + 1)
                    if g >= 1:
                        evict_out(g - 1, c)
                    for gg_, jj in FILL[c]:
                        if g + gg_ < BG:
                            evict_in(g + gg_, jj)
                    if c < 3 and g + 1 < BG:
                        conv_sigmoid(g + 1, c)
                    if c == GT - 1:
                        if g >= 1:
                            act.wait_ge(s_out, b * 16 + GT * g)
                        for h in range(HEADS):
                            act.wait_ge(s_post, b * 8 + 2 * g + h + 1)
                            act.activation(YSQ[h], Y[h], ACT.Square).then_inc(s_ysq, 1)
                for c in range(GT):
                    evict_out(BG - 1, c)
                act.wait_ge(s_oev, b * 16 + BT)
                act.sem_inc(s_rows, 1)
            sqrt(SD[:, :], ssq[:, :])
            sqrt(SD[:, :], VR[:, :])
            sqrt(SD[:, :], VR[:, :])
            evict_T(1)
            act.wait_ge(s_ex, 1)
            act.activation(tw[:, :], tw[:, :], ACT.Exp).then_inc(s_exd, 1)
            for g in range(GROUPS):
                act.wait_ge(s_cwt, g + 1)
                act.copy(cwT[:, g * GW:(g + 1) * GW], PB[g % 2][0:E, :]).then_inc(s_cwe, 1)
            for g in range(GROUPS):
                act.wait_ge(s_bd, g + 1)
                act.copy(A[:, g * GW:(g + 1) * GW], PB[2 + g % 2][:, :]).then_inc(s_bde, 1)
            act.wait_ge(s_wl, 16)
            act.sem_inc(s_gl, 1)
            with act.Fori(0, E) as e:
                with act.Fori(0, GROUPS // 2) as q:
                    for i in range(2):
                        for c in range(HC):
                            n = i * HC + c
                            act.wait_ge(s_up, e * 32 + q * 8 + n + 1)
                            if c == 0:
                                act.wait_ge(s_dn, e * 32 + q * 8 + 1)
                            act.sem_inc(s_apart, 1)
                            act.activation(HB[i][:, c * GW:(c + 1) * GW], PB[c][:, :], ACT.Gelu,
                                           bias=WL[:, bass.ds(e * HC + (LATER_AT["bup"][0] + c), 1)]).then_inc(s_gl, 1)
            sqrt(SD[:, :], VR[:, :])
            sqrt(SD[:, :], VR[:, :])
            evict_T(2)
            act.wait_ge(s_T, 3 * GROUPS)
            for g in range(GROUPS):
                a, z = g * GW, (g + 1) * GW
                for i in range(2):
                    act.wait_ge(s_gt, 2 * g + i + 1)
                    act.activation(G[i][:, a:z], PB[2 + 2 * (g % 2) + i][:, :], ACT.Sigmoid,
                                   bias=wl("ig_b" if i == 0 else "ag_b")).then_inc(s_gs, 1)
            act.wait_ge(s_gs, 2 * GROUPS)
            for b in range(BATCH):
                a, z = b * SEQ, (b + 1) * SEQ
                act.activation(G[2][:, a:z], G[1][:, a:z], ACT.Exp, scale=lru_c[:, 0:1]).then_inc(s_aa, 1)
                act.activation(G[3][:, a:z], G[1][:, a:z], ACT.Exp, scale=lru_c2[:, 0:1]).then_inc(s_aa, 1)
            for b in range(BATCH):
                a, z = b * SEQ, (b + 1) * SEQ
                act.wait_ge(s_1a, b + 1)
                act.activation(G[3][:, a:z], G[3][:, a:z], ACT.Sqrt).then_inc(s_mu, 1)
            for g in range(GROUPS):
                act.wait_ge(s_ht, g + 1)
                act.copy(A[:, g * GW:(g + 1) * GW], PB[g % 2][:, :]).then_inc(s_he, 1)
            sqrt(SD[:, :], VR[:, :])
            sqrt(SD[:, :], VR[:, :])
            act.wait_ge(s_sct, 1)
            act.copy(sc32[:, :], PB[2][0:TILES, 0:P]).then_inc(s_sce, 1)
            sqrt(SD[:, :], VR[:, :])
            sqrt(c1[1][:, 1:2], c1[0][:, 1:2])
            sqrt(c1[1][:, 1:2], c1[0][:, 5:6])
            act.wait_ge(s_pd, 1)
            act.activation(hT[:, :], PB[0][:, 0:P], ACT.Copy, scale=wl("g1")).then_inc(s_ad, 1)
            act.wait_ge(s_pd, 2)
            act.copy(qT[:, :], PB[1][:, 0:P]).then_inc(s_ad, 1)
            act.wait_ge(s_pd, 3)
            act.copy(kT[:, :], PB[2][:, 0:P]).then_inc(s_ad, 1)
            act.wait_ge(s_pd, 4)
            act.copy(vv[:, :], PB[3][:, 0:P]).then_inc(s_ad, 1)
            act.wait_ge(s_vd, 3)
            act.activation(SM, SM, ACT.Exp, scale=float(HD) ** -0.5).then_inc(s_ad, 1)
            for i in range(4):
                act.wait_ge(s_pd, 8 + i + 1)
                act.copy(PT[:, i * 512:(i + 1) * 512], PB[i][:, :]).then_inc(s_ad, 1)
            act.wait_ge(s_pd, 14)
            act.copy(OT[:, :], PB[5][:, 0:P]).then_inc(s_ad, 1)
            sqrt(c1[1][:, 1:2], c1[0][:, 5:6])
            act.wait_ge(s_pd, 16)
            act.activation(hT[:, :], PB[0][:, 0:P], ACT.Copy, scale=wl("g2")).then_inc(s_ad, 1)
            act.wait_ge(s_pd, 17)
            for i in range(3):
                act.activation(u1[i][0:FC[i], :], PB[3][0:FC[i], i * P:(i + 1) * P], ACT.Silu).then_inc(s_ad, 1)
            sqrt(c1[1][:, 1:2], c1[0][:, 1:2])

        @block.tensor
        def _(pe):
            def transposes(r):
                for g in range(GROUPS):
                    pe.wait_ge(s_xn, r * GROUPS + g + 1)
                    if g >= 2:
                        pe.wait_ge(s_T, r * GROUPS + g - 1)
                    for t in range(GT):
                        i = pe.transpose(PB[g % 2][:, t * P:(t + 1) * P], NX[:, g * GW + t * D:g * GW + (t + 1) * D], ident[:, :])
                    i.then_inc(s_tr, 1)

            pe.wait_ge(s_const, 3)
            transposes(0)
            pe.wait_ge(s_wm, 16)
            pe.wait_ge(s_T, GROUPS)
            for t in range(TILES):
                i = pe.matmul(PB[2][:, 2 * t:2 * t + 2], T[:, t * P:(t + 1) * P], wm("win", 640, 642), start=True, stop=True)
            i.then_inc(s_dtp, 1)
            pe.wait_ge(s_sp, 1)

            pe.sem_inc(s_rows, 1)
            with pe.Fori(0, BATCH) as b:
                def project_in(g, j):
                    n = 5 * g + j
                    if n >= 1:
                        pe.wait_ge(s_ev, b * 20 + n)
                    c = [256, 384, 512, 0, 128][j]
                    pe.matmul(IN[:, :], wm("win", c, c + P), T[:, bass.ds(b * SEQ + g * GW, GW)],
                              start=True, stop=True).then_inc(s_in, 1)

                def front(k):
                    q, (g, c) = k % 2, divmod(k, GT)
                    tok = slice(c * P, (c + 1) * P)
                    pe.wait_ge(s_diag, b * 16 + k + 1)
                    if k >= 2:
                        pe.wait_ge(s_Bw, b * 16 + k - 1)
                    pe.matmul(FR[q][:, 0:256], ones[:, :], diag[q][:, :, :].rearrange("p h t -> p (h t)"),
                              start=True, stop=True).then_inc(s_dec, 1)
                    pe.wait_ge(s_xc, b * 12 + 3 * g + 3)
                    if k >= 1:
                        pe.wait_ge(s_xt, b * 16 + k)
                    for h in range(HEADS):
                        i = pe.transpose(XP[:, h * P:(h + 1) * P], xc[g % 2][h][:, tok], ident[:, :])
                    i.then_inc(s_tp, 1)
                    pe.wait_ge(s_c0, b * 64 + 16 * (g + 1))
                    pe.matmul(FR[q][:, 256 + NS:256 + NS + P], xc[g % 2][2][0:NS, tok], C0[g % 2][:, tok],
                              start=True, stop=True)
                    pe.transpose(FR[q][:, 256:256 + NS], xc[g % 2][2][0:NS, tok], ident[0:NS, 0:NS]).then_inc(s_g, 1)

                def back(k):
                    q, (g, c) = k % 2, divmod(k, GT)
                    tok = slice(c * P, (c + 1) * P)
                    pe.wait_ge(s_M, b * 16 + k + 1)
                    pe.wait_ge(s_xt, b * 16 + k + 1)
                    if g >= 1:
                        pe.wait_ge(s_post, b * 8 + 2 * g)
                    pe.wait_ge(s_CE, b * 16 + k + 1)
                    pe.wait_ge(s_upd, b * 34 + 2 * k + 2)
                    for h in range(HEADS):
                        a, z = h * P, (h + 1) * P
                        pe.matmul(YP[h][:, tok], XT[q][:, a:z], MB[q][:, h, :], start=True, stop=False)
                        pe.matmul(YP[h][:, tok], ST[q][:, a:z], CE[q][:, h, :], start=False, stop=True)
                    pe.wait_ge(s_Bw, b * 16 + k + 1)
                    for h in range(HEADS):
                        a, z = h * P, (h + 1) * P
                        i = pe.matmul(SP[0:NS, a:z], BW[q][:, h, :], XT[q][:, a:z], start=True, stop=True)
                    i.then_inc(s_S, 1)

                def project_out(g, c):
                    k = g * GT + c
                    tok = slice(c * P, (c + 1) * P)
                    pe.wait_ge(s_yf, b * 8 + 2 * g + 2)
                    pe.wait_ge(s_ysq, b * 8 + 2 * g + 2)
                    if k >= 1:
                        pe.wait_ge(s_oev, b * 16 + k)
                    for h in range(HEADS):
                        pe.matmul(OP[:, D:D + 1], YSQ[h][:, tok], ones[:, 0:1], start=(h == 0), stop=(h == 1))
                    for h in range(HEADS):
                        i = pe.matmul(OP[:, 0:D], YF[h][:, tok], wm("wout", h * P, (h + 1) * P),
                                      start=(h == 0), stop=(h == 1))
                    i.then_inc(s_out, 1)

                row_begins(pe, b)
                for j in range(5):
                    project_in(0, j)
                project_in(1, 0)
                front(0)
                for k in range(BT):
                    g, c = divmod(k, GT)
                    if k + 1 < BT:
                        front(k + 1)
                    if g >= 1:
                        project_out(g - 1, c)
                    for gg_, jj in FILL[c]:
                        if g + gg_ < BG:
                            project_in(g + gg_, jj)
                    back(k)
                for c in range(GT):
                    project_out(BG - 1, c)
                pe.wait_ge(s_out, b * 16 + BT)
                pe.sem_inc(s_rows, 1)

            transposes(1)
            pe.wait_ge(s_wl, 16)
            pe.wait_ge(s_T, 2 * GROUPS)
            for t in range(TILES):
                i = pe.matmul(PB[2][:, E * t:E * t + E], T[:, t * P:(t + 1) * P], wl("gate"), start=True, stop=True)
            i.then_inc(s_lg, 1)
            pe.wait_ge(s_cw, 1)
            for g in range(GROUPS):
                if g >= 2:
                    pe.wait_ge(s_cwe, g - 1)
                for t in range(GT):
                    k = g * GT + t
                    i = pe.transpose(PB[g % 2][0:E, t * P:(t + 1) * P], CW[:, E * k:E * k + E], ident[:, :])
                i.then_inc(s_cwt, 1)
            for g in range(GROUPS):
                pe.wait_ge(s_cwe, g + 1)
                if g >= 2:
                    pe.wait_ge(s_bde, g - 1)
                for t in range(GT):
                    k = g * GT + t
                    i = pe.matmul(PB[2 + g % 2][:, t * P:(t + 1) * P], cwT[:, k * P:(k + 1) * P], wl("bdown", rows=E),
                                  start=True, stop=True)
                i.then_inc(s_bd, 1)
            pe.wait_ge(s_bde, GROUPS)
            pe.sem_inc(s_dn, 1)
            with pe.Fori(0, E // 2) as j:
                for p in range(2):
                    pe.wait_ge(s_we[p], j * 32 + 32)
                    pe.sem_inc(s_apart, 1)
                    with pe.Fori(0, GROUPS // 2) as q:
                        for i in range(2):
                            for c in range(HC):
                                n = i * HC + c
                                if i == 0:
                                    if c == 0:
                                        pe.wait_ge(s_gl, j * 64 + p * 32 + q * 8 + 1)
                                else:
                                    pe.wait_ge(s_gl, j * 64 + p * 32 + q * 8 + n - 2)
                                pe.matmul(PB[c][:, :], wu[p][:, c * P:(c + 1) * P], T[:, bass.ds(q * (2 * GW) + i * GW, GW)],
                                          start=True, stop=True).then_inc(s_up, 1)
                        for i in range(2):
                            pe.wait_ge(s_gl, j * 64 + p * 32 + q * 8 + 4 * i + 5)
                            for t in range(GT):
                                if i == 0:
                                    pe.wait_ge(s_acc, j * 64 + p * 32 + q * 8 + 1)
                                else:
                                    pe.wait_ge(s_acc, j * 64 + p * 32 + q * 8 + t + 2)
                                for c in range(HC):
                                    ins = pe.matmul(PB[4 + t][:, 0:D], HB[i][:, c * GW + t * P:c * GW + (t + 1) * P],
                                                    wd[p][:, c * D:(c + 1) * D], start=(c == 0), stop=(c == HC - 1))
                                ins.then_inc(s_dn, 1)

            transposes(2)
            for g in range(GROUPS):
                pe.wait_ge(s_T, 2 * GROUPS + g + 1)
                if g >= 2:
                    pe.wait_ge(s_gs, 2 * (g - 1))
                for i, w in enumerate(("ig", "ag")):
                    pe.matmul(PB[2 + 2 * (g % 2) + i][:, :], wl(w), T[:, g * GW:(g + 1) * GW], start=True, stop=True).then_inc(s_gt, 1)
            for g in range(GROUPS):
                pe.wait_ge(s_h, g // BG + 1)
                if g >= 2:
                    pe.wait_ge(s_he, g - 1)
                for t in range(GT):
                    k = g * GT + t
                    c = (k // BT) * PW + (k % BT) * P
                    i = pe.transpose(PB[g % 2][:, t * P:(t + 1) * P], CP[:, c:c + P], ident[:, :])
                i.then_inc(s_ht, 1)
            pe.wait_ge(s_sc, 1)
            pe.transpose(PB[2][0:TILES, 0:P], sc[:, :], ident[:, :]).then_inc(s_sct, 1)
            pe.wait_ge(s_vd, 1)
            pe.transpose(PB[0][:, 0:P], HN[:, :], ident[:, :]).then_inc(s_pd, 1)
            pe.wait_ge(s_ad, 1)
            pe.matmul(PB[1][:, 0:P], wl("wqkv", 0, D), hT[:, :], start=True, stop=True).then_inc(s_pd, 1)
            pe.matmul(PB[2][:, 0:P], wl("wqkv", D, 2 * D), hT[:, :], start=True, stop=True).then_inc(s_pd, 1)
            pe.matmul(PB[3][:, 0:P], hT[:, :], wl("wqkv", 2 * D, 3 * D), start=True, stop=True).then_inc(s_pd, 1)
            pe.wait_ge(s_vd, 2)
            pe.wait_ge(s_ad, 4)
            for i in range(4):
                pe.matmul(PB[i][:, :], qT[:, :], kM[:, i * 512:(i + 1) * 512], start=True, stop=True).then_inc(s_pd, 1)
            pe.wait_ge(s_ad, 5)
            for i in range(4):
                for h in range(4):
                    k = 4 * i + h
                    m = pe.transpose(PB[i][:, h * P:(h + 1) * P], SM[:, k * P:(k + 1) * P], ident[:, :])
                m.then_inc(s_pd, 1)
            for h in range(AH):
                pe.wait_ge(s_ad, 6 + h // 4)
                m = pe.matmul(PB[4][:, h * HD:(h + 1) * HD], PT[:, h * P:(h + 1) * P], vv[:, h * HD:(h + 1) * HD],
                              start=True, stop=True)
            m.then_inc(s_pd, 1)
            pe.wait_ge(s_vd, 4)
            pe.transpose(PB[5][:, 0:P], O[:, :], ident[:, :]).then_inc(s_pd, 1)
            pe.wait_ge(s_ad, 10)
            pe.matmul(PB[5][:, 0:D], OT[:, :], wl("wo"), start=True, stop=True).then_inc(s_pd, 1)
            pe.wait_ge(s_vd, 5)
            pe.transpose(PB[0][:, 0:P], HN[:, :], ident[:, :]).then_inc(s_pd, 1)
            pe.wait_ge(s_ad, 11)
            at = [0, 128, 256]
            for i in range(3):
                pe.matmul(PB[3][0:FC[i], i * P:(i + 1) * P], wl("w1", at[i], at[i] + FC[i]), hT[:, :], start=True, stop=True)
            for i in range(3):
                m = pe.matmul(PB[4][0:FC[i], i * P:(i + 1) * P], wl("w2", at[i], at[i] + FC[i]), hT[:, :], start=True, stop=True)
            m.then_inc(s_pd, 1)
            for i in range(3):
                pe.wait_ge(s_vd, 6 + i)
                m = pe.matmul(PB[5][:, 0:D], gg[i][0:FC[i], :], wl("w3", i * D, (i + 1) * D, rows=FC[i]),
                              start=(i == 0), stop=(i == 2))
            m.then_inc(s_pd, 1)


def kernel(**inputs):
    import numpy as np
    import concourse.bacc as bacc
    from concourse.bass_utils import run_bass_kernel_spmd

    f = {k: np.asarray(a) for k, a in inputs.items()}

    def rows(a, n=P):
        return np.broadcast_to(a.reshape(1, -1), (n, a.size))

    def pad(a):
        z = np.zeros((P, a.shape[1]), np.float32)
        z[:a.shape[0]] = a
        return z

    def block_diagonal(w):
        n = w.shape[1]
        z = np.zeros((P, P), np.float32)
        for h in range(w.shape[0]):
            z[h * n:(h + 1) * n, h * n:(h + 1) * n] = w[h]
        return z

    win = f["L0_attn_in_proj_w"].T
    conv_w = f["L0_attn_conv_w"].reshape(3, P, TAPS).transpose(1, 0, 2).reshape(P, 12)
    mixer = {
        "win": win, "wout": f["L0_attn_out_w"].T.reshape(2, P, D).transpose(1, 0, 2).reshape(P, 2 * D),
        "conv_w": conv_w, "conv_b": f["L0_attn_conv_b"].reshape(3, P).T, "rms_w": f["L0_attn_rms_w"].reshape(2, P).T,
        "dt_bias": rows(f["L0_attn_dt_bias"]), "a_log": rows(f["L0_attn_A_log"]), "d_skip": rows(f["L0_attn_D"]),
        "a_param": f["L1_attn_a_param"].reshape(P, 1),
    }
    w3 = f["L1_ffn_W3"].T
    later = {
        "gate": f["L0_ffn_Wg"], "bup": f["L0_ffn_bup"].reshape(E, HC, P).transpose(2, 0, 1).reshape(P, E * HC),
        "bdown": pad(f["L0_ffn_bdown"]), "ig": block_diagonal(f["L1_attn_ig_w"]), "ag": block_diagonal(f["L1_attn_ag_w"]),
        "ig_b": f["L1_attn_ig_b"].reshape(P, 1), "ag_b": f["L1_attn_ag_b"].reshape(P, 1),
        "router": rows(f["L1_ffn_w_router"]), "wqkv": f["L1_ffn_W_qkv"].T, "wo": f["L1_ffn_W_out"].T,
        "g1": f["L1_ffn_g1"].reshape(P, 1), "g2": f["L1_ffn_g2"].reshape(P, 1),
        "w1": f["L1_ffn_W1"].T, "w2": f["L1_ffn_W2"].T,
        "w3": np.concatenate([pad(w3[128 * i:128 * i + n]) for i, n in enumerate(FC)], axis=1),
    }
    arrays = {
        "u": f["L0_attn_u"].reshape(TOKENS, D),
        "mixer_w": np.concatenate([mixer[n] for n, _ in MIXER_COLS], axis=1),
        "later_w": np.concatenate([later[n] for n, _ in LATER_COLS], axis=1),
        "wup": f["L0_ffn_Wup"],
        "wdown": f["L0_ffn_Wdown"].reshape(E, HC, P, D).transpose(0, 2, 1, 3).reshape(E, P, HC * D),
    }
    arrays = {k: np.ascontiguousarray(a) for k, a in arrays.items()}
    nc = bacc.Bacc("TRN2", target_bir_lowering=False, num_devices=1)
    args = [nc.dram_tensor(k, a.shape, F32, kind="ExternalInput").ap() for k, a in arrays.items()]
    out = nc.dram_tensor("out", (TOKENS, D), F32, kind="ExternalOutput").ap()
    build(nc, *args, out)
    r = run_bass_kernel_spmd(nc, [arrays], core_ids=[0])
    return r.results[0]["out"].reshape(BATCH, SEQ, D)
```

```python
from contextlib import ExitStack

import concourse.bass as bass
from concourse import mybir

F32 = mybir.dt.float32
F32R = mybir.dt.float32r
U32 = mybir.dt.uint32
I32 = mybir.dt.int32
ALU = mybir.AluOpType
ACT = mybir.ActivationFunctionType
AX = mybir.AxisListType

P = 128
BATCH, SEQ, D = 2, 2048, 128
TOKENS = BATCH * SEQ
TILES = TOKENS // P
BT = SEQ // P
GT = 4
GW = GT * P
GROUPS = TILES // GT
BG = BT // GT
HEADS, NS, DI = 2, 64, 256
TAPS = 4
RING = 4
E, HID, TOPK = 12, 512, 3
HC = HID // P
HT_ = (TOPK * SEQ + E * (P - 1)) // P
HT_ += -HT_ % RING
ST_ = 2 * HT_
CAP, AH, HD = 64, 16, 8
DFF = 341
FC = [128, 128, 85]
LN_EPS, RMS_EPS, FF_EPS = 1e-5, 1e-5, 1e-6

MIXER_COLS = [("win", 642), ("wout", 256), ("conv_w", 12), ("conv_b", 3), ("rms_w", 2),
              ("dt_bias", 2), ("a_log", 2), ("d_skip", 2), ("a_param", 1)]
LATER_COLS = [("gate", E), ("ig", P), ("ag", P), ("ig_b", 1), ("ag_b", 1),
              ("router", D), ("wqkv", 3 * D), ("wo", D), ("g1", 1), ("g2", 1), ("w1", DFF), ("w2", DFF),
              ("w3", 3 * D)]


def columns(cols):
    at, out = 0, {}
    for name, n in cols:
        out[name] = (at, at + n)
        at += n
    return out, at


MIXER_AT, MIXER_N = columns(MIXER_COLS)
LATER_AT, LATER_N = columns(LATER_COLS)


def build(nc, u, mixer_w, later_w, wup, wdown, bup, bdown, out):
    with ExitStack() as ctx:
        def sb(name, shape, dt=F32):
            return ctx.enter_context(nc.sbuf_tensor(name, shape, dt))

        def sem(name):
            return ctx.enter_context(nc.semaphore(name))

        X = sb("X", [P, TILES * D])
        A = sb("A", [P, TILES * D])
        T = sb("T", [P, TOKENS])
        F = sb("F", [P, 6 * TOKENS])
        NX = A
        WM = sb("WM", [P, MIXER_N])
        WL = sb("WL", [P, LATER_N])
        ident = sb("ident", [P, P])
        ones = sb("ones", [P, P])
        zeros = sb("zeros", [P, 1])
        st6 = sb("st6", [P, TILES * 6])
        MN = sb("MN", [P, TILES])
        DF = sb("DF", [P, TILES])
        VR = sb("VR", [P, TILES])
        SD = sb("SD", [P, TILES])
        RS = sb("RS", [P, TILES])
        NT = 2 * TILES + 1
        dt0 = sb("dt0", [P, NT])
        dt1 = sb("dt1", [P, NT])
        dt2 = sb("dt2", [P, NT])
        dt3 = sb("dt3", [P, NT])
        decay = sb("decay", [P, 2 * TILES])
        negA = sb("negA", [P, 2])
        lru_c = sb("lru_c", [P, 1])
        lru_c2 = sb("lru_c2", [P, 1])
        ssq = sb("ssq", [P, TILES])

        def wm(name, lo=0, hi=None, rows=P):
            a, b = MIXER_AT[name]
            return WM[0:rows, a + lo:(a + hi if hi is not None else b)]

        def wl(name, lo=0, hi=None, rows=P):
            a, b = LATER_AT[name]
            return WL[0:rows, a + lo:(a + hi if hi is not None else b)]

        at = [0]

        def carve(n):
            at[0] += n
            assert at[0] <= 6 * TOKENS
            return F[:, at[0] - n:at[0]]

        XW = SEQ + TAPS - 1
        xin = [carve(XW) for _ in range(3)]
        cv = [[carve(GW) for _ in range(3)] for _ in range(2)]
        sg = [carve(GW) for _ in range(2)]
        xc = [[carve(GW) for _ in range(3)] for _ in range(2)]
        sigz = [[carve(GW) for _ in range(2)] for _ in range(2)]
        Y = [carve(GW) for _ in range(2)]
        YSQ = [carve(GW) for _ in range(2)]
        YF = [carve(GW) for _ in range(2)]

        def carve3(a, b, rows=P):
            return carve(a * b)[0:rows, :].rearrange("p (a b) -> p a b", a=a)

        C0 = [carve(GW)[0:NS, :] for _ in range(2)]
        diag = [carve3(HEADS, P) for _ in range(2)]
        LB = [carve3(HEADS, P) for _ in range(2)]
        EB = [carve3(HEADS, P, NS) for _ in range(2)]
        MB = [carve3(HEADS, P) for _ in range(2)]
        BW = [carve3(HEADS, NS) for _ in range(2)]
        CE = [carve3(HEADS, P, NS) for _ in range(2)]
        XT = [carve(DI) for _ in range(2)]
        ST = [carve(DI)[0:NS, :] for _ in range(2)]

        WU = F[:, 0:E * HID]
        WD = F[:, E * HID:2 * E * HID]
        RG = F[:, 2 * E * HID:2 * E * HID + TOPK * TOKENS]
        LG = sb("LG", [P, TILES * E])
        route_at = [6 * TOKENS]

        def route(n):
            route_at[0] -= n
            return F[:, route_at[0]:route_at[0] + n]

        top8 = sb("top8", [P, TILES * 8])
        sel8 = sb("sel8", [P, TILES * 8], U32)
        self_ = sb("sel_f", [P, TILES * 8])
        tw = sb("tw", [P, TILES * TOPK])
        tsum = sb("tsum", [P, TILES])
        iotaE = sb("iotaE", [P, E])
        oh = [route(E * TILES) for _ in range(TOPK)]
        MK = route(E * TILES)
        PI = route(E * TILES)
        PO = route(E * TILES)
        OP_ = route(E * TILES)
        segE = sb("segE", [P, E * TILES])
        segB = sb("segB", [P, 2 * E])
        TCf = sb("TCf", [P, 2 * E])
        TCi = sb("TCi", [P, 2 * E], I32)
        BT0 = sb("BT0", [P, 2 * E])
        BS = sb("BS", [P, 2 * E])
        posf = sb("posf", [P, TOPK * TILES])
        posu = sb("posu", [P, TOPK * TILES], U32)
        iotaJ = sb("iotaJ", [P, HT_])
        GE = route(HT_ * E)
        etf = sb("etf", [P, ST_])
        eti = sb("eti", [P, ST_], I32)
        pidx = sb("pidx", [2 * 32, 1])
        SEL = sb("SEL", [2 * 32, ST_])
        upper = sb("upper", [P, P])
        biasr = sb("biasr", [2 * 32, HID + D])
        biash = sb("biash", [2 * 32, HID + D], F32R)
        biast = sb("biast", [2 * 32, HID + D])
        SELB = [sb(f"SELB{i}", [2 * 32, P], F32R) for i in range(RING)]
        zt = sb("zt", [P, 512])
        XG = [sb(f"XG{i}", [P, D]) for i in range(RING)]
        XGT = [sb(f"XGT{i}", [P, P]) for i in range(2)]
        WUB = [sb(f"WUB{i}", [P, HID]) for i in range(2)]
        HB = [sb(f"HB{i}", [P, HID]) for i in range(2)]
        YT = [sb(f"YT{i}", [P, D]) for i in range(RING)]
        slots_x = nc.dram_tensor("slots_x", [ST_ * P, D], F32, kind="Internal").ap()
        slots_y = nc.dram_tensor("slots_y", [ST_ * P, D], F32, kind="Internal").ap()

        G = [F[:, i * TOKENS:(i + 1) * TOKENS] for i in range(4)]
        PW = SEQ + 1
        CP = F[:, 4 * TOKENS:4 * TOKENS + BATCH * PW]

        sc = sb("sc", [P, TILES])
        sc32 = sb("sc32", [TILES, P])
        row = F[0:BATCH, 5 * TOKENS + BATCH:5 * TOKENS + BATCH + SEQ]
        v8 = sb("v8", [BATCH, CAP])
        i8 = sb("i8", [BATCH, CAP], U32)
        rowoff = sb("rowoff", [BATCH, 1])
        i8g = sb("i8g", [BATCH, CAP], U32)
        idx = sb("idx", [P, 1], U32)
        hmask = sb("hmask", [P, AH])
        amask = sb("amask", [P, P])
        XS = sb("XS", [P, D])
        XN = sb("XN", [P, D])
        SQ = sb("SQ", [P, D])
        HN = sb("HN", [P, D])
        hT = sb("hT", [P, P])
        qT = sb("qT", [P, P])
        kT = sb("kT", [P, P])
        vv = sb("vv", [P, P])
        kM = F[:, 0:AH * P]
        SM = F[:, AH * P:2 * AH * P]
        PT = F[:, 2 * AH * P:3 * AH * P]
        mx = sb("mx", [P, AH])
        sm = sb("sm", [P, AH])
        O = sb("O", [P, D])
        OT = sb("OT", [P, P])
        XA = sb("XA", [P, D])
        u1 = [sb(f"u1_{i}", [P, P]) for i in range(3)]
        gg = [sb(f"gg_{i}", [P, P]) for i in range(3)]
        PR = sb("PR", [P, D])
        c1 = [sb(f"c1_{i}", [P, 8]) for i in range(2)]

        PB = [ctx.enter_context(nc.psum_tensor(f"PB{i}", [P, 512], F32)) for i in range(8)]

        IN, XP, SP, OP = PB[0], PB[1], PB[4], PB[7]
        FR = [PB[2], PB[3]]
        YP = [PB[5], PB[6]]

        x3_dram = nc.dram_tensor("x3_scratch", [TOKENS, D], F32, kind="Internal").ap()

        s_apart = sem("s_apart")
        s_u = sem("s_u")
        s_wm = sem("s_wm")
        s_wl = sem("s_wl")
        s_const = sem("s_const")
        s_cstep = sem("s_cstep")
        s_stat = sem("s_stat")
        s_dve = sem("s_dve")
        s_var = sem("s_var")
        s_sd = sem("s_sd")
        s_xn = sem("s_xn")
        s_tr = sem("s_tr")
        s_T = sem("s_T")
        s_dtp = sem("s_dtp")
        s_sp = sem("s_sp")
        s_spa = sem("s_spa")
        s_decay = sem("s_decay")
        s_zero = sem("s_zero")
        s_in = sem("s_in")
        s_ev = sem("s_ev")
        s_conv = sem("s_conv")
        s_sig = sem("s_sig")
        s_xc = sem("s_xc")
        s_c0 = sem("s_c0")
        s_diag = sem("s_diag")
        s_dec = sem("s_dec")
        s_tp = sem("s_tp")
        s_g = sem("s_g")
        s_xt = sem("s_xt")
        s_L = sem("s_L")
        s_E = sem("s_E")
        s_M = sem("s_M")
        s_Bw = sem("s_Bw")
        s_CE = sem("s_CE")
        s_S = sem("s_S")
        s_upd = sem("s_upd")
        s_post = sem("s_post")
        s_ysq = sem("s_ysq")
        s_yf = sem("s_yf")
        s_out = sem("s_out")
        s_oev = sem("s_oev")
        s_res = sem("s_res")
        s_X = sem("s_X")
        s_lg = sem("s_lg")
        s_top = sem("s_top")
        s_ex = sem("s_ex")
        s_exd = sem("s_exd")
        s_wup = sem("s_wup")
        s_bias = sem("s_bias")
        s_bh = sem("s_bh")
        s_mk = sem("s_mk")
        s_rk = sem("s_rk")
        s_pos = sem("s_pos")
        s_et = sem("s_et")
        s_zf = sem("s_zf")
        s_sx = [sem(f"s_sx{h}") for h in range(2)]
        s_xl = [sem(f"s_xl{i}") for i in range(RING)]
        s_ys = [sem(f"s_ys{i}") for i in range(RING)]
        s_xp = sem("s_xp")
        s_xe = sem("s_xe")
        s_up = sem("s_up")
        s_gl = sem("s_gl")
        s_wb = sem("s_wb")
        s_dn = sem("s_dn")
        s_ye = sem("s_ye")
        s_rg0 = sem("s_rg0")
        s_rg1 = [sem(f"s_rg1_{g}") for g in range(BG)]
        s_cmb = sem("s_cmb")
        s_gt = sem("s_gt")
        s_gs = sem("s_gs")
        s_aa = sem("s_aa")
        s_1a = sem("s_1a")
        s_mu = sem("s_mu")
        s_xg = sem("s_xg")
        s_h = sem("s_h")
        s_ht = sem("s_ht")
        s_he = sem("s_he")
        s_wx = sem("s_wx")
        s_sc = sem("s_sc")
        s_sct = sem("s_sct")
        s_sce = sem("s_sce")
        s_row = sem("s_row")
        s_tk = sem("s_tk")
        s_idx = sem("s_idx")
        s_fin = sem("s_fin")
        s_st = sem("s_st")
        s_x3 = sem("s_x3")
        s_gat = sem("s_gat")
        s_sca = sem("s_sca")
        s_pd = sem("s_pd")
        s_vd = sem("s_vd")
        s_ad = sem("s_ad")

        s_rows = sem("s_rows")

        QS = ST_ // RING

        def tile(q, j):
            return q * RING + j, j % RING, q + j // RING

        def since(n, least=1):
            return n >= least if isinstance(n, int) else True

        def pipeline(eng, step):
            for i in range(RING):
                step(0, i)
            with eng.Fori(1, QS - 1) as q:
                for i in range(RING):
                    step(q, i)
            for i in range(RING):
                step(QS - 1, i)

        block = ctx.enter_context(nc.Block())

        def row_begins(eng, b):
            eng.wait_ge(s_rows, b * 5 + 5)
            eng.sem_inc(s_apart, 1)

        def cols(t, start, n):
            return t[:, bass.ds(start, n)]

        CB = [2, 0, 1]
        EARLY = [[], [], [(0, 4)], []]
        FILL = [[(1, 2)], [(0, 3)], [(2, 0)], [(2, 1)]]
        CONV = [[(1, 1)], [(1, 2)], [], [(2, 0)]]
        GATE = [[(1, 0)], [(1, 1)], [(1, 2)], []]
        BLOCKS = BG * 5
        block_order = [(0, 0), (0, 1), (0, 2), (1, 0), (1, 1)]
        for g_ in range(BG):
            for c_ in range(GT):
                block_order += [(g_ + a_, j_) for a_, j_ in EARLY[c_] + FILL[c_] if g_ + a_ < BG]
        assert len(block_order) == BLOCKS

        def carried(table, g, c):
            return [(g + ahead, j) for ahead, j in table[c] if g + ahead < BG]

        N_NORM = 3
        N_CONST = 15

        @block.sync
        def _(sp):
            uv = u.rearrange("(g t p) d -> g p t d", t=GT, p=P)
            for g in range(GROUPS):
                sp.dma_start(X[:, g * GW:(g + 1) * GW].rearrange("p (t d) -> p t d", t=GT), uv[g]).then_inc(s_u, 16)
                if g == 3:
                    sp.dma_start(WM[:, :], mixer_w).then_inc(s_wm, 16)
            sp.dma_start(WL[:, :], later_w).then_inc(s_wl, 16)

            sp.wait_ge(s_const, N_CONST)
            for h in range(2):
                sp.dma_start(slots_x[h * HT_ * P:(h + 1) * HT_ * P, :].rearrange("(p n) d -> p (n d)", p=P)
                             .rearrange("p (a b) -> p a b", b=512),
                             zt[:, :].unsqueeze(1).broadcast_to([P, HT_ * D // 512, 512])).then_inc(s_zf, 16)
            for q in range(2):
                sp.dma_start(biasr[32 * q:32 * q + E, 0:HID], bup).then_inc(s_bias, 16)
                sp.dma_start(biasr[32 * q:32 * q + E, HID:HID + D], bdown).then_inc(s_bias, 16)
            sp.sem_inc(s_rows, 1)
            with sp.Fori(0, BATCH) as b:
                row_begins(sp, b)
                for g in range(BG):
                    sp.wait_ge(s_xc, b * 12 + 3 * g + 1)
                    sp.sem_inc(s_apart, 1)
                    if g >= 2:
                        sp.wait_ge(s_CE, b * 16 + GT * (g - 1))
                        sp.sem_inc(s_apart, 1)
                        sp.wait_ge(s_g, b * 16 + GT * (g - 1))
                        sp.sem_inc(s_apart, 1)
                    if g >= 1:
                        sp.wait_ge(s_c0, b * 64 + 16 * g)
                        sp.sem_inc(s_apart, 1)
                    sp.dma_start(C0[g % 2][:, :], xc[g % 2][2][NS:2 * NS, :]).then_inc(s_c0, 16)
                sp.wait_ge(s_c0, b * 64 + 16 * BG)
                sp.sem_inc(s_rows, 1)
            sp.wait_ge(s_X, 1)
            for e in range(0, E, 3):
                sp.dma_start(WU[:, e * HID:(e + 3) * HID].rearrange("p (e n) -> p e n", e=3),
                             wup[e:e + 3].rearrange("e p n -> p e n")).then_inc(s_wup, 16)
                sp.dma_start(WD[:, e * HID:(e + 3) * HID].rearrange("p (e n) -> p e n", e=3),
                             wdown[e:e + 3].rearrange("e p n -> p e n")).then_inc(s_wup, 16)

            def load_slots(q, j):
                n, i, _ = tile(q, j)
                if since(n, RING):
                    sp.wait_ge(s_xp, n - RING + 1)
                    sp.sem_inc(s_apart, 1)
                src = slots_x[n * P:(n + 1) * P, :] if isinstance(n, int) else slots_x[bass.ds(n * P, P), :]
                sp.dma_start(XG[i][:, :], src).then_inc(s_xl[i], 16)

            sp.wait_ge(s_sx[0], 16 * TOPK * BT)
            for i in range(RING):
                load_slots(0, i)
            with sp.Fori(1, QS // 2) as q:
                for i in range(RING):
                    load_slots(q, i)
            sp.wait_ge(s_sx[1], 16 * TOPK * BT)
            with sp.Fori(QS // 2, QS) as q:
                for i in range(RING):
                    load_slots(q, i)
            sp.wait_ge(s_X, 8 * 3)
            sp.dma_start(x3_dram.rearrange("(t p) d -> p t d", p=P), X[:, :].rearrange("p (t d) -> p t d", t=TILES)).then_inc(s_x3, 16)
            sp.wait_ge(s_sce, 1)
            sp.dma_start(row[:, :].rearrange("b (t p) -> b t p", p=P), sc32[:, :]).then_inc(s_row, 16)
            ov = out.rearrange("(g t p) d -> g p t d", t=GT, p=P)
            for g in range(GROUPS):
                sp.wait_ge(s_fin, g + 1)
                sp.dma_start(ov[g], A[:, g * GW:(g + 1) * GW].rearrange("p (t d) -> p t d", t=GT)).then_inc(s_st, 16)
            sp.wait_ge(s_tk, 25)
            sp.dma_start(idx[:, :], i8g[:, :]).then_inc(s_idx, 16)
            sp.wait_ge(s_st, 16 * GROUPS)
            sp.wait_ge(s_sca, 16)

        @block.gpsimd
        def _(pool):
            pool.memset(ident[:, :], 0.0).then_inc(s_cstep, 1)
            pool.memset(ones[:, :], 1.0).then_inc(s_const, 1)
            pool.memset(zeros[:, :], 0.0).then_inc(s_const, 1)
            pool.memset(hmask[:, :], 1.0).then_inc(s_cstep, 1)
            pool.memset(amask[:, :], 0.0).then_inc(s_cstep, 1)
            pool.memset(upper[:, :], 1.0).then_inc(s_cstep, 1)
            pool.memset(segE[:, :], 1.0).then_inc(s_cstep, 1)
            pool.memset(segB[:, :], 1.0).then_inc(s_cstep, 1)
            pool.memset(zt[:, :], 0.0).then_inc(s_const, 1)
            pool.memset(biasr[:, :], 0.0).then_inc(s_const, 1)
            pool.wait_ge(s_cstep, 6)
            pool.affine_select(out=ident[:, :], in_=ident[:, :], compare_op=ALU.not_equal, fill=1.0, base=0,
                               pattern=[[-1, P]], channel_multiplier=1).then_inc(s_const, 1)
            pool.affine_select(out=hmask[:, :], in_=hmask[:, :], compare_op=ALU.is_ge, fill=0.0, base=0,
                               pattern=[[-HD, AH]], channel_multiplier=1).then_inc(s_cstep, 1)
            pool.affine_select(out=amask[:, :], in_=amask[:, :], compare_op=ALU.is_ge, fill=-1e30, base=0,
                               pattern=[[-1, P]], channel_multiplier=1).then_inc(s_cstep, 1)
            pool.affine_select(out=upper[:, :], in_=upper[:, :], compare_op=ALU.is_gt, fill=0.0, base=0,
                               pattern=[[1, P]], channel_multiplier=-1).then_inc(s_const, 1)
            pool.memset(segE[:, :].rearrange("p (s t) -> p s t", t=BT)[:, :, 0:1], 0.0).then_inc(s_const, 1)
            pool.memset(segB[:, :].rearrange("p (h e) -> p h e", h=2)[:, :, 0:1], 0.0).then_inc(s_const, 1)
            pool.iota(iotaJ[:, :], pattern=[[1, HT_]], base=0, channel_multiplier=0,
                      allow_small_or_imprecise_dtypes=True).then_inc(s_const, 1)
            pool.wait_ge(s_cstep, 8)
            pool.affine_select(out=hmask[:, :], in_=hmask[:, :], compare_op=ALU.is_ge, fill=0.0, base=HD - 1,
                               pattern=[[HD, AH]], channel_multiplier=-1).then_inc(s_const, 1)
            pool.wait_ge(s_const, 10)
            pool.memset(amask[CAP:P, 0:CAP], -1e30).then_inc(s_const, 1)
            pool.wait_ge(s_const, 11)
            pool.iota(iotaE[:, :], pattern=[[1, E]], base=0, channel_multiplier=0,
                      allow_small_or_imprecise_dtypes=True).then_inc(s_const, 1)
            pool.iota(rowoff[:, :], pattern=[[1, 1]], base=0, channel_multiplier=SEQ,
                      allow_small_or_imprecise_dtypes=True).then_inc(s_const, 1)
            for q in range(2):
                pool.wait_ge(s_const, 13 + q)
                pool.iota(pidx[32 * q:32 * q + 32, :], pattern=[[1, 1]], base=0, channel_multiplier=1,
                          allow_small_or_imprecise_dtypes=True).then_inc(s_const, 1)
            pool.wait_ge(s_const, N_CONST)
            for j in range(3):
                pool.memset(xin[j][:, 0:TAPS - 1], 0.0).then_inc(s_zero, 1)
            pool.wait_ge(s_const, N_CONST)
            pool.wait_ge(s_decay, 1)

            pool.sem_inc(s_rows, 1)
            with pool.Fori(0, BATCH) as b:
                def make_diag(k):
                    if k >= 2:
                        pool.wait_ge(s_dec, b * 16 + k - 1)
                    dk = decay[:, bass.ds(b * 32 + 2 * k, 2)]
                    pool.tensor_tensor(diag[k % 2][:, :, :], ident[:, :].unsqueeze(1).broadcast_to([P, HEADS, P]),
                                       dk.unsqueeze(2).broadcast_to([P, HEADS, P]), ALU.mult).then_inc(s_diag, 1)

                def silu(g, j):
                    n = 3 * g + j
                    pool.wait_ge(s_sig, b * 12 + n + 1)
                    if g >= 2 and j == 0:
                        pool.wait_ge(s_g, b * 16 + GT * (g - 1))
                        pool.wait_ge(s_c0, b * 64 + 16 * (g - 1))
                    elif g >= 2:
                        pool.wait_ge(s_post, b * 8 + 2 * (g - 1))
                    pool.tensor_tensor(xc[g % 2][CB[j]], cv[g % 2][CB[j]], sg[n % 2], ALU.mult).then_inc(s_xc, 1)

                def decayed_c(k):
                    g = k // GT
                    pool.wait_ge(s_c0, b * 64 + 16 * (g + 1))
                    pool.wait_ge(s_E, b * 32 + 2 * (k + 1))
                    if k >= 2:
                        pool.wait_ge(s_S, b * 16 + k - 1)
                    c = C0[g % 2][:, (k % GT) * P:(k % GT + 1) * P]
                    pool.tensor_tensor(CE[k % 2][:, :, :], c.unsqueeze(1).broadcast_to([NS, HEADS, P]),
                                       EB[k % 2][:, :, :], ALU.mult).then_inc(s_CE, 1)

                row_begins(pool, b)
                make_diag(0)
                make_diag(1)
                for j in range(3):
                    silu(0, j)
                decayed_c(0)
                for k in range(BT):
                    g, c = divmod(k, GT)
                    if k + 2 < BT:
                        make_diag(k + 2)
                    if k + 1 < BT:
                        decayed_c(k + 1)
                    for gj in carried(GATE, g, c):
                        silu(*gj)
                pool.wait_ge(s_CE, b * 16 + BT)
                pool.sem_inc(s_rows, 1)
            pool.wait_ge(s_xn, 2 * GROUPS)
            pool.wait_ge(s_pos, 1)
            pool.wait_ge(s_zf, 32)
            for h in range(2):
                for t in range(h * BT, (h + 1) * BT):
                    for k in range(TOPK):
                        c = k * TILES + t
                        pool.indirect_dma_start(slots_x, bass.IndirectOffsetOnAxis(posu[:, c:c + 1], 0),
                                                NX[:, t * D:(t + 1) * D], None).then_inc(s_sx[h], 16)
            for h in range(2):
                for i in range(RING):
                    pool.wait_ge(s_ys[i], 16 * (h + 1) * HT_ // RING)
                for t in range(h * BT, (h + 1) * BT):
                    done = s_rg0 if h == 0 else s_rg1[t // GT - BG]
                    for k in range(TOPK):
                        c = k * TILES + t
                        pool.indirect_dma_start(RG[:, (t * TOPK + k) * D:(t * TOPK + k + 1) * D], None, slots_y[0:(h + 1) * HT_ * P, :],
                                                bass.IndirectOffsetOnAxis(posu[:, c:c + 1], 0)).then_inc(done, 16)
            for b in range(BATCH):
                pool.wait_ge(s_gs, 8 * (b + 1))
                a, z = b * SEQ, (b + 1) * SEQ
                pool.tensor_tensor(G[0][:, a:z], T[:, a:z], G[0][:, a:z], ALU.mult).then_inc(s_xg, 1)
            rw = wl("router").unsqueeze(1).broadcast_to([P, BT, D])
            for b in range(BATCH):
                pool.wait_ge(s_xn, 8 * N_NORM + 4 * (b + 1))
                a, z = b * SEQ, (b + 1) * SEQ
                pool.tensor_tensor(G[1][:, a:z].rearrange("p (t d) -> p t d", d=D),
                                   NX[:, a:z].rearrange("p (t d) -> p t d", d=D), rw, ALU.mult).then_inc(s_wx, 1)
            pool.wait_ge(s_idx, 16)
            pool.wait_ge(s_x3, 16)
            pool.indirect_dma_start(XS[:, :], None, x3_dram, bass.IndirectOffsetOnAxis(idx[:, :], 0)).then_inc(s_gat, 16)
            pool.wait_ge(s_vd, 9)
            pool.wait_ge(s_st, 16 * GROUPS)
            pool.indirect_dma_start(out, bass.IndirectOffsetOnAxis(idx[:, :], 0), PR[:, :], None).then_inc(s_sca, 16)

        @block.vector
        def _(v):
            link = [0]
            nstat = [0]
            nvar = [0]

            def step(ins):
                ins.then_inc(s_dve, 1)
                link[0] += 1

            def settle():
                v.wait_ge(s_dve, link[0])

            def root(src, dst):
                nvar[0] += 1
                v.wait_ge(s_sd, nvar[0])
                step(v.reciprocal(dst, src))
                settle()

            def stats(src, eps):
                with v.Fori(0, GROUPS) as g:
                    for t in range(GT):
                        v.bn_stats(st6[:, bass.ds(g * GT * 6 + t * 6, 6)], cols(src, g * GW + t * D, D)).then_inc(s_stat, 1)
                nstat[0] += TILES
                v.wait_ge(s_stat, nstat[0])
                s6 = st6[:, :].rearrange("p (t s) -> p t s", s=6)
                step(v.tensor_tensor(MN[:, :], s6[:, :, 1], s6[:, :, 4], ALU.add))
                step(v.tensor_tensor(DF[:, :], s6[:, :, 1], s6[:, :, 4], ALU.subtract))
                step(v.tensor_tensor(VR[:, :], s6[:, :, 2], s6[:, :, 5], ALU.add))
                settle()
                step(v.tensor_scalar(MN[:, :], MN[:, :], 0.5, None, ALU.mult))
                step(v.scalar_tensor_tensor(DF[:, :], DF[:, :], 0.25, DF[:, :], ALU.mult, ALU.mult))
                step(v.tensor_scalar(VR[:, :], VR[:, :], 1.0 / D, eps, ALU.mult, ALU.add))
                settle()

            def to_root():
                v.tensor_tensor(VR[:, :], VR[:, :], DF[:, :], ALU.add).then_inc(s_var, 1)

            def norm(r):
                stats(X, LN_EPS)
                to_root()
                root(SD[:, :], RS[:, :])
                with v.Fori(0, GROUPS) as g:
                    for t in range(GT):
                        i = v.tensor_scalar(NX[:, bass.ds(g * GW + t * D, D)], cols(X, g * GW + t * D, D),
                                            MN[:, bass.ds(g * GT + t, 1)], RS[:, bass.ds(g * GT + t, 1)],
                                            ALU.subtract, ALU.mult)
                        if t == GT - 1:
                            i.then_inc(s_xn, 1)
                v.wait_ge(s_xn, GROUPS * (r + 1))

            def residual(e):
                with v.Fori(0, GROUPS) as g:
                    for t in range(GT):
                        a = cols(A, g * GW + t * D, D)
                        v.tensor_scalar(a, a, MN[:, bass.ds(g * GT + t, 1)], RS[:, bass.ds(g * GT + t, 1)],
                                        ALU.subtract, ALU.mult).then_inc(s_res, 1)
                v.wait_ge(s_res, TILES * (e + 1))
                with v.Fori(0, GROUPS) as g:
                    x = cols(X, g * GW, GW)
                    v.tensor_tensor(x, x, cols(A, g * GW, GW), ALU.add).then_inc(s_X, 1)
                v.wait_ge(s_X, GROUPS * (e + 1))

            v.wait_ge(s_u, 16 * GROUPS)
            norm(0)

            v.wait_ge(s_wm, 16)
            v.wait_ge(s_dtp, 1)
            N2 = 2 * TILES
            step(v.tensor_tensor(dt0[:, 0:N2].rearrange("p (t h) -> p t h", h=2),
                                 PB[2][:, 0:N2].rearrange("p (t h) -> p t h", h=2),
                                 wm("dt_bias").unsqueeze(1).broadcast_to([P, TILES, 2]), ALU.add))
            step(v.tensor_copy(dt0[:, N2:NT], wm("a_param")))
            settle()
            step(v.tensor_scalar(dt1[:, :], dt0[:, :], -1.0, None, ALU.mult))
            settle()
            v.tensor_tensor(dt1[:, :], dt1[:, :], dt0[:, :], ALU.min).then_inc(s_sp, 1)
            v.wait_ge(s_spa, 1)
            v.tensor_scalar(dt2[:, :], dt1[:, :], 1.0, None, ALU.add).then_inc(s_sp, 1)
            v.wait_ge(s_sp, 2)
            step(v.tensor_scalar(dt3[:, :], dt2[:, :], -1.0, None, ALU.add))
            settle()
            step(v.tensor_tensor(dt3[:, :], dt1[:, :], dt3[:, :], ALU.subtract))
            v.wait_ge(s_spa, 2)
            settle()
            step(v.reciprocal(dt1[:, :], dt2[:, :]))
            settle()
            step(v.tensor_tensor(dt3[:, :], dt3[:, :], dt1[:, :], ALU.mult))
            step(v.tensor_scalar(dt0[:, :], dt0[:, :], 0.0, None, ALU.max))
            settle()
            step(v.tensor_tensor(dt3[:, :], dt3[:, :], LG[:, 0:NT], ALU.add))
            settle()
            step(v.tensor_tensor(dt3[:, :], dt3[:, :], dt0[:, :], ALU.add))
            v.wait_ge(s_spa, 3)
            settle()
            step(v.tensor_scalar(lru_c[:, :], dt3[:, N2:NT], -8.0, None, ALU.mult))
            step(v.tensor_scalar(lru_c2[:, :], dt3[:, N2:NT], -16.0, None, ALU.mult))
            v.scalar_tensor_tensor(dt2[:, 0:N2].rearrange("p (t h) -> p t h", h=2),
                                   dt3[:, 0:N2].rearrange("p (t h) -> p t h", h=2), -1.0,
                                   negA[:, :].unsqueeze(1).broadcast_to([P, TILES, 2]), ALU.mult, ALU.mult).then_inc(s_sp, 1)
            v.wait_ge(s_zero, 3)
            v.wait_ge(s_const, N_CONST)

            v.sem_inc(s_rows, 1)
            with v.Fori(0, BATCH) as b:
                def conv(g, j):
                    n = 3 * g + j
                    v.wait_ge(s_ev, b * 20 + block_order.index((g, j)) + 1)
                    if g >= 2:
                        v.wait_ge(s_xc, b * 12 + n - 5)
                    j = CB[j]
                    o = cv[g % 2][j]
                    for k in range(TAPS):
                        i = xin[j][:, g * GW + k:g * GW + k + GW]
                        w = wm("conv_w", 4 * j + k, 4 * j + k + 1)
                        if k == 0:
                            v.tensor_scalar(o, i, w, wm("conv_b", j, j + 1), ALU.mult, ALU.add).then_inc(s_conv, 1)
                        else:
                            v.wait_ge(s_conv, b * 48 + 4 * n + k)
                            v.scalar_tensor_tensor(o, i, w, o, ALU.mult, ALU.add).then_inc(s_conv, 1)

                def front(k):
                    q = k % 2
                    dec = FR[q][:, 0:256].rearrange("p (h t) -> p h t", h=2)
                    v.wait_ge(s_g, b * 16 + k + 1)
                    if k >= 2:
                        v.wait_ge(s_Bw, b * 16 + k - 1)
                    for h in range(HEADS):
                        v.tensor_tensor_scan(LB[q][:, h, :], dec[:, h, :], ident[:, :], 0.0, ALU.mult, ALU.add).then_inc(s_L, 1)
                    if k >= 2:
                        v.wait_ge(s_CE, b * 16 + k - 1)
                        v.wait_ge(s_upd, b * 34 + 2 * k)
                    for h in range(HEADS):
                        v.tensor_tensor_scan(EB[q][:, h, :], dec[0:NS, h, :], zeros[0:NS, :].broadcast_to([NS, P]),
                                             1.0, ALU.mult, ALU.add).then_inc(s_E, 1)
                    v.wait_ge(s_L, b * 32 + 2 * k + 2)
                    if k >= 2:
                        v.wait_ge(s_S, b * 16 + k - 1)
                    gp = FR[q][:, 256:256 + NS + P]
                    v.tensor_tensor(MB[q][:, :, :], LB[q][:, :, :], gp[:, NS:NS + P].unsqueeze(1).broadcast_to([P, HEADS, P]),
                                    ALU.mult).then_inc(s_M, 1)
                    v.tensor_tensor(BW[q][:, :, :], LB[q][:, :, P - 1:P].broadcast_to([P, HEADS, NS]),
                                    gp[:, 0:NS].unsqueeze(1).broadcast_to([P, HEADS, NS]), ALU.mult).then_inc(s_Bw, 1)

                def back(k):
                    q = k % 2
                    v.wait_ge(s_S, b * 16 + k + 1)
                    v.wait_ge(s_E, b * 32 + 2 * k + 2)
                    v.wait_ge(s_upd, b * 34 + 2 * k + 2)
                    for h in range(HEADS):
                        a, z = h * P, (h + 1) * P
                        v.scalar_tensor_tensor(ST[1 - q][:, a:z], ST[q][:, a:z], EB[q][:, h, P - 1:P],
                                               SP[0:NS, a:z], ALU.mult, ALU.add).then_inc(s_upd, 1)

                def post(g):
                    for h in range(HEADS):
                        if g >= 1:
                            v.wait_ge(s_ysq, b * 8 + 2 * g)
                            v.wait_ge(s_yf, b * 8 + 2 * g)
                        v.scalar_tensor_tensor(Y[h], xc[g % 2][h], wm("d_skip", h, h + 1), YP[h][:, :],
                                               ALU.mult, ALU.add).then_inc(s_post, 1)
                    v.wait_ge(s_post, b * 8 + 2 * g + 2)
                    v.wait_ge(s_ev, b * 20 + block_order.index((g, 4)) + 1)
                    if g >= 1:
                        v.wait_ge(s_out, b * 16 + GT * g)
                    for h in range(HEADS):
                        v.scalar_tensor_tensor(YF[h], Y[h], wm("rms_w", h, h + 1), sigz[g % 2][h],
                                               ALU.mult, ALU.mult).then_inc(s_yf, 1)

                row_begins(v, b)
                v.memset(ST[0][:, 0:P], 0.0).then_inc(s_upd, 1)
                v.memset(ST[0][:, P:DI], 0.0).then_inc(s_upd, 1)
                for j in range(3):
                    conv(0, j)
                front(0)
                conv(1, 0)
                for k in range(BT):
                    g, c = divmod(k, GT)
                    if k + 1 < BT:
                        front(k + 1)
                    for gj in carried(CONV, g, c):
                        conv(*gj)
                    back(k)
                    if c == GT - 1:
                        post(g)
                v.wait_ge(s_yf, b * 8 + 8)
                v.wait_ge(s_upd, b * 34 + 34)
                v.sem_inc(s_rows, 1)

            v.wait_ge(s_oev, TILES)
            v.tensor_scalar(ssq[:, :], ssq[:, :], 1.0 / DI, RMS_EPS, ALU.mult, ALU.add).then_inc(s_var, 1)
            root(SD[:, :], ssq[:, :])
            stats(A, 0.0)
            step(v.tensor_tensor(VR[:, :], VR[:, :], DF[:, :], ALU.add))
            settle()
            step(v.tensor_tensor(VR[:, :], VR[:, :], ssq[:, :], ALU.mult))
            settle()
            step(v.tensor_tensor(VR[:, :], VR[:, :], ssq[:, :], ALU.mult))
            settle()
            v.tensor_scalar(VR[:, :], VR[:, :], LN_EPS, None, ALU.add).then_inc(s_var, 1)
            root(SD[:, :], RS[:, :])
            step(v.tensor_tensor(RS[:, :], RS[:, :], ssq[:, :], ALU.mult))
            settle()
            residual(0)
            norm(1)

            v.wait_ge(s_lg, 1)
            step(v.tensor_copy(LG[:, :], PB[2][:, 0:TILES * E]))
            settle()
            for t in range(TILES):
                step(v.max(top8[:, 8 * t:8 * t + 8], LG[:, E * t:E * t + E]))
            settle()
            for t in range(TILES):
                step(v.max_index(sel8[:, 8 * t:8 * t + 8], top8[:, 8 * t:8 * t + 8], LG[:, E * t:E * t + E]))
            t8 = top8[:, :].rearrange("p (t k) -> p t k", k=8)
            tw3 = tw[:, :].rearrange("p (t k) -> p t k", k=TOPK)
            v.tensor_tensor(tw3, t8[:, :, 0:TOPK], t8[:, :, 0:1].broadcast_to([P, TILES, TOPK]), ALU.subtract).then_inc(s_ex, 1)
            settle()
            step(v.tensor_copy(self_[:, :], sel8[:, :]))
            v.wait_ge(s_exd, 1)
            step(v.tensor_reduce(tsum[:, :], tw3, AX.X, ALU.add))
            settle()
            step(v.reciprocal(tsum[:, :], tsum[:, :]))
            settle()
            step(v.tensor_tensor(tw3, tw3, tsum[:, :].unsqueeze(2).broadcast_to([P, TILES, TOPK]), ALU.mult))
            s8 = self_[:, :].rearrange("p (t k) -> p t k", k=8)
            for k in range(TOPK):
                step(v.tensor_tensor(oh[k][:, :].rearrange("p (e t) -> p e t", e=E),
                                     iotaE[:, :].unsqueeze(2).broadcast_to([P, E, TILES]),
                                     s8[:, :, k:k + 1].rearrange("p t k -> p k t").broadcast_to([P, E, TILES]), ALU.is_equal))
            settle()
            step(v.tensor_tensor(MK[:, :], oh[0][:, :], oh[1][:, :], ALU.add))
            settle()
            v.tensor_tensor(MK[:, :], MK[:, :], oh[2][:, :], ALU.add).then_inc(s_mk, 1)
            NEC = E * TILES
            v.wait_ge(s_rk, 1)
            step(v.tensor_tensor_scan(PI[:, :], segE[:, :], PB[3][:, 0:NEC], 0.0, ALU.mult, ALU.add))
            settle()
            step(v.tensor_tensor(PO[:, :], PI[:, :], PB[3][:, 0:NEC], ALU.subtract))
            n_e = PI[:, :].rearrange("p (e h t) -> p h e t", e=E, h=2)[:, :, :, BT - 1]
            step(v.tensor_scalar(TCi[:, :].rearrange("p (h e) -> p h e", h=2), n_e, 1.0 / P,
                                 127.0 / P - 0.5 + 1.0 / 256, ALU.mult, ALU.add))
            settle()
            step(v.tensor_copy(TCf[:, :], TCi[:, :]))
            step(v.tensor_tensor(PO[:, :], PO[:, :], PB[2][:, 0:NEC], ALU.add))
            settle()
            step(v.tensor_tensor_scan(BT0[:, :], segB[:, :], TCf[:, :], 0.0, ALU.mult, ALU.add))
            settle()
            step(v.tensor_tensor(BT0[:, :], BT0[:, :], TCf[:, :], ALU.subtract))
            settle()
            for h in range(2):
                hs = slice(h * E, (h + 1) * E)
                step(v.tensor_scalar(BS[:, hs], BT0[:, hs], float(P), float(h * HT_ * P), ALU.mult, ALU.add))
            settle()
            for h in range(2):
                po = PO[:, :].rearrange("p (e h t) -> p e h t", e=E, h=2)[:, :, h, :]
                step(v.tensor_tensor(po, po, BS[:, h * E:(h + 1) * E].unsqueeze(2).broadcast_to([P, E, BT]), ALU.add))
            settle()
            for k in range(TOPK):
                step(v.tensor_tensor(OP_[:, :], oh[k][:, :], PO[:, :], ALU.mult))
                settle()
                step(v.tensor_reduce(posf[:, k * TILES:(k + 1) * TILES], OP_[:, :].rearrange("p (e t) -> p t e", e=E),
                                     AX.X, ALU.add))
                settle()
            v.tensor_copy(posu[:, :], posf[:, :]).then_inc(s_pos, 1)
            for h in range(2):
                ge = GE[:, :].rearrange("p (j e) -> p j e", e=E)
                step(v.tensor_tensor(ge, iotaJ[:, :].unsqueeze(2).broadcast_to([P, HT_, E]),
                                     BT0[:, h * E:(h + 1) * E].unsqueeze(1).broadcast_to([P, HT_, E]), ALU.is_ge))
                settle()
                step(v.tensor_reduce(etf[:, h * HT_:(h + 1) * HT_], ge, AX.X, ALU.add))
                settle()
            step(v.tensor_scalar(etf[:, :], etf[:, :], -1.0, None, ALU.add))
            settle()
            v.tensor_copy(eti[:, :], etf[:, :]).then_inc(s_et, 1)
            step(v.tensor_scalar(SEL[:, :], etf[0:64, :], pidx[:, :], None, ALU.is_equal))
            v.wait_ge(s_bias, 64)
            step(v.tensor_copy(biash[:, :], biasr[:, :]))
            settle()
            step(v.tensor_copy(biast[32:64, :], biash[32:64, :].bitcast(F32)))
            settle()
            v.tensor_tensor(biash[32:64, :], biasr[32:64, :], biast[32:64, :], ALU.subtract).then_inc(s_bh, 1)
            settle()

            def evict_slots(q, j):
                n, i, _ = tile(q, j)
                v.wait_ge(s_xp, n + 1)
                if since(n - 1):
                    v.wait_ge(s_up, n - 1)
                v.tensor_copy(XGT[i % 2][:, :], PB[i % 2][:, 0:P]).then_inc(s_xe, 1)
                if since(n - 3):
                    v.wait_ge(s_dn, n - 3)
                col = SEL[:, n:n + 1] if isinstance(n, int) else SEL[:, bass.ds(n, 1)]
                v.tensor_copy(SELB[i][:, :], col.broadcast_to([64, P])).then_inc(s_xe, 1)

            def evict_result(q, j):
                n, i, turn = tile(q, j)
                v.wait_ge(s_dn, n + 1)
                if since(turn):
                    v.wait_ge(s_ys[i], turn * 16)
                v.tensor_copy(YT[i][:, :], PB[6 + i % 2][:, 0:D]).then_inc(s_ye, 1)

            def dve_step(q, i):
                if not (isinstance(q, int) and q * RING + i + 2 >= ST_):
                    evict_slots(q, i + 2)
                evict_result(q, i)

            evict_slots(0, 0)
            evict_slots(0, 1)
            pipeline(v, dve_step)

            tw3 = tw[:, :].rearrange("p (t k) -> p t k", k=TOPK)
            for g in range(GROUPS):
                if g < BG:
                    v.wait_ge(s_rg0, 16 * TOPK * BT)
                else:
                    v.wait_ge(s_rg1[g - BG], 16 * TOPK * GT)
                for k in range(TOPK):
                    for t in range(g * GT, (g + 1) * GT):
                        r = RG[:, (t * TOPK + k) * D:(t * TOPK + k + 1) * D]
                        a, w = A[:, t * D:(t + 1) * D], tw3[:, t, k:k + 1]
                        if k == 0:
                            v.tensor_scalar(a, r, w, None, ALU.mult).then_inc(s_cmb, 1)
                        else:
                            v.wait_ge(s_cmb, g * GT * TOPK + (k - 1) * GT + t % GT + 1)
                            v.scalar_tensor_tensor(a, r, w, a, ALU.mult, ALU.add).then_inc(s_cmb, 1)
            v.wait_ge(s_cmb, TILES * TOPK)
            stats(A, LN_EPS)
            to_root()
            root(SD[:, :], RS[:, :])
            residual(1)
            norm(2)

            v.wait_ge(s_T, 3 * GROUPS)
            for b in range(BATCH):
                a, z = b * SEQ, (b + 1) * SEQ
                pa, pz = b * PW, b * PW + SEQ
                step(v.memset(CP[:, pa:pa + 1], 1.0))
                v.wait_ge(s_aa, 2 * b + 1)
                step(v.tensor_tensor_scan(CP[:, pa + 1:pz + 1], G[2][:, a:z], zeros[:, :].broadcast_to([P, SEQ]),
                                          1.0, ALU.mult, ALU.add))
                v.wait_ge(s_aa, 2 * b + 2)
                step(v.tensor_scalar(G[3][:, a:z], G[3][:, a:z], -1.0, 1.0, ALU.mult, ALU.add))
                settle()
                v.tensor_scalar(G[3][:, a:z], G[3][:, a:z], 1e-7, None, ALU.max).then_inc(s_1a, 1)
                step(v.tensor_scalar(G[1][:, a:z], CP[:, pa:pz], 1e-7, None, ALU.max))
                settle()
                step(v.reciprocal(G[2][:, a:z], G[1][:, a:z]))
                v.wait_ge(s_mu, b + 1)
                v.wait_ge(s_xg, b + 1)
                step(v.tensor_tensor(G[0][:, a:z], G[0][:, a:z], G[3][:, a:z], ALU.mult))
                settle()
                step(v.tensor_tensor(G[0][:, a:z], G[0][:, a:z], G[2][:, a:z], ALU.mult))
                settle()
                step(v.tensor_tensor_scan(G[3][:, a:z], G[0][:, a:z], zeros[:, :].broadcast_to([P, SEQ]),
                                          0.0, ALU.add, ALU.add))
                settle()
                v.tensor_tensor(CP[:, pa:pz], G[1][:, a:z], G[3][:, a:z], ALU.mult).then_inc(s_h, 1)
            v.wait_ge(s_he, GROUPS)
            stats(A, LN_EPS)
            to_root()
            root(SD[:, :], RS[:, :])
            residual(2)
            norm(3)

            for b in range(BATCH):
                a, z = b * SEQ, (b + 1) * SEQ
                v.wait_ge(s_wx, b + 1)
                step(v.tensor_reduce(sc[:, b * BT:(b + 1) * BT], G[1][:, a:z].rearrange("p (t d) -> p t d", d=D), AX.X, ALU.add))
            v.wait_ge(s_dve, link[0])
            v.sem_inc(s_sc, 1)
            v.wait_ge(s_xn, GROUPS * 4)
            stats(NX, LN_EPS)
            to_root()
            root(SD[:, :], RS[:, :])
            for g in range(GROUPS):
                for t in range(GT):
                    i = g * GT + t
                    step(v.tensor_scalar(A[:, i * D:(i + 1) * D], NX[:, i * D:(i + 1) * D], MN[:, i:i + 1], RS[:, i:i + 1],
                                         ALU.subtract, ALU.mult))
                settle()
                a = A[:, g * GW:(g + 1) * GW]
                v.tensor_tensor(a, a, X[:, g * GW:(g + 1) * GW], ALU.add).then_inc(s_fin, 1)

            v.wait_ge(s_row, 16)
            for r in range(CAP // 8):
                k8 = slice(8 * r, 8 * r + 8)
                v.max(v8[:, k8], row[:, :]).then_inc(s_tk, 1)
                v.wait_ge(s_tk, 3 * r + 1)
                v.max_index(i8[:, k8], v8[:, k8], row[:, :]).then_inc(s_tk, 1)
                v.wait_ge(s_tk, 3 * r + 2)
                v.match_replace(row[:, :], v8[:, k8], row[:, :], -3.0e38).then_inc(s_tk, 1)
                v.wait_ge(s_tk, 3 * r + 3)
            v.tensor_scalar(i8g[:, :], i8[:, :], rowoff[:, 0:1], None, ALU.add).then_inc(s_tk, 1)

            vd = [0]

            def vstep(ins):
                ins.then_inc(s_vd, 1)
                vd[0] += 1

            def vsettle():
                v.wait_ge(s_vd, vd[0])

            def row_stats(src, eps):
                step(v.bn_stats(st6[:, 0:6], src))
                settle()
                step(v.bn_aggr(c1[0][:, 0:2], st6[:, 0:6]))
                settle()
                v.tensor_scalar(c1[0][:, 1:2], c1[0][:, 1:2], eps, None, ALU.add).then_inc(s_var, 1)
                root(c1[1][:, 1:2], c1[1][:, 2:3])

            def row_norm(dst, src, eps):
                row_stats(src, eps)
                step(v.tensor_scalar(dst, src, c1[0][:, 0:1], c1[1][:, 2:3], ALU.subtract, ALU.mult))
                settle()

            def rms(dst, src):
                step(v.tensor_tensor(SQ[:, :], src, src, ALU.mult))
                settle()
                step(v.tensor_reduce(c1[0][:, 4:5], SQ[:, :], AX.X, ALU.add))
                settle()
                v.tensor_scalar(c1[0][:, 5:6], c1[0][:, 4:5], 1.0 / D, FF_EPS, ALU.mult, ALU.add).then_inc(s_var, 1)
                root(c1[1][:, 1:2], c1[1][:, 3:4])
                vstep(v.tensor_scalar(dst, src, c1[1][:, 3:4], None, ALU.mult))

            v.wait_ge(s_gat, 16)
            row_norm(XN[:, :], XS[:, :], LN_EPS)
            rms(HN[:, :], XN[:, :])
            v.wait_ge(s_ad, 3)
            kM3 = kM.rearrange("p (h k) -> p h k", h=AH)
            vstep(v.tensor_tensor(kM3, kT[:, :].unsqueeze(1).broadcast_to([P, AH, P]),
                                  hmask[:, :].unsqueeze(2).broadcast_to([P, AH, P]), ALU.mult))
            for i in range(4):
                v.wait_ge(s_pd, 4 + i + 1)
                step(v.tensor_tensor(SM[:, i * 512:(i + 1) * 512].rearrange("p (h k) -> p h k", h=4),
                                     PB[i][:, :].rearrange("p (h k) -> p h k", h=4),
                                     amask[:, :].unsqueeze(1).broadcast_to([P, 4, P]), ALU.add))
            settle()
            SM3 = SM.rearrange("p (h k) -> p h k", h=AH)
            step(v.tensor_reduce(mx[:, :], SM3, AX.X, ALU.max))
            settle()
            vstep(v.tensor_tensor(SM3, SM3, mx[:, :].unsqueeze(2).broadcast_to([P, AH, P]), ALU.subtract))
            v.wait_ge(s_ad, 5)
            step(v.tensor_reduce(sm[:, :], SM3, AX.X, ALU.add))
            settle()
            step(v.reciprocal(sm[:, :], sm[:, :]))
            settle()
            v.wait_ge(s_pd, 13)
            vstep(v.tensor_tensor(O[:, :].rearrange("p (h d) -> p h d", h=AH),
                                  PB[4][:, 0:D].rearrange("p (h d) -> p h d", h=AH),
                                  sm[:, :].unsqueeze(2).broadcast_to([P, AH, HD]), ALU.mult))
            v.wait_ge(s_pd, 15)
            step(v.tensor_tensor(XA[:, :], XN[:, :], PB[5][:, 0:D], ALU.add))
            settle()
            rms(HN[:, :], XA[:, :])
            for i in range(3):
                v.wait_ge(s_ad, 12 + i)
                vstep(v.tensor_tensor(gg[i][0:FC[i], :], u1[i][0:FC[i], :], PB[4][0:FC[i], i * P:(i + 1) * P], ALU.mult))
            v.wait_ge(s_pd, 18)
            step(v.tensor_tensor(PR[:, :], XA[:, :], PB[5][:, 0:D], ALU.add))
            settle()
            row_norm(PR[:, :], PR[:, :], LN_EPS)
            vstep(v.tensor_tensor(PR[:, :], PR[:, :], XS[:, :], ALU.add))
            assert vd[0] == 9, vd

        @block.scalar
        def _(act):
            nvar = [0]

            def sqrt(dst, src):
                nvar[0] += 1
                act.wait_ge(s_var, nvar[0])
                act.activation(dst, src, ACT.Sqrt).then_inc(s_sd, 1)

            def evict_T(r):
                for g in range(GROUPS):
                    act.wait_ge(s_tr, r * GROUPS + g + 1)
                    act.copy(T[:, g * GW:(g + 1) * GW], PB[g % 2][:, :]).then_inc(s_T, 1)

            sqrt(SD[:, :], VR[:, :])
            evict_T(0)
            act.wait_ge(s_sp, 1)
            act.activation(dt1[:, :], dt1[:, :], ACT.Exp).then_inc(s_spa, 1)
            act.wait_ge(s_sp, 2)
            act.activation(LG[:, 0:NT], dt2[:, :], ACT.Ln).then_inc(s_spa, 1)
            act.wait_ge(s_wm, 16)
            act.activation(negA[:, :], wm("a_log"), ACT.Exp).then_inc(s_spa, 1)
            act.wait_ge(s_sp, 3)
            act.activation(decay[:, :], dt2[:, 0:2 * TILES], ACT.Exp).then_inc(s_decay, 1)

            act.sem_inc(s_rows, 1)
            with act.Fori(0, BATCH) as b:
                def evict_in(g, j):
                    n = block_order.index((g, j))
                    act.wait_ge(s_in, b * 20 + n + 1)
                    src = IN[:, :]
                    if j < 3:
                        act.copy(xin[CB[j]][:, TAPS - 1 + g * GW:TAPS - 1 + (g + 1) * GW], src).then_inc(s_ev, 1)
                    else:
                        if g >= 2:
                            act.wait_ge(s_yf, b * 8 + 2 * (g - 1))
                        act.activation(sigz[g % 2][j - 3], src, ACT.Sigmoid).then_inc(s_ev, 1)

                def conv_sigmoid(g, j):
                    n = 3 * g + j
                    act.wait_ge(s_conv, b * 48 + 4 * n + 4)
                    if n >= 2:
                        act.wait_ge(s_xc, b * 12 + n - 1)
                    act.activation(sg[n % 2], cv[g % 2][CB[j]], ACT.Sigmoid).then_inc(s_sig, 1)

                def evict_x(k):
                    q = k % 2
                    act.wait_ge(s_tp, b * 16 + k + 1)
                    if k >= 2:
                        act.wait_ge(s_S, b * 16 + k - 1)
                    act.copy(XT[q][:, :], XP[:, 0:DI]).then_inc(s_xt, 1)

                def evict_out(g, c):
                    k = g * GT + c
                    act.wait_ge(s_out, b * 16 + k + 1)
                    act.sem_inc(s_apart, 1)
                    act.copy(A[:, bass.ds(b * SEQ + k * D, D)], OP[:, 0:D])
                    act.copy(ssq[:, bass.ds(b * BT + k, 1)], OP[:, D:D + 1]).then_inc(s_oev, 1)

                row_begins(act, b)
                for j in range(3):
                    evict_in(0, j)
                conv_sigmoid(0, 0)
                conv_sigmoid(0, 1)
                evict_in(1, 0)
                conv_sigmoid(0, 2)
                evict_x(0)
                evict_in(1, 1)
                for k in range(BT):
                    g, c = divmod(k, GT)
                    if k + 1 < BT:
                        evict_x(k + 1)
                    for gj in carried(EARLY, g, c):
                        evict_in(*gj)
                    for gj in carried(GATE, g, c):
                        conv_sigmoid(*gj)
                    if g >= 1:
                        evict_out(g - 1, c)
                    for gj in carried(FILL, g, c):
                        evict_in(*gj)
                    if c == GT - 1:
                        if g >= 1:
                            act.wait_ge(s_out, b * 16 + GT * g)
                        for h in range(HEADS):
                            act.wait_ge(s_post, b * 8 + 2 * g + h + 1)
                            act.activation(YSQ[h], Y[h], ACT.Square).then_inc(s_ysq, 1)
                act.wait_ge(s_out, b * 16 + BT)
                act.sem_inc(s_apart, 1)
                act.copy(A[:, bass.ds(b * SEQ + SEQ - GW, GW)], IN[:, :])
                act.copy(ssq[:, bass.ds(b * BT + BT - GT, GT)], OP[:, 0:GT]).then_inc(s_oev, GT)
                act.wait_ge(s_oev, b * 16 + BT)
                act.sem_inc(s_rows, 1)
            sqrt(SD[:, :], ssq[:, :])
            sqrt(SD[:, :], VR[:, :])
            sqrt(SD[:, :], VR[:, :])
            evict_T(1)
            act.wait_ge(s_ex, 1)
            act.activation(tw[:, :], tw[:, :], ACT.Exp).then_inc(s_exd, 1)

            act.wait_ge(s_et, 1)
            act.wait_ge(s_wup, 16 * 8)

            def fetch_up_weights(q, j):
                n, i, _ = tile(q, j)
                if since(n - 1):
                    act.wait_ge(s_up, n - 1)
                    act.sem_inc(s_apart, 1)
                src = eti[0:1, n:n + 1] if isinstance(n, int) else eti[0:1, bass.ds(n, 1)]
                e = act.value_load(src, min_val=0, max_val=E - 1)
                act.activation(WUB[i % 2][:, :], WU[:, bass.ds(e * HID, HID)], ACT.Copy).then_inc(s_wb, 1)

            def gelu(q, j):
                n, i, _ = tile(q, j)
                act.wait_ge(s_up, n + 1)
                if since(n - 1):
                    act.wait_ge(s_dn, n - 1)
                act.activation(HB[i % 2][:, :], PB[2 + i % 2][:, :], ACT.Gelu).then_inc(s_gl, 1)

            def store(q, j):
                n, i, _ = tile(q, j)
                act.wait_ge(s_ye, n + 1)
                act.sem_inc(s_apart, 1)
                dst = slots_y[n * P:(n + 1) * P, :] if isinstance(n, int) else slots_y[bass.ds(n * P, P), :]
                act.dma_start(dst, YT[i][:, :]).then_inc(s_ys[i], 16)

            def act_step(q, i):
                n = q * RING + i
                if not (isinstance(n, int) and n + 2 >= ST_):
                    fetch_up_weights(q, i + 2)
                if not (isinstance(n, int) and n + 1 >= ST_):
                    gelu(q, i + 1)
                if since(n):
                    store(q, i - 1)

            fetch_up_weights(0, 0)
            fetch_up_weights(0, 1)
            gelu(0, 0)
            pipeline(act, act_step)
            store(QS - 1, RING - 1)
            sqrt(SD[:, :], VR[:, :])
            sqrt(SD[:, :], VR[:, :])
            evict_T(2)
            act.wait_ge(s_T, 3 * GROUPS)
            for g in range(GROUPS):
                a, z = g * GW, (g + 1) * GW
                for i in range(2):
                    act.wait_ge(s_gt, 2 * g + i + 1)
                    act.activation(G[i][:, a:z], PB[2 + 2 * (g % 2) + i][:, :], ACT.Sigmoid,
                                   bias=wl("ig_b" if i == 0 else "ag_b")).then_inc(s_gs, 1)
            act.wait_ge(s_gs, 2 * GROUPS)
            for b in range(BATCH):
                a, z = b * SEQ, (b + 1) * SEQ
                act.activation(G[2][:, a:z], G[1][:, a:z], ACT.Exp, scale=lru_c[:, 0:1]).then_inc(s_aa, 1)
                act.activation(G[3][:, a:z], G[1][:, a:z], ACT.Exp, scale=lru_c2[:, 0:1]).then_inc(s_aa, 1)
            for b in range(BATCH):
                a, z = b * SEQ, (b + 1) * SEQ
                act.wait_ge(s_1a, b + 1)
                act.activation(G[3][:, a:z], G[3][:, a:z], ACT.Sqrt).then_inc(s_mu, 1)
            for g in range(GROUPS):
                act.wait_ge(s_ht, g + 1)
                act.copy(A[:, g * GW:(g + 1) * GW], PB[g % 2][:, :]).then_inc(s_he, 1)
            sqrt(SD[:, :], VR[:, :])
            sqrt(SD[:, :], VR[:, :])
            act.wait_ge(s_sct, 1)
            act.copy(sc32[:, :], PB[2][0:TILES, 0:P]).then_inc(s_sce, 1)
            sqrt(SD[:, :], VR[:, :])
            sqrt(c1[1][:, 1:2], c1[0][:, 1:2])
            sqrt(c1[1][:, 1:2], c1[0][:, 5:6])
            act.wait_ge(s_pd, 1)
            act.activation(hT[:, :], PB[0][:, 0:P], ACT.Copy, scale=wl("g1")).then_inc(s_ad, 1)
            act.wait_ge(s_pd, 2)
            act.copy(qT[:, :], PB[1][:, 0:P]).then_inc(s_ad, 1)
            act.wait_ge(s_pd, 3)
            act.copy(kT[:, :], PB[2][:, 0:P]).then_inc(s_ad, 1)
            act.wait_ge(s_pd, 4)
            act.copy(vv[:, :], PB[3][:, 0:P]).then_inc(s_ad, 1)
            act.wait_ge(s_vd, 3)
            act.activation(SM, SM, ACT.Exp, scale=float(HD) ** -0.5).then_inc(s_ad, 1)
            for i in range(4):
                act.wait_ge(s_pd, 8 + i + 1)
                act.copy(PT[:, i * 512:(i + 1) * 512], PB[i][:, :]).then_inc(s_ad, 1)
            act.wait_ge(s_pd, 14)
            act.copy(OT[:, :], PB[5][:, 0:P]).then_inc(s_ad, 1)
            sqrt(c1[1][:, 1:2], c1[0][:, 5:6])
            act.wait_ge(s_pd, 16)
            act.activation(hT[:, :], PB[0][:, 0:P], ACT.Copy, scale=wl("g2")).then_inc(s_ad, 1)
            act.wait_ge(s_pd, 17)
            for i in range(3):
                act.activation(u1[i][0:FC[i], :], PB[3][0:FC[i], i * P:(i + 1) * P], ACT.Silu).then_inc(s_ad, 1)
            sqrt(c1[1][:, 1:2], c1[0][:, 1:2])

        @block.tensor
        def _(pe):
            def transposes(r):
                for g in range(GROUPS):
                    pe.wait_ge(s_xn, r * GROUPS + g + 1)
                    if g >= 2:
                        pe.wait_ge(s_T, r * GROUPS + g - 1)
                    for t in range(GT):
                        i = pe.transpose(PB[g % 2][:, t * P:(t + 1) * P], NX[:, g * GW + t * D:g * GW + (t + 1) * D], ident[:, :])
                    i.then_inc(s_tr, 1)

            pe.wait_ge(s_const, N_CONST)
            transposes(0)
            pe.wait_ge(s_wm, 16)
            pe.wait_ge(s_T, GROUPS)
            for t in range(TILES):
                i = pe.matmul(PB[2][:, 2 * t:2 * t + 2], T[:, t * P:(t + 1) * P], wm("win", 640, 642), start=True, stop=True)
            i.then_inc(s_dtp, 1)
            pe.wait_ge(s_sp, 1)

            pe.sem_inc(s_rows, 1)
            with pe.Fori(0, BATCH) as b:
                def project_in(g, j):
                    n = block_order.index((g, j))
                    if n >= 1:
                        pe.wait_ge(s_ev, b * 20 + n)
                    c = [512, 256, 384, 0, 128][j]
                    pe.matmul(IN[:, :], wm("win", c, c + P), T[:, bass.ds(b * SEQ + g * GW, GW)],
                              start=True, stop=True).then_inc(s_in, 1)

                def front(k):
                    q, (g, c) = k % 2, divmod(k, GT)
                    tok = slice(c * P, (c + 1) * P)
                    pe.wait_ge(s_diag, b * 16 + k + 1)
                    if k >= 2:
                        pe.wait_ge(s_Bw, b * 16 + k - 1)
                    pe.matmul(FR[q][:, 0:256], ones[:, :], diag[q][:, :, :].rearrange("p h t -> p (h t)"),
                              start=True, stop=True).then_inc(s_dec, 1)
                    pe.wait_ge(s_xc, b * 12 + 3 * g + 3)
                    if k >= 1:
                        pe.wait_ge(s_xt, b * 16 + k)
                    for h in range(HEADS):
                        i = pe.transpose(XP[:, h * P:(h + 1) * P], xc[g % 2][h][:, tok], ident[:, :])
                    i.then_inc(s_tp, 1)
                    pe.wait_ge(s_c0, b * 64 + 16 * (g + 1))
                    pe.matmul(FR[q][:, 256 + NS:256 + NS + P], xc[g % 2][2][0:NS, tok], C0[g % 2][:, tok],
                              start=True, stop=True)
                    pe.transpose(FR[q][:, 256:256 + NS], xc[g % 2][2][0:NS, tok], ident[0:NS, 0:NS]).then_inc(s_g, 1)

                def back(k):
                    q, (g, c) = k % 2, divmod(k, GT)
                    tok = slice(c * P, (c + 1) * P)
                    pe.wait_ge(s_M, b * 16 + k + 1)
                    pe.wait_ge(s_xt, b * 16 + k + 1)
                    if g >= 1:
                        pe.wait_ge(s_post, b * 8 + 2 * g)
                    pe.wait_ge(s_CE, b * 16 + k + 1)
                    pe.wait_ge(s_upd, b * 34 + 2 * k + 2)
                    for h in range(HEADS):
                        a, z = h * P, (h + 1) * P
                        pe.matmul(YP[h][:, tok], XT[q][:, a:z], MB[q][:, h, :], start=True, stop=False)
                        pe.matmul(YP[h][:, tok], ST[q][:, a:z], CE[q][:, h, :], start=False, stop=True)
                    pe.wait_ge(s_Bw, b * 16 + k + 1)
                    for h in range(HEADS):
                        a, z = h * P, (h + 1) * P
                        i = pe.matmul(SP[0:NS, a:z], BW[q][:, h, :], XT[q][:, a:z], start=True, stop=True)
                    i.then_inc(s_S, 1)

                def project_out(g, c):
                    k = g * GT + c
                    tok = slice(c * P, (c + 1) * P)
                    pe.wait_ge(s_yf, b * 8 + 2 * g + 2)
                    pe.wait_ge(s_ysq, b * 8 + 2 * g + 2)
                    if k >= 1:
                        pe.wait_ge(s_oev, b * 16 + k)
                    for h in range(HEADS):
                        pe.matmul(OP[:, D:D + 1], YSQ[h][:, tok], ones[:, 0:1], start=(h == 0), stop=(h == 1))
                    for h in range(HEADS):
                        i = pe.matmul(OP[:, 0:D], YF[h][:, tok], wm("wout", h * P, (h + 1) * P),
                                      start=(h == 0), stop=(h == 1))
                    i.then_inc(s_out, 1)

                row_begins(pe, b)
                for j in range(3):
                    project_in(0, j)
                project_in(1, 0)
                front(0)
                project_in(1, 1)
                for k in range(BT):
                    g, c = divmod(k, GT)
                    if k + 1 < BT:
                        front(k + 1)
                    for gj in carried(EARLY, g, c):
                        project_in(*gj)
                    back(k)
                    if g >= 1:
                        project_out(g - 1, c)
                    for gj in carried(FILL, g, c):
                        project_in(*gj)
                pe.wait_ge(s_ev, b * 20 + BLOCKS)
                pe.wait_ge(s_yf, b * 8 + 2 * BG)
                for t in range(GT):
                    for h in range(HEADS):
                        pe.matmul(IN[:, t * D:(t + 1) * D], YF[h][:, t * P:(t + 1) * P], wm("wout", h * P, (h + 1) * P),
                                  start=(h == 0), stop=(h == 1))
                pe.wait_ge(s_ysq, b * 8 + 2 * BG)
                pe.wait_ge(s_oev, b * 16 + BT - GT)
                for t in range(GT):
                    for h in range(HEADS):
                        i = pe.matmul(OP[:, t:t + 1], YSQ[h][:, t * P:(t + 1) * P], ones[:, 0:1], start=(h == 0), stop=(h == 1))
                i.then_inc(s_out, GT)
                pe.wait_ge(s_out, b * 16 + BT)
                pe.sem_inc(s_rows, 1)

            transposes(1)
            pe.wait_ge(s_wl, 16)
            pe.wait_ge(s_T, 2 * GROUPS)
            for t in range(TILES):
                i = pe.matmul(PB[2][:, E * t:E * t + E], T[:, t * P:(t + 1) * P], wl("gate"), start=True, stop=True)
            i.then_inc(s_lg, 1)
            pe.wait_ge(s_mk, 1)
            pe.matmul(PB[2][:, 0:E * TILES], upper[:, :], MK[:, :], start=True, stop=True)
            pe.matmul(PB[3][:, 0:E * TILES], ones[:, :], MK[:, :], start=True, stop=True).then_inc(s_rk, 1)

            def transpose_slots(q, j):
                n, i, turn = tile(q, j)
                pe.wait_ge(s_xl[i], turn * 16 + 16)
                if since(n - 1):
                    pe.wait_ge(s_xe, 2 * n - 2)
                pe.transpose(PB[i % 2][:, 0:P], XG[i][:, :], ident[:, :]).then_inc(s_xp, 1)

            def project_up(q, j):
                n, i, _ = tile(q, j)
                pe.wait_ge(s_xe, 2 * n + 2)
                pe.wait_ge(s_wb, n + 1)
                if since(n - 1):
                    pe.wait_ge(s_gl, n - 1)
                for c in range(HC):
                    b = PB[2 + i % 2][:, c * P:(c + 1) * P]
                    pe.matmul(b, biash[:, c * P:(c + 1) * P], SELB[i][:, :], start=True, stop=False)
                    m = pe.matmul(b, WUB[i % 2][:, c * P:(c + 1) * P], XGT[i % 2][:, :], start=False, stop=True)
                m.then_inc(s_up, 1)

            def project_down(q, j):
                n, i, _ = tile(q, j)
                src = eti[0:1, n:n + 1] if isinstance(n, int) else eti[0:1, bass.ds(n, 1)]
                e = pe.value_load(src, min_val=0, max_val=E - 1)
                pe.wait_ge(s_gl, n + 1)
                if since(n - 1):
                    pe.wait_ge(s_ye, n - 1)
                b = PB[6 + i % 2][:, 0:D]
                pe.matmul(b, SELB[i][:, :], biash[:, HID:HID + D], start=True, stop=False)
                for c in range(HC):
                    m = pe.matmul(b, HB[i % 2][:, c * P:(c + 1) * P], WD[:, bass.ds(e * HID + c * D, D)],
                                  start=False, stop=(c == HC - 1))
                m.then_inc(s_dn, 1)

            def pe_step(q, i):
                n = q * RING + i
                if not (isinstance(n, int) and n + 2 >= ST_):
                    transpose_slots(q, i + 2)
                if not (isinstance(n, int) and n + 1 >= ST_):
                    project_up(q, i + 1)
                project_down(q, i)

            pe.wait_ge(s_et, 1)
            pe.wait_ge(s_bh, 1)
            pe.wait_ge(s_wup, 16 * 8)
            transpose_slots(0, 0)
            transpose_slots(0, 1)
            project_up(0, 0)
            pipeline(pe, pe_step)
            transposes(2)
            for g in range(GROUPS):
                pe.wait_ge(s_T, 2 * GROUPS + g + 1)
                if g >= 2:
                    pe.wait_ge(s_gs, 2 * (g - 1))
                for i, w in enumerate(("ig", "ag")):
                    pe.matmul(PB[2 + 2 * (g % 2) + i][:, :], wl(w), T[:, g * GW:(g + 1) * GW], start=True, stop=True).then_inc(s_gt, 1)
            for g in range(GROUPS):
                pe.wait_ge(s_h, g // BG + 1)
                if g >= 2:
                    pe.wait_ge(s_he, g - 1)
                for t in range(GT):
                    k = g * GT + t
                    c = (k // BT) * PW + (k % BT) * P
                    i = pe.transpose(PB[g % 2][:, t * P:(t + 1) * P], CP[:, c:c + P], ident[:, :])
                i.then_inc(s_ht, 1)
            pe.wait_ge(s_sc, 1)
            pe.transpose(PB[2][0:TILES, 0:P], sc[:, :], ident[:, :]).then_inc(s_sct, 1)
            pe.wait_ge(s_vd, 1)
            pe.transpose(PB[0][:, 0:P], HN[:, :], ident[:, :]).then_inc(s_pd, 1)
            pe.wait_ge(s_ad, 1)
            pe.matmul(PB[1][:, 0:P], wl("wqkv", 0, D), hT[:, :], start=True, stop=True).then_inc(s_pd, 1)
            pe.matmul(PB[2][:, 0:P], wl("wqkv", D, 2 * D), hT[:, :], start=True, stop=True).then_inc(s_pd, 1)
            pe.matmul(PB[3][:, 0:P], hT[:, :], wl("wqkv", 2 * D, 3 * D), start=True, stop=True).then_inc(s_pd, 1)
            pe.wait_ge(s_vd, 2)
            pe.wait_ge(s_ad, 4)
            for i in range(4):
                pe.matmul(PB[i][:, :], qT[:, :], kM[:, i * 512:(i + 1) * 512], start=True, stop=True).then_inc(s_pd, 1)
            pe.wait_ge(s_ad, 5)
            for i in range(4):
                for h in range(4):
                    k = 4 * i + h
                    m = pe.transpose(PB[i][:, h * P:(h + 1) * P], SM[:, k * P:(k + 1) * P], ident[:, :])
                m.then_inc(s_pd, 1)
            for h in range(AH):
                pe.wait_ge(s_ad, 6 + h // 4)
                m = pe.matmul(PB[4][:, h * HD:(h + 1) * HD], PT[:, h * P:(h + 1) * P], vv[:, h * HD:(h + 1) * HD],
                              start=True, stop=True)
            m.then_inc(s_pd, 1)
            pe.wait_ge(s_vd, 4)
            pe.transpose(PB[5][:, 0:P], O[:, :], ident[:, :]).then_inc(s_pd, 1)
            pe.wait_ge(s_ad, 10)
            pe.matmul(PB[5][:, 0:D], OT[:, :], wl("wo"), start=True, stop=True).then_inc(s_pd, 1)
            pe.wait_ge(s_vd, 5)
            pe.transpose(PB[0][:, 0:P], HN[:, :], ident[:, :]).then_inc(s_pd, 1)
            pe.wait_ge(s_ad, 11)
            at = [0, 128, 256]
            for i in range(3):
                pe.matmul(PB[3][0:FC[i], i * P:(i + 1) * P], wl("w1", at[i], at[i] + FC[i]), hT[:, :], start=True, stop=True)
            for i in range(3):
                m = pe.matmul(PB[4][0:FC[i], i * P:(i + 1) * P], wl("w2", at[i], at[i] + FC[i]), hT[:, :], start=True, stop=True)
            m.then_inc(s_pd, 1)
            for i in range(3):
                pe.wait_ge(s_vd, 6 + i)
                m = pe.matmul(PB[5][:, 0:D], gg[i][0:FC[i], :], wl("w3", i * D, (i + 1) * D, rows=FC[i]),
                              start=(i == 0), stop=(i == 2))
            m.then_inc(s_pd, 1)


def kernel(**inputs):
    import numpy as np
    import concourse.bacc as bacc
    from concourse.bass_utils import run_bass_kernel_spmd

    f = {k: np.asarray(a) for k, a in inputs.items()}

    def rows(a, n=P):
        return np.broadcast_to(a.reshape(1, -1), (n, a.size))

    def pad(a):
        z = np.zeros((P, a.shape[1]), np.float32)
        z[:a.shape[0]] = a
        return z

    def block_diagonal(w):
        n = w.shape[1]
        z = np.zeros((P, P), np.float32)
        for h in range(w.shape[0]):
            z[h * n:(h + 1) * n, h * n:(h + 1) * n] = w[h]
        return z

    win = f["L0_attn_in_proj_w"].T
    conv_w = f["L0_attn_conv_w"].reshape(3, P, TAPS).transpose(1, 0, 2).reshape(P, 12)
    mixer = {
        "win": win, "wout": f["L0_attn_out_w"].T.reshape(2, P, D).transpose(1, 0, 2).reshape(P, 2 * D),
        "conv_w": conv_w, "conv_b": f["L0_attn_conv_b"].reshape(3, P).T, "rms_w": f["L0_attn_rms_w"].reshape(2, P).T,
        "dt_bias": rows(f["L0_attn_dt_bias"]), "a_log": rows(f["L0_attn_A_log"]), "d_skip": rows(f["L0_attn_D"]),
        "a_param": f["L1_attn_a_param"].reshape(P, 1),
    }
    w3 = f["L1_ffn_W3"].T
    later = {
        "gate": f["L0_ffn_Wg"], "ig": block_diagonal(f["L1_attn_ig_w"]), "ag": block_diagonal(f["L1_attn_ag_w"]),
        "ig_b": f["L1_attn_ig_b"].reshape(P, 1), "ag_b": f["L1_attn_ag_b"].reshape(P, 1),
        "router": rows(f["L1_ffn_w_router"]), "wqkv": f["L1_ffn_W_qkv"].T, "wo": f["L1_ffn_W_out"].T,
        "g1": f["L1_ffn_g1"].reshape(P, 1), "g2": f["L1_ffn_g2"].reshape(P, 1),
        "w1": f["L1_ffn_W1"].T, "w2": f["L1_ffn_W2"].T,
        "w3": np.concatenate([pad(w3[128 * i:128 * i + n]) for i, n in enumerate(FC)], axis=1),
    }
    arrays = {
        "u": f["L0_attn_u"].reshape(TOKENS, D),
        "mixer_w": np.concatenate([mixer[n] for n, _ in MIXER_COLS], axis=1),
        "later_w": np.concatenate([later[n] for n, _ in LATER_COLS], axis=1),
        "wup": f["L0_ffn_Wup"],
        "wdown": f["L0_ffn_Wdown"].reshape(E, HC, P, D).transpose(0, 2, 1, 3).reshape(E, P, HC * D),
        "bup": f["L0_ffn_bup"],
        "bdown": f["L0_ffn_bdown"],
    }
    arrays = {k: np.ascontiguousarray(a) for k, a in arrays.items()}
    nc = bacc.Bacc("TRN2", target_bir_lowering=False, num_devices=1)
    args = [nc.dram_tensor(k, a.shape, F32, kind="ExternalInput").ap() for k, a in arrays.items()]
    out = nc.dram_tensor("out", (TOKENS, D), F32, kind="ExternalOutput").ap()
    build(nc, *args, out)
    r = run_bass_kernel_spmd(nc, [arrays], core_ids=[0])
    return r.results[0]["out"].reshape(BATCH, SEQ, D)
```

```python
from contextlib import ExitStack

import concourse.bass as bass
from concourse import mybir

F32 = mybir.dt.float32
F32R = mybir.dt.float32r
U32 = mybir.dt.uint32
I32 = mybir.dt.int32
ALU = mybir.AluOpType
ACT = mybir.ActivationFunctionType
AX = mybir.AxisListType

P = 128
BATCH, SEQ, D = 2, 2048, 128
TOKENS = BATCH * SEQ
TILES = TOKENS // P
BT = SEQ // P
GT = 4
GW = GT * P
GROUPS = TILES // GT
BG = BT // GT
AHEAD = 2
PAIR = 2
OWN = 3
HEADS, NS, DI = 2, 64, 256
TAPS = 4
RING = 4
E, HID, TOPK = 12, 512, 3
HC = HID // P
HT_ = (TOPK * SEQ + E * (P - 1)) // P
HT_ += -HT_ % RING
ST_ = 2 * HT_
CAP, AH, HD = 64, 16, 8
DFF = 341
FC = [128, 128, 85]
LN_EPS, RMS_EPS, FF_EPS = 1e-5, 1e-5, 1e-6

MIXER_COLS = [("win", 642), ("wout", 256), ("conv_w", 12), ("conv_b", 3), ("rms_w", 2),
              ("dt_bias", 2), ("a_log", 2), ("d_skip", 2), ("a_param", 1)]
LATER_COLS = [("row_expert", 1), ("row_chunk", HC), ("gate", E), ("ig", P), ("ag", P), ("ig_b", 1), ("ag_b", 1),
              ("router", D), ("wqkv", 3 * D), ("wo", D), ("g1", 1), ("g2", 1), ("w1", DFF), ("w2", DFF),
              ("w3", 3 * D)]


def columns(cols):
    at, out = 0, {}
    for name, n in cols:
        out[name] = (at, at + n)
        at += n
    return out, at


MIXER_AT, MIXER_N = columns(MIXER_COLS)
LATER_AT, LATER_N = columns(LATER_COLS)


def build(nc, u, mixer_w, later_w, wup, wdown, biases, out):
    with ExitStack() as ctx:
        def sb(name, shape, dt=F32):
            return ctx.enter_context(nc.sbuf_tensor(name, shape, dt))

        def sem(name):
            return ctx.enter_context(nc.semaphore(name))

        X = sb("X", [P, TILES * D])
        A = sb("A", [P, TILES * D])
        T = sb("T", [P, TOKENS])
        F = sb("F", [P, 6 * TOKENS])
        NX = A
        WM = sb("WM", [P, MIXER_N])
        WL = sb("WL", [P, LATER_N])
        ident = sb("ident", [P, P])
        ones = sb("ones", [P, P])
        zeros = sb("zeros", [P, 1])
        floor = sb("floor", [P, 1])
        st6 = sb("st6", [P, TILES * 6])
        MN = sb("MN", [P, TILES])
        DF = sb("DF", [P, TILES])
        VR = sb("VR", [P, TILES])
        SD = sb("SD", [P, TILES])
        RS = sb("RS", [P, TILES])
        NB = sb("NB", [P, TILES])
        DS = sb("DS", [P, TILES])
        DB = sb("DB", [P, TILES])
        NT = 2 * TILES + 1
        dt0 = sb("dt0", [P, NT])
        dt1 = sb("dt1", [P, NT])
        dt2 = sb("dt2", [P, NT])
        dt3 = sb("dt3", [P, NT])
        decay = sb("decay", [P, 2 * TILES])
        negA = sb("negA", [P, 2])
        lru_c = sb("lru_c", [P, 1])
        lru_c2 = sb("lru_c2", [P, 1])
        ssq = sb("ssq", [P, TILES])

        def wm(name, lo=0, hi=None, rows=P):
            a, b = MIXER_AT[name]
            return WM[0:rows, a + lo:(a + hi if hi is not None else b)]

        def wl(name, lo=0, hi=None, rows=P):
            a, b = LATER_AT[name]
            return WL[0:rows, a + lo:(a + hi if hi is not None else b)]

        at = [0]

        def carve(n):
            at[0] += n
            assert at[0] <= 6 * TOKENS
            return F[:, at[0] - n:at[0]]

        XW = SEQ + TAPS - 1
        xin = [carve(XW) for _ in range(3)]
        cv = [[carve(GW) for _ in range(3)] for _ in range(2)]
        sg = [carve(GW) for _ in range(2)]
        xc = [[carve(GW) for _ in range(3)] for _ in range(2)]
        sigz = [[carve(GW) for _ in range(2)] for _ in range(2)]
        Y = [carve(GW) for _ in range(2)]
        YSQ = [carve(GW) for _ in range(2)]
        YF = [carve(GW) for _ in range(2)]

        def carve3(a, b, rows=P):
            return carve(a * b)[0:rows, :].rearrange("p (a b) -> p a b", a=a)

        C0 = [carve(GW)[0:NS, :] for _ in range(2)]
        diag = [carve3(HEADS, P) for _ in range(2)]
        LB = [carve3(HEADS, P) for _ in range(2)]
        EB = [carve3(HEADS, P, NS) for _ in range(2)]
        MB = [carve3(HEADS, P) for _ in range(2)]
        BW = [carve3(HEADS, NS) for _ in range(2)]
        CE = [carve3(HEADS, P, NS) for _ in range(2)]
        XT = [carve(DI) for _ in range(2)]
        ST = [carve(DI)[0:NS, :] for _ in range(2)]

        WU = F[:, 0:E * HID]
        WD = F[:, E * HID:2 * E * HID]
        RG = F[:, 2 * E * HID:2 * E * HID + TOPK * TOKENS]
        LG = sb("LG", [P, TILES * E])
        route_at = [6 * TOKENS]

        def route(n):
            route_at[0] -= n
            return F[:, route_at[0]:route_at[0] + n]

        top8 = sb("top8", [P, TILES * 8])
        sel8 = sb("sel8", [P, TILES * 8], U32)
        self_ = sb("sel_f", [P, TILES * 8])
        tw = sb("tw", [P, TILES * TOPK])
        tsum = sb("tsum", [P, TILES])
        iotaE = sb("iotaE", [P, E])
        oh = [route(E * TILES) for _ in range(TOPK)]
        MK = route(E * TILES)
        PI = route(E * TILES)
        PO = route(E * TILES)
        OP_ = route(E * TILES)
        segE = sb("segE", [P, E * BT])
        TCf = sb("TCf", [P, 2 * E])
        TCi = sb("TCi", [P, 2 * E], I32)
        BT0 = sb("BT0", [P, 2 * E])
        BS = sb("BS", [P, 2 * E])
        posf = sb("posf", [P, TOPK * TILES])
        posu = sb("posu", [P, TOPK * TILES], U32)
        iotaJ = sb("iotaJ", [P, HT_])
        GE = route(HT_ * E)
        etf = sb("etf", [P, ST_])
        eti = sb("eti", [P, ST_], I32)
        SEL = sb("SEL", [P, ST_])
        cmask = sb("cmask", [P, HC, P])
        upper = sb("upper", [P, P])
        BR = HC * E
        LOW = 64
        biasr = sb("biasr", [P, 2 * P])
        biash = sb("biash", [P, 2 * P], F32R)
        biast = sb("biast", [P, 2 * P])
        SELB = [sb(f"SELB{i}", [P, HC * P], F32R) for i in range(RING)]
        zt = sb("zt", [P, 512])
        XG = [sb(f"XG{i}", [P, D]) for i in range(RING)]
        XGT = [sb(f"XGT{i}", [P, P]) for i in range(2)]
        WUB = [sb(f"WUB{i}", [P, HID]) for i in range(2)]
        HB = [sb(f"HB{i}", [P, HID]) for i in range(2)]
        YT = [sb(f"YT{i}", [P, D]) for i in range(RING)]
        slots_x = nc.dram_tensor("slots_x", [ST_ * P, D], F32, kind="Internal").ap()
        slots_y = nc.dram_tensor("slots_y", [ST_ * P, D], F32, kind="Internal").ap()

        PW = SEQ + 1
        LRU = 4 * SEQ + PW
        G = [[F[:, b * LRU + i * SEQ:b * LRU + (i + 1) * SEQ] for i in range(4)] for b in range(BATCH)]
        CP = [F[:, b * LRU + 4 * SEQ:(b + 1) * LRU] for b in range(BATCH)]

        sc = sb("sc", [P, TILES])
        sc32 = sb("sc32", [TILES, P])
        PARTS = 4
        PL = SEQ // PARTS
        NP_ = BATCH * PARTS
        row = F[0:NP_, 5 * TOKENS + BATCH:5 * TOKENS + BATCH + PL]
        spare = F[0:NP_, 5 * TOKENS + BATCH + PL:5 * TOKENS + BATCH + 2 * PL]
        v8 = sb("v8", [NP_, CAP])
        i8 = sb("i8", [NP_, CAP], U32)
        i8g = sb("i8g", [NP_, CAP], U32)
        rowoff = sb("rowoff", [NP_, 1])
        row2 = sb("row2", [BATCH, PARTS * CAP])
        spare2 = F[0:BATCH, 0:PARTS * CAP]
        v2 = sb("v2", [BATCH, CAP])
        i2 = sb("i2", [BATCH, CAP], U32)
        i2g = sb("i2g", [BATCH, CAP], U32)
        rowoff2 = sb("rowoff2", [BATCH, 1])
        pick = sb("pick", [P, 1], U32)
        winners = nc.dram_tensor("winners", [NP_ * CAP, 1], U32, kind="Internal").ap()
        idx = sb("idx", [P, 1], U32)
        hmask = sb("hmask", [P, AH])
        amask = sb("amask", [P, P])
        tail_at = [6 * TOKENS]

        def tail(n):
            tail_at[0] -= n
            return F[:, tail_at[0]:tail_at[0] + n]

        XS = tail(P)
        XN = tail(P)
        SQ = tail(P)
        HN = tail(P)
        hT = tail(P)
        qT = tail(P)
        kT = tail(P)
        vv = tail(P)
        kM = F[:, 0:AH * P]
        SM = F[:, AH * P:2 * AH * P]
        PT = F[:, 2 * AH * P:3 * AH * P]
        mx = sb("mx", [P, AH])
        sm = sb("sm", [P, AH])
        O = tail(P)
        OT = tail(P)
        XA = tail(P)
        u1 = [tail(P) for i in range(3)]
        gg = [tail(P) for i in range(3)]
        PR = tail(P)
        c1 = [sb(f"c1_{i}", [P, 8]) for i in range(2)]

        PB = [ctx.enter_context(nc.psum_tensor(f"PB{i}", [P, 512], F32)) for i in range(8)]

        IN, XP, SP, OP = PB[0], PB[1], PB[4], PB[7]
        FR = [PB[2], PB[3]]
        YP = [PB[5], PB[6]]

        x3_dram = nc.dram_tensor("x3_scratch", [TOKENS, D], F32, kind="Internal").ap()

        s_apart = sem("s_apart")
        s_u = [sem(f"s_u{b}") for b in range(BATCH)]
        s_wm = sem("s_wm")
        s_wl = sem("s_wl")
        s_const = sem("s_const")
        s_cstep = sem("s_cstep")
        s_stat = sem("s_stat")
        s_dve = sem("s_dve")
        s_var = sem("s_var")
        s_sd = sem("s_sd")
        s_cf = sem("s_cf")
        s_xn = [[sem(f"s_xn{r}{b}") for b in range(BATCH)] for r in range(3)]
        s_tr = [[sem(f"s_tr{r}{b}") for b in range(BATCH)] for r in range(3)]
        s_T = [[sem(f"s_T{r}{b}") for b in range(BATCH)] for r in range(3)]
        s_dtp = sem("s_dtp")
        s_sp = sem("s_sp")
        s_spa = sem("s_spa")
        s_decay = sem("s_decay")
        s_zero = sem("s_zero")
        s_in = sem("s_in")
        s_ev = sem("s_ev")
        s_conv = sem("s_conv")
        s_sig = sem("s_sig")
        s_xc = sem("s_xc")
        s_c0 = sem("s_c0")
        s_diag = sem("s_diag")
        s_dec = sem("s_dec")
        s_tp = sem("s_tp")
        s_g = sem("s_g")
        s_xt = sem("s_xt")
        s_L = sem("s_L")
        s_E = sem("s_E")
        s_M = sem("s_M")
        s_Bw = sem("s_Bw")
        s_CE = sem("s_CE")
        s_S = sem("s_S")
        s_upd = sem("s_upd")
        s_post = sem("s_post")
        s_ysq = sem("s_ysq")
        s_yf = sem("s_yf")
        s_out = sem("s_out")
        s_oev = sem("s_oev")
        s_res = [[sem(f"s_res{e}{b}") for b in range(BATCH)] for e in range(3)]
        s_xv = {e: [sem(f"s_xv{e}{b}") for b in range(BATCH)] for e in (1, 2)}
        s_X = [[sem(f"s_X{e}{b}") for b in range(BATCH)] for e in range(3)]
        s_lg = sem("s_lg")
        s_top = sem("s_top")
        s_ex = sem("s_ex")
        s_exd = sem("s_exd")
        s_wup = sem("s_wup")
        s_bias = sem("s_bias")
        s_bh = sem("s_bh")
        s_mk = sem("s_mk")
        s_rk = sem("s_rk")
        s_pos = sem("s_pos")
        s_et = sem("s_et")
        s_zf = sem("s_zf")
        s_sx = [sem(f"s_sx{h}") for h in range(2)]
        s_xl = [sem(f"s_xl{i}") for i in range(RING)]
        s_ys = [sem(f"s_ys{i}") for i in range(RING)]
        s_xp = sem("s_xp")
        s_xe = sem("s_xe")
        s_up = sem("s_up")
        s_gl = sem("s_gl")
        s_wb = sem("s_wb")
        s_dn = sem("s_dn")
        s_ye = sem("s_ye")
        s_rg0 = sem("s_rg0")
        s_rg1 = [sem(f"s_rg1_{i}") for i in range(BT // PAIR)]
        s_cmb0 = sem("s_cmb0")
        s_cmb = sem("s_cmb")
        s_gt = sem("s_gt")
        s_gs = sem("s_gs")
        s_aa = sem("s_aa")
        s_1a = sem("s_1a")
        s_mu = sem("s_mu")
        s_xg = sem("s_xg")
        s_h = sem("s_h")
        s_ht = sem("s_ht")
        s_he = sem("s_he")
        s_sc = sem("s_sc")
        s_sct = sem("s_sct")
        s_sce = sem("s_sce")
        s_row = sem("s_row")
        s_tk = sem("s_tk")
        s_tk2 = sem("s_tk2")
        s_row2 = sem("s_row2")
        s_win = sem("s_win")
        s_pk = sem("s_pk")
        s_idx = sem("s_idx")
        s_fin = sem("s_fin")
        s_st = sem("s_st")
        s_x3 = sem("s_x3")
        s_gat = sem("s_gat")
        s_sca = sem("s_sca")
        s_pd = sem("s_pd")
        s_vd = sem("s_vd")
        s_ad = sem("s_ad")



        QS = ST_ // RING

        def tile(q, j):
            return q * RING + j, j % RING, q + j // RING

        def since(n, least=1):
            return n >= least if isinstance(n, int) else True

        BESIDE = 6

        def pipeline(eng, step, beside):
            for i in range(RING):
                step(0, i)
            with eng.Fori(1, QS - BESIDE) as q:
                for i in range(RING):
                    step(q, i)
            for q in range(QS - BESIDE, QS):
                for i in range(RING):
                    step(q, i)
                    beside((q - QS + BESIDE) * RING + i)

        tw3 = tw[:, :].rearrange("p (t k) -> p t k", k=TOPK)

        block = ctx.enter_context(nc.Block())

        def cols(t, start, n):
            return t[:, bass.ds(start, n)]

        CB = [2, 0, 1]
        EARLY = [[], [], [], [(0, 4)]]
        FILL = [[(1, 2)], [(0, 3)], [(2, 0)], [(2, 1)]]
        CONV = [[(1, 1)], [(1, 2)], [], [(2, 0)]]
        GATE = [[(1, 0)], [(1, 1)], [(1, 2)], []]
        LATE = {29: [("T", 0), ("T", 1)], 30: [("T", 2), ("T", 3)], 31: [("logits", 0)]}
        BLOCKS = GROUPS * 5 + BG + 1
        block_order = [(0, 0), (0, 1), (0, 2), (1, 0), (1, 1)]
        for g_ in range(GROUPS):
            for c_ in range(GT):
                block_order += [(g_ + a_, j_) for a_, j_ in EARLY[c_] + FILL[c_] if g_ + a_ < GROUPS]
                block_order += LATE.get(g_ * GT + c_, [])
        assert len(block_order) == BLOCKS

        def carried(table, g, c):
            return [(g + ahead, j) for ahead, j in table[c] if g + ahead < GROUPS]

        N_CONST = 14

        @block.sync
        def _(sp):
            uv = u.rearrange("(g t p) d -> g p t d", t=GT, p=P)
            for g in range(GROUPS):
                sp.dma_start(X[:, g * GW:(g + 1) * GW].rearrange("p (t d) -> p t d", t=GT), uv[g]).then_inc(s_u[g // BG], 16)
                if g == 3:
                    sp.dma_start(WM[:, :], mixer_w).then_inc(s_wm, 16)
            sp.dma_start(WL[:, :], later_w).then_inc(s_wl, 16)

            sp.wait_ge(s_const, N_CONST)
            for h in range(2):
                sp.dma_start(slots_x[h * HT_ * P:(h + 1) * HT_ * P, :].rearrange("(p n) d -> p (n d)", p=P)
                             .rearrange("p (a b) -> p a b", b=512),
                             zt[:, :].unsqueeze(1).broadcast_to([P, HT_ * D // 512, 512])).then_inc(s_zf, 16)
            for r in (0, LOW):
                sp.dma_start(biasr[r:r + BR, :], biases).then_inc(s_bias, 16)

            for g in range(GROUPS):
                sp.wait_ge(s_xc, 3 * g + 1)
                if g >= 2:
                    sp.wait_ge(s_CE, GT * (g - 1))
                    sp.wait_ge(s_g, GT * (g - 1))
                if g >= 1:
                    sp.wait_ge(s_c0, 16 * g)
                sp.dma_start(C0[g % 2][:, :], xc[g % 2][2][NS:2 * NS, :]).then_inc(s_c0, 16)
            sp.wait_ge(s_c0, 16 * GROUPS)
            sp.wait_ge(s_post, 2 * GROUPS)
            for e in range(0, E, 3):
                sp.dma_start(WU[:, e * HID:(e + 3) * HID].rearrange("p (e n) -> p e n", e=3),
                             wup[e:e + 3].rearrange("e p n -> p e n")).then_inc(s_wup, 16)
                sp.dma_start(WD[:, e * HID:(e + 3) * HID].rearrange("p (e n) -> p e n", e=3),
                             wdown[e:e + 3].rearrange("e p n -> p e n")).then_inc(s_wup, 16)

            def load_slots(q, j):
                n, i, _ = tile(q, j)
                if since(n, RING):
                    sp.wait_ge(s_xp, n - RING + 1)
                    sp.sem_inc(s_apart, 1)
                src = slots_x[n * P:(n + 1) * P, :] if isinstance(n, int) else slots_x[bass.ds(n * P, P), :]
                sp.dma_start(XG[i][:, :], src).then_inc(s_xl[i], 16)

            sp.wait_ge(s_sx[0], 16 * TOPK * BT)
            for i in range(RING):
                load_slots(0, i)
            with sp.Fori(1, QS // 2) as q:
                for i in range(RING):
                    load_slots(q, i)
            sp.wait_ge(s_sx[1], 16 * TOPK * BT)
            with sp.Fori(QS // 2, QS) as q:
                for i in range(RING):
                    load_slots(q, i)
            ov = out.rearrange("(g t p) d -> g p t d", t=GT, p=P)
            x3v = x3_dram.rearrange("(b t p) d -> b p t d", t=BT, p=P)
            for b in range(BATCH):
                sp.wait_ge(s_xv[2][b], OWN)
                sp.wait_ge(s_X[2][b], BG - OWN)
                sp.dma_start(x3v[b], X[:, b * SEQ:(b + 1) * SEQ].rearrange("p (t d) -> p t d", t=BT)).then_inc(s_x3, 16)
                if b == BATCH - 1:
                    sp.wait_ge(s_sce, 1)
                    sp.dma_start(row.rearrange("b (t p) -> b t p", p=P), sc32[:, :]).then_inc(s_row, 16)
                for g in range(b * BG, (b + 1) * BG):
                    sp.wait_ge(s_fin, g + 1)
                    sp.dma_start(ov[g], A[:, g * GW:(g + 1) * GW].rearrange("p (t d) -> p t d", t=GT)).then_inc(s_st, 16)
            sp.wait_ge(s_tk, 3 * CAP // 8 - 1)
            sp.dma_start(row2[:, :], v8[:, :]).then_inc(s_row2, 16)
            sp.wait_ge(s_tk, 3 * CAP // 8)
            sp.dma_start(winners.rearrange("(q c) o -> q (c o)", c=CAP), i8g[:, :]).then_inc(s_win, 16)
            sp.wait_ge(s_tk2, 3 * CAP // 8)
            sp.dma_start(pick[:, :], i2g[:, :]).then_inc(s_pk, 16)
            sp.wait_ge(s_st, 16 * GROUPS)
            sp.wait_ge(s_sca, 16)

        @block.gpsimd
        def _(pool):
            pool.memset(ident[:, :], 0.0).then_inc(s_cstep, 1)
            pool.memset(ones[:, :], 1.0).then_inc(s_const, 1)
            pool.memset(zeros[:, :], 0.0).then_inc(s_const, 1)
            pool.memset(floor[:, :], 1e-7).then_inc(s_const, 1)
            pool.memset(hmask[:, :], 1.0).then_inc(s_cstep, 1)
            pool.memset(amask[:, :], 0.0).then_inc(s_cstep, 1)
            pool.memset(upper[:, :], 1.0).then_inc(s_cstep, 1)
            pool.memset(segE[:, :], 1.0).then_inc(s_cstep, 1)
            pool.memset(zt[:, :], 0.0).then_inc(s_const, 1)
            pool.memset(biasr[:, :], 0.0).then_inc(s_const, 1)
            pool.wait_ge(s_cstep, 5)
            pool.affine_select(out=ident[:, :], in_=ident[:, :], compare_op=ALU.not_equal, fill=1.0, base=0,
                               pattern=[[-1, P]], channel_multiplier=1).then_inc(s_const, 1)
            pool.affine_select(out=hmask[:, :], in_=hmask[:, :], compare_op=ALU.is_ge, fill=0.0, base=0,
                               pattern=[[-HD, AH]], channel_multiplier=1).then_inc(s_cstep, 1)
            pool.affine_select(out=amask[:, :], in_=amask[:, :], compare_op=ALU.is_ge, fill=-1e30, base=0,
                               pattern=[[-1, P]], channel_multiplier=1).then_inc(s_cstep, 1)
            pool.affine_select(out=upper[:, :], in_=upper[:, :], compare_op=ALU.is_gt, fill=0.0, base=0,
                               pattern=[[1, P]], channel_multiplier=-1).then_inc(s_const, 1)
            pool.memset(segE[:, :].rearrange("p (s t) -> p s t", t=BT)[:, :, 0:1], 0.0).then_inc(s_const, 1)
            pool.iota(iotaJ[:, :], pattern=[[1, HT_]], base=0, channel_multiplier=0,
                      allow_small_or_imprecise_dtypes=True).then_inc(s_const, 1)
            pool.wait_ge(s_cstep, 7)
            pool.affine_select(out=hmask[:, :], in_=hmask[:, :], compare_op=ALU.is_ge, fill=0.0, base=HD - 1,
                               pattern=[[HD, AH]], channel_multiplier=-1).then_inc(s_const, 1)
            pool.wait_ge(s_const, 10)
            pool.memset(amask[CAP:P, 0:CAP], -1e30).then_inc(s_const, 1)
            pool.wait_ge(s_const, 11)
            pool.iota(iotaE[:, :], pattern=[[1, E]], base=0, channel_multiplier=0,
                      allow_small_or_imprecise_dtypes=True).then_inc(s_const, 1)
            pool.iota(rowoff[:, :], pattern=[[1, 1]], base=0, channel_multiplier=PL,
                      allow_small_or_imprecise_dtypes=True).then_inc(s_const, 1)
            pool.iota(rowoff2[:, :], pattern=[[1, 1]], base=0, channel_multiplier=PARTS * CAP,
                      allow_small_or_imprecise_dtypes=True).then_inc(s_const, 1)
            pool.wait_ge(s_const, N_CONST)
            for j in range(3):
                pool.memset(xin[j][:, 0:TAPS - 1], 0.0).then_inc(s_zero, 1)
            pool.wait_ge(s_const, N_CONST)
            pool.wait_ge(s_decay, 1)

            def make_diag(k):
                if k >= 2:
                    pool.wait_ge(s_dec, k - 1)
                dk = decay[:, bass.ds(2 * k, 2)]
                pool.tensor_tensor(diag[k % 2][:, :, :], ident[:, :].unsqueeze(1).broadcast_to([P, HEADS, P]),
                                   dk.unsqueeze(2).broadcast_to([P, HEADS, P]), ALU.mult).then_inc(s_diag, 1)

            def silu(g, j):
                n = 3 * g + j
                pool.wait_ge(s_sig, n + 1)
                if g >= 2 and j == 0:
                    pool.wait_ge(s_g, GT * (g - 1))
                    pool.wait_ge(s_c0, 16 * (g - 1))
                elif g >= 2:
                    pool.wait_ge(s_post, 2 * (g - 1))
                pool.tensor_tensor(xc[g % 2][CB[j]], cv[g % 2][CB[j]], sg[n % 2], ALU.mult).then_inc(s_xc, 1)

            def decayed_c(k):
                g = k // GT
                pool.wait_ge(s_c0, 16 * (g + 1))
                pool.wait_ge(s_E, 2 * (k + 1))
                if k >= 2:
                    pool.wait_ge(s_S, k - 1)
                c = C0[g % 2][:, (k % GT) * P:(k % GT + 1) * P]
                pool.tensor_tensor(CE[k % 2][:, :, :], c.unsqueeze(1).broadcast_to([NS, HEADS, P]),
                                   EB[k % 2][:, :, :], ALU.mult).then_inc(s_CE, 1)
            def gated(g):
                pool.wait_ge(s_ev, block_order.index((g, 4)) + 1)
                if g >= 1:
                    pool.wait_ge(s_out, GT * g)
                for h in range(HEADS):
                    pool.wait_ge(s_post, 2 * g + h + 1)
                    pool.tensor_tensor(YF[h], Y[h], sigz[g % 2][h], ALU.mult).then_inc(s_yf, 1)

            make_diag(0)
            make_diag(1)
            for j in range(3):
                silu(0, j)
            decayed_c(0)
            for k in range(TILES):
                g, c = divmod(k, GT)
                if k + 2 < TILES:
                    make_diag(k + 2)
                if k + 1 < TILES:
                    decayed_c(k + 1)
                for gj in carried(GATE, g, c):
                    silu(*gj)
                if c == GT - 1:
                    gated(g)
                if k in (24, 25):
                    for r in (2 * (k - 24), 2 * (k - 24) + 1):
                        pool.wait_ge(s_res[0][0], r + 1)
                        x = slice(r * GW, (r + 1) * GW)
                        pool.tensor_tensor(X[:, x], X[:, x], A[:, x], ALU.add).then_inc(s_X[0][0], 1)
            pool.wait_ge(s_CE, TILES)
            pool.wait_ge(s_zf, 32)
            for h in range(2):
                pool.wait_ge(s_xn[1][h], BG)
                pool.wait_ge(s_pos, h + 1)
                for t in range(h * BT, (h + 1) * BT):
                    for k in range(TOPK):
                        c = k * TILES + t
                        pool.indirect_dma_start(slots_x, bass.IndirectOffsetOnAxis(posu[:, c:c + 1], 0),
                                                NX[:, t * D:(t + 1) * D], None).then_inc(s_sx[h], 16)
            for h in range(2):
                for i in range(RING):
                    pool.wait_ge(s_ys[i], 16 * (h + 1) * HT_ // RING)
                for t in range(h * BT, (h + 1) * BT):
                    done = s_rg0 if h == 0 else s_rg1[(t - BT) // PAIR]
                    for k in range(TOPK):
                        c = k * TILES + t
                        pool.indirect_dma_start(RG[:, (t * TOPK + k) * D:(t * TOPK + k + 1) * D], None,
                                                slots_y[0:(h + 1) * HT_ * P, :],
                                                bass.IndirectOffsetOnAxis(posu[:, c:c + 1], 0)).then_inc(done, 16)
                if h == 0:
                    pool.wait_ge(s_rg0, 16 * TOPK * BT)
                    r = RG[:, 0:BT * TOPK * D].rearrange("p (t k d) -> p t k d", k=TOPK, d=D)
                    a = A[:, 0:SEQ].rearrange("p (t d) -> p t d", d=D)
                    w = tw[:, 0:BT * TOPK]
                    r1 = RG[:, 0:BT * TOPK * D].rearrange("p (c d) -> p c d", d=D)
                    pool.tensor_tensor(r1, r1, w.unsqueeze(2).broadcast_to([P, BT * TOPK, D]), ALU.mult).then_inc(s_cmb0, 1)
                    pool.wait_ge(s_cmb0, 1)
                    pool.tensor_tensor(a, r[:, :, 0, :], r[:, :, 1, :], ALU.add).then_inc(s_cmb0, 1)
                    pool.wait_ge(s_cmb0, 2)
                    pool.tensor_tensor(a, a, r[:, :, 2, :], ALU.add).then_inc(s_cmb0, 1)
            def add_to_x(e, b):
                for g in range(OWN, BG):
                    pool.wait_ge(s_res[e][b], g - OWN + 1)
                    x = slice((b * BG + g) * GW, (b * BG + g + 1) * GW)
                    pool.tensor_tensor(X[:, x], X[:, x], A[:, x], ALU.add).then_inc(s_X[e][b], 1)

            add_to_x(1, 1)
            add_to_x(2, 0)
            pool.wait_ge(s_gs, 4 * BG)
            pool.tensor_tensor(G[1][0], T[:, SEQ:2 * SEQ], G[1][0], ALU.mult).then_inc(s_xg, 1)
            pool.wait_ge(s_xg, 1)
            pool.wait_ge(s_mu, 2)
            pool.tensor_tensor(G[1][0], G[1][0], G[1][3], ALU.mult).then_inc(s_xg, 1)
            add_to_x(2, 1)
            pool.wait_ge(s_pk, 16)
            pool.wait_ge(s_win, 16)
            pool.indirect_dma_start(idx[:, :], None, winners, bass.IndirectOffsetOnAxis(pick[:, :], 0)).then_inc(s_idx, 16)
            pool.wait_ge(s_idx, 16)
            pool.wait_ge(s_x3, 32)
            pool.indirect_dma_start(XS[:, :], None, x3_dram, bass.IndirectOffsetOnAxis(idx[:, :], 0)).then_inc(s_gat, 16)
            pool.wait_ge(s_vd, 9)
            pool.wait_ge(s_st, 16 * GROUPS)
            pool.indirect_dma_start(out, bass.IndirectOffsetOnAxis(idx[:, :], 0), PR[:, :], None).then_inc(s_sca, 16)

        @block.vector
        def _(v):
            link = [0]
            nstat = [0]
            nvar = [0]
            noff = [0]

            def step(ins):
                ins.then_inc(s_dve, 1)
                link[0] += 1

            def settle():
                v.wait_ge(s_dve, link[0])

            def root(src, dst):
                nvar[0] += 1
                v.wait_ge(s_sd, nvar[0])
                step(v.reciprocal(dst, src))
                settle()

            def tile_stats(src, t):
                v.bn_stats(st6[:, t * 6:t * 6 + 6], src[:, t * D:(t + 1) * D]).then_inc(s_stat, 1)
                nstat[0] += 1

            def moments(b, eps):
                v.wait_ge(s_stat, nstat[0])
                h = slice(b * BT, (b + 1) * BT)
                s6 = st6[:, b * BT * 6:(b + 1) * BT * 6].rearrange("p (t s) -> p t s", s=6)
                step(v.tensor_tensor(DF[:, h], s6[:, :, 1], s6[:, :, 4], ALU.subtract))
                step(v.tensor_tensor(VR[:, h], s6[:, :, 2], s6[:, :, 5], ALU.add))
                step(v.tensor_tensor(MN[:, h], s6[:, :, 1], s6[:, :, 4], ALU.add))
                settle()
                step(v.scalar_tensor_tensor(DF[:, h], DF[:, h], 0.25, DF[:, h], ALU.mult, ALU.mult))
                step(v.tensor_scalar(VR[:, h], VR[:, h], 1.0 / D, eps, ALU.mult, ALU.add))
                step(v.tensor_scalar(MN[:, h], MN[:, h], 0.5, None, ALU.mult))
                settle()

            def offsets(h):
                v.scalar_tensor_tensor(NB[:, h], MN[:, h], -1.0, RS[:, h], ALU.mult, ALU.mult).then_inc(s_cf, 1)
                noff[0] += 1

            def group_stats(src, b, g, ready=None):
                if ready is not None:
                    v.wait_ge(ready, g + 1)
                for t in range(b * BT + g * GT, b * BT + (g + 1) * GT):
                    tile_stats(src, t)

            def ask_for_root(b):
                h = slice(b * BT, (b + 1) * BT)
                moments(b, LN_EPS)
                v.tensor_tensor(VR[:, h], VR[:, h], DF[:, h], ALU.add).then_inc(s_var, 1)

            def finish_norm(b):
                h = slice(b * BT, (b + 1) * BT)
                root(SD[:, h], RS[:, h])
                offsets(h)

            def layer_norm(src, b, ready=None):
                for g in range(BG):
                    group_stats(src, b, g, ready)
                ask_for_root(b)
                finish_norm(b)

            def add_result(b):
                for g in range(BG):
                    v.wait_ge(s_res[0][b], g + 1)
                    x = slice((b * BG + g) * GW, (b * BG + g + 1) * GW)
                    v.tensor_tensor(X[:, x], X[:, x], A[:, x], ALU.add).then_inc(s_X[0][b], 1)

            def add_to_x(e, b):
                v.wait_ge(s_cf, noff[0])
                for t in range(b * BT, b * BT + OWN * GT):
                    a = A[:, t * D:(t + 1) * D]
                    step(v.tensor_scalar(a, a, RS[:, t:t + 1], NB[:, t:t + 1], ALU.mult, ALU.add))
                settle()
                for g in range(OWN):
                    x = slice((b * BG + g) * GW, (b * BG + g + 1) * GW)
                    v.tensor_tensor(X[:, x], X[:, x], A[:, x], ALU.add).then_inc(s_xv[e][b], 1)
                for g in range(BG):
                    if g < OWN:
                        v.wait_ge(s_xv[e][b], g + 1)
                    else:
                        v.wait_ge(s_X[e][b], g - OWN + 1)
                    group_stats(X, b, g)

            for b in range(BATCH):
                v.wait_ge(s_u[b], 16 * BG)
                layer_norm(X, b)

            v.wait_ge(s_wm, 16)
            v.wait_ge(s_dtp, 1)
            N2 = 2 * TILES
            step(v.tensor_tensor(dt0[:, 0:N2].rearrange("p (t h) -> p t h", h=2),
                                 PB[2][:, 0:N2].rearrange("p (t h) -> p t h", h=2),
                                 wm("dt_bias").unsqueeze(1).broadcast_to([P, TILES, 2]), ALU.add))
            step(v.tensor_copy(dt0[:, N2:NT], wm("a_param")))
            for h in range(HEADS):
                w = wm("wout", h * P, (h + 1) * P)
                step(v.tensor_scalar(w, w, wm("rms_w", h, h + 1), None, ALU.mult))
            settle()
            step(v.tensor_scalar(dt1[:, :], dt0[:, :], -1.0, None, ALU.mult))
            settle()
            v.tensor_tensor(dt1[:, :], dt1[:, :], dt0[:, :], ALU.min).then_inc(s_sp, 1)
            v.wait_ge(s_spa, 1)
            v.tensor_scalar(dt2[:, :], dt1[:, :], 1.0, None, ALU.add).then_inc(s_sp, 1)
            v.wait_ge(s_sp, 2)
            step(v.tensor_scalar(dt3[:, :], dt2[:, :], -1.0, None, ALU.add))
            settle()
            step(v.tensor_tensor(dt3[:, :], dt1[:, :], dt3[:, :], ALU.subtract))
            v.wait_ge(s_spa, 2)
            settle()
            step(v.reciprocal(dt1[:, :], dt2[:, :]))
            settle()
            step(v.tensor_tensor(dt3[:, :], dt3[:, :], dt1[:, :], ALU.mult))
            step(v.tensor_scalar(dt0[:, :], dt0[:, :], 0.0, None, ALU.max))
            settle()
            step(v.tensor_tensor(dt3[:, :], dt3[:, :], LG[:, 0:NT], ALU.add))
            settle()
            step(v.tensor_tensor(dt3[:, :], dt3[:, :], dt0[:, :], ALU.add))
            v.wait_ge(s_spa, 3)
            settle()
            step(v.tensor_scalar(lru_c[:, :], dt3[:, N2:NT], -8.0, None, ALU.mult))
            step(v.tensor_scalar(lru_c2[:, :], dt3[:, N2:NT], -16.0, None, ALU.mult))
            v.scalar_tensor_tensor(dt2[:, 0:N2].rearrange("p (t h) -> p t h", h=2),
                                   dt3[:, 0:N2].rearrange("p (t h) -> p t h", h=2), -1.0,
                                   negA[:, :].unsqueeze(1).broadcast_to([P, TILES, 2]), ALU.mult, ALU.mult).then_inc(s_sp, 1)
            v.wait_ge(s_zero, 3)
            v.wait_ge(s_const, N_CONST)

            def conv(g, j):
                n = 3 * g + j
                v.wait_ge(s_ev, block_order.index((g, j)) + 1)
                if g >= 2:
                    v.wait_ge(s_xc, n - 5)
                j = CB[j]
                o = cv[g % 2][j]
                for k in range(TAPS):
                    i = xin[j][:, (g % BG) * GW + k:(g % BG) * GW + k + GW]
                    w = wm("conv_w", 4 * j + k, 4 * j + k + 1)
                    if k == 0:
                        v.tensor_scalar(o, i, w, wm("conv_b", j, j + 1), ALU.mult, ALU.add).then_inc(s_conv, 1)
                    else:
                        v.wait_ge(s_conv, 4 * n + k)
                        v.scalar_tensor_tensor(o, i, w, o, ALU.mult, ALU.add).then_inc(s_conv, 1)

            def front(k):
                q = k % 2
                dec = FR[q][:, 0:256].rearrange("p (h t) -> p h t", h=2)
                v.wait_ge(s_g, k + 1)
                if k >= 2:
                    v.wait_ge(s_Bw, k - 1)
                for h in range(HEADS):
                    v.tensor_tensor_scan(LB[q][:, h, :], dec[:, h, :], ident[:, :], 0.0, ALU.mult, ALU.add).then_inc(s_L, 1)
                if k >= 2:
                    v.wait_ge(s_CE, k - 1)
                    v.wait_ge(s_upd, 2 * k)
                for h in range(HEADS):
                    v.tensor_tensor_scan(EB[q][:, h, :], dec[0:NS, h, :], zeros[0:NS, :].broadcast_to([NS, P]),
                                         1.0, ALU.mult, ALU.add).then_inc(s_E, 1)
                v.wait_ge(s_L, 2 * k + 2)
                if k >= 2:
                    v.wait_ge(s_S, k - 1)
                gp = FR[q][:, 256:256 + NS + P]
                v.tensor_tensor(MB[q][:, :, :], LB[q][:, :, :], gp[:, NS:NS + P].unsqueeze(1).broadcast_to([P, HEADS, P]),
                                ALU.mult).then_inc(s_M, 1)
                v.tensor_tensor(BW[q][:, :, :], LB[q][:, :, P - 1:P].broadcast_to([P, HEADS, NS]),
                                gp[:, 0:NS].unsqueeze(1).broadcast_to([P, HEADS, NS]), ALU.mult).then_inc(s_Bw, 1)

            def back(k):
                q = k % 2
                v.wait_ge(s_S, k + 1)
                v.wait_ge(s_E, 2 * k + 2)
                v.wait_ge(s_upd, 2 * k + 2)
                if k == BT - 1:
                    for h in range(HEADS):
                        v.memset(ST[1 - q][:, h * P:(h + 1) * P], 0.0).then_inc(s_upd, 1)
                    return
                for h in range(HEADS):
                    a, z = h * P, (h + 1) * P
                    v.scalar_tensor_tensor(ST[1 - q][:, a:z], ST[q][:, a:z], EB[q][:, h, P - 1:P],
                                           SP[0:NS, a:z], ALU.mult, ALU.add).then_inc(s_upd, 1)

            def post(g):
                for h in range(HEADS):
                    if g >= 1:
                        v.wait_ge(s_ysq, 2 * g)
                        v.wait_ge(s_yf, 2 * g)
                    v.scalar_tensor_tensor(Y[h], xc[g % 2][h], wm("d_skip", h, h + 1), YP[h][:, :],
                                           ALU.mult, ALU.add).then_inc(s_post, 1)

            def ask_for_r(b):
                h = slice(b * BT, (b + 1) * BT)
                v.wait_ge(s_oev, BT * (b + 1))
                v.tensor_scalar(ssq[:, h], ssq[:, h], 1.0 / DI, RMS_EPS, ALU.mult, ALU.add).then_inc(s_var, 1)

            def result_moments(b):
                h = slice(b * BT, (b + 1) * BT)
                root(SD[:, h], ssq[:, h])
                moments(b, 0.0)
                step(v.tensor_tensor(VR[:, h], VR[:, h], DF[:, h], ALU.add))
                step(v.tensor_tensor(SD[:, h], ssq[:, h], ssq[:, h], ALU.mult))
                settle()
                step(v.tensor_tensor(VR[:, h], VR[:, h], SD[:, h], ALU.mult))
                settle()
                v.tensor_scalar(VR[:, h], VR[:, h], LN_EPS, None, ALU.add).then_inc(s_var, 1)

            def result_scale(b):
                h = slice(b * BT, (b + 1) * BT)
                root(SD[:, h], RS[:, h])
                step(v.tensor_tensor(RS[:, h], RS[:, h], ssq[:, h], ALU.mult))
                settle()
                offsets(h)

            def first_row(k):
                if k == 20:
                    ask_for_r(0)
                    group_stats(A, 0, 0)
                    group_stats(A, 0, 1)
                elif k == 21:
                    group_stats(A, 0, 2)
                    group_stats(A, 0, 3)
                    result_moments(0)
                elif k == 22:
                    result_scale(0)
                elif k == 25:
                    group_stats(X, 0, 0, s_X[0][0])
                    group_stats(X, 0, 1, s_X[0][0])
                elif k == 26:
                    group_stats(X, 0, 2, s_X[0][0])
                    group_stats(X, 0, 3, s_X[0][0])
                    ask_for_root(0)
                elif k == 27:
                    finish_norm(0)

            v.memset(ST[0][:, 0:P], 0.0).then_inc(s_upd, 1)
            v.memset(ST[0][:, P:DI], 0.0).then_inc(s_upd, 1)
            for j in range(3):
                conv(0, j)
            front(0)
            conv(1, 0)
            for k in range(TILES):
                g, c = divmod(k, GT)
                if k + 1 < TILES:
                    front(k + 1)
                for gj in carried(CONV, g, c):
                    conv(*gj)
                back(k)
                if c == GT - 1:
                    post(g)
                first_row(k)
            v.wait_ge(s_yf, 8)
            v.wait_ge(s_upd, 34)

            NEC = E * BT
            for h in range(2):
                lg = LG[:, h * NEC:(h + 1) * NEC]
                if h == 0:
                    v.wait_ge(s_ev, block_order.index(("logits", 0)) + 1)
                else:
                    ask_for_r(1)
                    for g in range(BG):
                        group_stats(A, 1, g)
                    result_moments(1)
                    result_scale(1)
                    add_result(1)
                    layer_norm(X, 1, s_X[0][1])
                    v.wait_ge(s_lg, 1)
                    step(v.tensor_copy(lg, PB[3][:, 0:NEC]))
                    settle()
                for t in range(BT):
                    k = 8 * (h * BT + t)
                    step(v.max(top8[:, k:k + 8], lg[:, E * t:E * t + E]))
                settle()
                for t in range(BT):
                    k = 8 * (h * BT + t)
                    step(v.max_index(sel8[:, k:k + 8], top8[:, k:k + 8], lg[:, E * t:E * t + E]))
                k8 = slice(8 * h * BT, 8 * (h + 1) * BT)
                t8 = top8[:, k8].rearrange("p (t k) -> p t k", k=8)
                w3 = tw3[:, h * BT:(h + 1) * BT, :]
                v.tensor_tensor(w3, t8[:, :, 0:TOPK], t8[:, :, 0:1].broadcast_to([P, BT, TOPK]), ALU.subtract).then_inc(s_ex, 1)
                settle()
                step(v.tensor_copy(self_[:, k8], sel8[:, k8]))
                settle()
                s8 = self_[:, k8].rearrange("p (t k) -> p t k", k=8)
                hc = slice(h * NEC, (h + 1) * NEC)
                for k in range(TOPK):
                    step(v.tensor_tensor(oh[k][:, hc].rearrange("p (e t) -> p e t", e=E),
                                         iotaE[:, :].unsqueeze(2).broadcast_to([P, E, BT]),
                                         s8[:, :, k:k + 1].rearrange("p t k -> p k t").broadcast_to([P, E, BT]), ALU.is_equal))
                settle()
                step(v.tensor_tensor(MK[:, hc], oh[0][:, hc], oh[1][:, hc], ALU.add))
                settle()
                v.tensor_tensor(MK[:, hc], MK[:, hc], oh[2][:, hc], ALU.add).then_inc(s_mk, 1)
                v.wait_ge(s_rk, h + 1)
                rank, count = PB[4 + 2 * h][:, 0:NEC], PB[5 + 2 * h][:, 0:NEC]
                step(v.tensor_tensor_scan(PI[:, hc], segE[:, :], count, 0.0, ALU.mult, ALU.add))
                settle()
                step(v.tensor_tensor(PO[:, hc], PI[:, hc], count, ALU.subtract))
                n_e = PI[:, hc].rearrange("p (e t) -> p e t", e=E)[:, :, BT - 1]
                hs = slice(h * E, (h + 1) * E)
                step(v.tensor_scalar(TCi[:, hs], n_e, 1.0 / P, 127.0 / P - 0.5 + 1.0 / 256, ALU.mult, ALU.add))
                settle()
                step(v.tensor_copy(TCf[:, hs], TCi[:, hs]))
                step(v.tensor_tensor(PO[:, hc], PO[:, hc], rank, ALU.add))
                settle()
                step(v.tensor_tensor_scan(BT0[:, hs], ones[:, 0:E], TCf[:, hs], 0.0, ALU.mult, ALU.add))
                settle()
                step(v.tensor_tensor(BT0[:, hs], BT0[:, hs], TCf[:, hs], ALU.subtract))
                settle()
                step(v.tensor_scalar(BS[:, hs], BT0[:, hs], float(P), float(h * HT_ * P), ALU.mult, ALU.add))
                settle()
                po = PO[:, hc].rearrange("p (e t) -> p e t", e=E)
                step(v.tensor_tensor(po, po, BS[:, hs].unsqueeze(2).broadcast_to([P, E, BT]), ALU.add))
                settle()
                pk = posf[:, :].rearrange("p (k t) -> p k t", k=TOPK)
                for k in range(TOPK):
                    step(v.tensor_tensor(oh[k][:, hc], oh[k][:, hc], PO[:, hc], ALU.mult))
                settle()
                for k in range(TOPK):
                    step(v.tensor_reduce(pk[:, k, h * BT:(h + 1) * BT], oh[k][:, hc].rearrange("p (e t) -> p t e", e=E),
                                         AX.X, ALU.add))
                settle()
                v.tensor_copy(posu[:, :].rearrange("p (k t) -> p k t", k=TOPK)[:, :, h * BT:(h + 1) * BT],
                              pk[:, :, h * BT:(h + 1) * BT]).then_inc(s_pos, 1)
                ts = tsum[:, h * BT:(h + 1) * BT]
                v.wait_ge(s_exd, h + 1)
                step(v.tensor_reduce(ts, w3, AX.X, ALU.add))
                settle()
                step(v.reciprocal(ts, ts))
                settle()
                step(v.tensor_tensor(w3, w3, ts.unsqueeze(2).broadcast_to([P, BT, TOPK]), ALU.mult))
                settle()
            for h in range(2):
                ge = GE[:, :].rearrange("p (j e) -> p j e", e=E)
                step(v.tensor_tensor(ge, iotaJ[:, :].unsqueeze(2).broadcast_to([P, HT_, E]),
                                     BT0[:, h * E:(h + 1) * E].unsqueeze(1).broadcast_to([P, HT_, E]), ALU.is_ge))
                settle()
                step(v.tensor_reduce(etf[:, h * HT_:(h + 1) * HT_], ge, AX.X, ALU.add))
                settle()
            step(v.tensor_scalar(etf[:, :], etf[:, :], -1.0, None, ALU.add))
            settle()
            v.tensor_copy(eti[:, :], etf[:, :]).then_inc(s_et, 1)
            step(v.tensor_scalar(SEL[:, :], etf[:, :], wl("row_expert"), None, ALU.is_equal))
            step(v.tensor_copy(cmask[:, :, :], wl("row_chunk").unsqueeze(2).broadcast_to([P, HC, P])))
            v.wait_ge(s_bias, 32)
            step(v.tensor_copy(biash[:, :], biasr[:, :]))
            settle()
            step(v.tensor_copy(biast[LOW:P, :], biash[LOW:P, :].bitcast(F32)))
            settle()
            v.tensor_tensor(biash[LOW:P, :], biasr[LOW:P, :], biast[LOW:P, :], ALU.subtract).then_inc(s_bh, 1)
            settle()

            def evict_slots(q, j):
                n, i, _ = tile(q, j)
                v.wait_ge(s_xp, n + 1)
                if since(n - 1):
                    v.wait_ge(s_up, n - 1)
                v.tensor_copy(XGT[i % 2][:, :], PB[i % 2][:, 0:P]).then_inc(s_xe, 1)
                if since(n - 3):
                    v.wait_ge(s_dn, n - 3)
                col = SEL[:, n:n + 1] if isinstance(n, int) else SEL[:, bass.ds(n, 1)]
                v.tensor_scalar(SELB[i][:, :], cmask[:, :, :].rearrange("p c t -> p (c t)"), col, None,
                                ALU.mult).then_inc(s_xe, 1)

            def evict_result(q, j):
                n, i, turn = tile(q, j)
                v.wait_ge(s_dn, n + 1)
                if since(turn):
                    v.wait_ge(s_ys[i], turn * 16)
                v.tensor_copy(YT[i][:, :], PB[6 + i % 2][:, 0:D]).then_inc(s_ye, 1)

            def dve_step(q, i):
                if not (isinstance(q, int) and q * RING + i + 2 >= ST_):
                    evict_slots(q, i + 2)
                evict_result(q, i)

            evict_slots(0, 0)
            evict_slots(0, 1)

            def beside(m):
                if m == 0:
                    v.wait_ge(s_cmb0, 3)
                if m < 4:
                    group_stats(A, 0, m)
                elif m == 4:
                    ask_for_root(0)
                elif m == 6:
                    finish_norm(0)
                elif 8 <= m < 12:
                    v.wait_ge(s_res[1][0], m - 7)
                    x = slice((m - 8) * GW, (m - 7) * GW)
                    v.tensor_tensor(X[:, x], X[:, x], A[:, x], ALU.add).then_inc(s_X[1][0], 1)
                elif 12 <= m < 16:
                    group_stats(X, 0, m - 12, s_X[1][0])
                    if m == 15:
                        ask_for_root(0)
                elif m == 17:
                    finish_norm(0)

            pipeline(v, dve_step, beside)

            nsum = [0]

            def sums(i):
                v.wait_ge(s_rg1[i], 16 * TOPK * PAIR)
                tiles = range(BT + i * PAIR, BT + (i + 1) * PAIR)
                for k in range(TOPK):
                    for t in tiles:
                        r = RG[:, (t * TOPK + k) * D:(t * TOPK + k + 1) * D]
                        a, w = A[:, t * D:(t + 1) * D], tw3[:, t, k:k + 1]
                        if k == 0:
                            v.tensor_scalar(a, r, w, None, ALU.mult).then_inc(s_cmb, 1)
                        else:
                            v.wait_ge(s_cmb, nsum[0] - PAIR + 1)
                            v.scalar_tensor_tensor(a, r, w, a, ALU.mult, ALU.add).then_inc(s_cmb, 1)
                        nsum[0] += 1
                v.wait_ge(s_cmb, nsum[0])
                for t in tiles:
                    tile_stats(A, t)

            def merge(b):
                h = slice(b * BT, (b + 1) * BT)
                moments(b, LN_EPS)
                v.tensor_tensor(VR[:, h], VR[:, h], DF[:, h], ALU.add).then_inc(s_var, 1)
                root(SD[:, h], RS[:, h])
                offsets(h)
                add_to_x(1, b)
                ask_for_root(b)
                finish_norm(b)

            def lru(b):
                G0, G1, G2, G3 = G[b]
                cp = CP[b]
                step(v.memset(cp[:, 0:1], 1.0))
                if b == 0:
                    v.wait_ge(s_gs, 2 * BG)
                    step(v.tensor_tensor(G0, T[:, 0:SEQ], G0, ALU.mult))
                settle()
                v.wait_ge(s_aa, 2 * b + 1)
                step(v.tensor_tensor_scan(cp[:, 1:SEQ], G2[:, 0:SEQ - 1], floor[:, :].broadcast_to([P, SEQ - 1]),
                                          1.0, ALU.mult, ALU.max))
                v.wait_ge(s_aa, 2 * b + 2)
                v.tensor_scalar(G3, G3, 1.0, -1e-7, ALU.subtract, ALU.min).then_inc(s_1a, 1)
                if b == 1:
                    default_scale(0)
                settle()
                step(v.reciprocal(G2, cp[:, 0:SEQ]))
                if b == 1:
                    default_offset(0)
                if b == 0:
                    v.wait_ge(s_mu, 1)
                    step(v.tensor_tensor(G0, G0, G3, ALU.mult))
                else:
                    v.wait_ge(s_xg, 2)
                settle()
                step(v.tensor_tensor(G0, G0, G2, ALU.mult))
                settle()
                step(v.tensor_tensor_scan(G3, G0, zeros[:, :].broadcast_to([P, SEQ]), 0.0, ALU.add, ALU.add))
                settle()
                for g in range(BG):
                    x = slice(g * GW, (g + 1) * GW)
                    v.tensor_tensor(G1[:, x], cp[:, x], G3[:, x], ALU.mult).then_inc(s_h, 1)

            def scores(b):
                h = slice(b * BT, (b + 1) * BT)
                for g in range(BG):
                    v.wait_ge(s_he, BG * b + g + 1)
                    group_stats(A, b, g)
                ask_for_root(b)
                finish_norm(b)
                add_to_x(2, b)

                moments(b, 0.0)
                step(v.tensor_tensor(VR[:, h], VR[:, h], DF[:, h], ALU.add))
                settle()
                v.tensor_scalar(DF[:, h], VR[:, h], LN_EPS, None, ALU.add).then_inc(s_var, 1)
                for t in range(b * BT, (b + 1) * BT):
                    products = G[b][2][:, (t % BT) * D:(t % BT + 1) * D]
                    step(v.scalar_tensor_tensor(products, X[:, t * D:(t + 1) * D], MN[:, t:t + 1], wl("router"),
                                                ALU.subtract, ALU.mult, accum_out=sc[:, t:t + 1]))

            def default_scale(b):
                h = slice(b * BT, (b + 1) * BT)
                root(SD[:, h], RS[:, h])
                v.tensor_tensor(sc[:, h], sc[:, h], RS[:, h], ALU.mult).then_inc(s_sc, 1)
                step(v.tensor_tensor(VR[:, h], VR[:, h], RS[:, h], ALU.mult))
                settle()
                step(v.tensor_tensor(VR[:, h], VR[:, h], RS[:, h], ALU.mult))
                settle()
                v.tensor_scalar(VR[:, h], VR[:, h], LN_EPS, None, ALU.add).then_inc(s_var, 1)

            def default_offset(b):
                h = slice(b * BT, (b + 1) * BT)
                root(SD[:, h], DF[:, h])
                step(v.tensor_tensor(DF[:, h], DF[:, h], RS[:, h], ALU.mult))
                settle()
                step(v.tensor_scalar(DS[:, h], DF[:, h], 1.0, None, ALU.add))
                settle()
                v.scalar_tensor_tensor(DB[:, h], MN[:, h], -1.0, DF[:, h], ALU.mult, ALU.mult).then_inc(s_cf, 1)
                noff[0] += 1

            lru(0)
            for i in range(BT // PAIR):
                sums(i)
            merge(1)
            scores(0)
            lru(1)
            scores(1)
            default_scale(1)
            default_offset(1)

            def largest(values, spare, winners_v, winners_i, steps):
                rounds = CAP // 8
                for r in range(rounds):
                    k8 = slice(8 * r, 8 * r + 8)
                    v.max(winners_v[:, k8], values).then_inc(steps, 1)
                    v.wait_ge(steps, 3 * r + 1)
                    if r + 1 < rounds:
                        v.match_replace(spare, winners_v[:, k8], values, -3.0e38).then_inc(steps, 1)
                    v.max_index(winners_i[:, k8], winners_v[:, k8], values).then_inc(steps, 1)
                    if r + 1 < rounds:
                        v.wait_ge(steps, 3 * r + 3)
                    values, spare = spare, values
                v.wait_ge(steps, 3 * rounds - 1)

            v.wait_ge(s_row, 16)
            largest(row, spare, v8, i8, s_tk)
            v.tensor_scalar(i8g[:, :], i8[:, :], rowoff[:, 0:1], None, ALU.add).then_inc(s_tk, 1)
            v.wait_ge(s_row2, 16)
            largest(row2[:, :], spare2[:, :], v2, i2, s_tk2)
            v.tensor_scalar(i2g[:, :], i2[:, :], rowoff2[:, 0:1], None, ALU.add).then_inc(s_tk2, 1)

            vd = [0]

            def vstep(ins):
                ins.then_inc(s_vd, 1)
                vd[0] += 1

            def vsettle():
                v.wait_ge(s_vd, vd[0])

            def row_stats(src, eps):
                step(v.bn_stats(st6[:, 0:6], src))
                settle()
                step(v.bn_aggr(c1[0][:, 0:2], st6[:, 0:6]))
                settle()
                v.tensor_scalar(c1[0][:, 1:2], c1[0][:, 1:2], eps, None, ALU.add).then_inc(s_var, 1)
                root(c1[1][:, 1:2], c1[1][:, 2:3])

            def row_norm(dst, src, eps):
                row_stats(src, eps)
                step(v.tensor_scalar(dst, src, c1[0][:, 0:1], c1[1][:, 2:3], ALU.subtract, ALU.mult))
                settle()

            def rms(dst, src):
                step(v.tensor_tensor(SQ[:, :], src, src, ALU.mult))
                settle()
                step(v.tensor_reduce(c1[0][:, 4:5], SQ[:, :], AX.X, ALU.add))
                settle()
                v.tensor_scalar(c1[0][:, 5:6], c1[0][:, 4:5], 1.0 / D, FF_EPS, ALU.mult, ALU.add).then_inc(s_var, 1)
                root(c1[1][:, 1:2], c1[1][:, 3:4])
                vstep(v.tensor_scalar(dst, src, c1[1][:, 3:4], None, ALU.mult))

            v.wait_ge(s_gat, 16)
            row_norm(XN[:, :], XS[:, :], LN_EPS)
            rms(HN[:, :], XN[:, :])
            v.wait_ge(s_ad, 3)
            kM3 = kM.rearrange("p (h k) -> p h k", h=AH)
            vstep(v.tensor_tensor(kM3, kT[:, :].unsqueeze(1).broadcast_to([P, AH, P]),
                                  hmask[:, :].unsqueeze(2).broadcast_to([P, AH, P]), ALU.mult))
            for i in range(4):
                v.wait_ge(s_pd, 4 + i + 1)
                step(v.tensor_tensor(SM[:, i * 512:(i + 1) * 512].rearrange("p (h k) -> p h k", h=4),
                                     PB[i][:, :].rearrange("p (h k) -> p h k", h=4),
                                     amask[:, :].unsqueeze(1).broadcast_to([P, 4, P]), ALU.add))
            settle()
            SM3 = SM.rearrange("p (h k) -> p h k", h=AH)
            step(v.tensor_reduce(mx[:, :], SM3, AX.X, ALU.max))
            settle()
            vstep(v.tensor_tensor(SM3, SM3, mx[:, :].unsqueeze(2).broadcast_to([P, AH, P]), ALU.subtract))
            v.wait_ge(s_ad, 5)
            step(v.tensor_reduce(sm[:, :], SM3, AX.X, ALU.add))
            settle()
            step(v.reciprocal(sm[:, :], sm[:, :]))
            settle()
            v.wait_ge(s_pd, 13)
            vstep(v.tensor_tensor(O[:, :].rearrange("p (h d) -> p h d", h=AH),
                                  PB[4][:, 0:D].rearrange("p (h d) -> p h d", h=AH),
                                  sm[:, :].unsqueeze(2).broadcast_to([P, AH, HD]), ALU.mult))
            v.wait_ge(s_pd, 15)
            step(v.tensor_tensor(XA[:, :], XN[:, :], PB[5][:, 0:D], ALU.add))
            settle()
            rms(HN[:, :], XA[:, :])
            for i in range(3):
                v.wait_ge(s_ad, 12 + i)
                vstep(v.tensor_tensor(gg[i][0:FC[i], :], u1[i][0:FC[i], :], PB[4][0:FC[i], i * P:(i + 1) * P], ALU.mult))
            v.wait_ge(s_pd, 18)
            step(v.tensor_tensor(PR[:, :], XA[:, :], PB[5][:, 0:D], ALU.add))
            settle()
            row_norm(PR[:, :], PR[:, :], LN_EPS)
            vstep(v.tensor_tensor(PR[:, :], PR[:, :], XS[:, :], ALU.add))
            assert vd[0] == 9, vd

        @block.scalar
        def _(act):
            nvar = [0]

            def sqrt(dst, src):
                nvar[0] += 1
                act.wait_ge(s_var, nvar[0])
                act.activation(dst, src, ACT.Sqrt).then_inc(s_sd, 1)

            ncf = [0]

            def normalise(dst, src, g, done, scale=RS, offset=NB):
                for t in range(g * GT, (g + 1) * GT):
                    i = act.activation(dst[:, t * D:(t + 1) * D], src[:, t * D:(t + 1) * D], ACT.Identity,
                                       scale=scale[:, t:t + 1], bias=offset[:, t:t + 1])
                i.then_inc(done, 1)

            def coefficients():
                ncf[0] += 1
                act.wait_ge(s_cf, ncf[0])

            def root_of_row(b):
                sqrt(SD[:, b * BT:(b + 1) * BT], VR[:, b * BT:(b + 1) * BT])

            def norm(r, b, rooted=False, next_root=None, early_root=None):
                if not rooted:
                    root_of_row(b)
                coefficients()
                for g in range(BG + 1):
                    if g == BG - 1 and early_root is not None:
                        root_of_row(early_root)
                    if g < BG:
                        normalise(NX, X, b * BG + g, s_xn[r][b])
                    if g == BG - 1 and next_root is not None:
                        root_of_row(next_root)
                    if g >= 1:
                        k = b * BG + g - 1
                        act.wait_ge(s_tr[r][b], g)
                        act.activation(T[:, k * GW:(k + 1) * GW], PB[k % 2][:, :], ACT.Copy).then_inc(s_T[r][b], 1)

            def normalise_result(e, b, rooted=False):
                if not rooted:
                    root_of_row(b)
                coefficients()
                for g in range(OWN if e else 0, BG):
                    normalise(A, A, b * BG + g, s_res[e][b])

            norm(0, 0, next_root=1)
            norm(0, 1, rooted=True)
            act.wait_ge(s_sp, 1)
            act.activation(dt1[:, :], dt1[:, :], ACT.Exp).then_inc(s_spa, 1)
            act.wait_ge(s_sp, 2)
            act.activation(LG[:, 0:NT], dt2[:, :], ACT.Ln).then_inc(s_spa, 1)
            act.wait_ge(s_wm, 16)
            act.activation(negA[:, :], wm("a_log"), ACT.Exp).then_inc(s_spa, 1)
            act.wait_ge(s_sp, 3)
            act.activation(decay[:, :], dt2[:, 0:2 * TILES], ACT.Exp).then_inc(s_decay, 1)

            def evict_in(g, j):
                n = block_order.index((g, j))
                act.wait_ge(s_in, n + 1)
                src = IN[:, :]
                if g == "T":
                    act.activation(T[:, j * GW:(j + 1) * GW], src, ACT.Copy).then_inc(s_ev, 1)
                elif g == "logits":
                    act.activation(LG[:, 0:E * BT], IN[:, 0:E * BT], ACT.Copy).then_inc(s_ev, 1)
                elif j < 3:
                    if g >= BG:
                        act.wait_ge(s_conv, TAPS * (3 * (g - 3) + j + 1))
                    c = TAPS - 1 + (g % BG) * GW
                    act.copy(xin[CB[j]][:, c:c + GW], src).then_inc(s_ev, 1)
                else:
                    if g >= 2:
                        act.wait_ge(s_yf, 2 * (g - 1))
                    act.activation(sigz[g % 2][j - 3], src, ACT.Sigmoid).then_inc(s_ev, 1)

            def conv_sigmoid(g, j):
                n = 3 * g + j
                act.wait_ge(s_conv, 4 * n + 4)
                if n >= 2:
                    act.wait_ge(s_xc, n - 1)
                act.activation(sg[n % 2], cv[g % 2][CB[j]], ACT.Sigmoid).then_inc(s_sig, 1)

            def evict_x(k):
                q = k % 2
                act.wait_ge(s_tp, k + 1)
                if k >= 2:
                    act.wait_ge(s_S, k - 1)
                act.copy(XT[q][:, :], XP[:, 0:DI]).then_inc(s_xt, 1)

            def evict_out(g, c):
                k = g * GT + c
                act.wait_ge(s_out, k + 1)
                act.copy(A[:, k * D:(k + 1) * D], OP[:, 0:D])
                act.copy(ssq[:, k:k + 1], OP[:, D:D + 1]).then_inc(s_oev, 1)
            for j in range(3):
                evict_in(0, j)
            conv_sigmoid(0, 0)
            conv_sigmoid(0, 1)
            evict_in(1, 0)
            conv_sigmoid(0, 2)
            evict_x(0)
            evict_in(1, 1)
            def first_row(k):
                h = slice(0, BT)
                if k == 21:
                    sqrt(SD[:, h], ssq[:, h])
                elif k == 22:
                    sqrt(SD[:, h], VR[:, h])
                elif k == 23:
                    coefficients()
                    for g in (0, 1):
                        normalise(A, A, g, s_res[0][0])
                elif k == 24:
                    for g in (2, 3):
                        normalise(A, A, g, s_res[0][0])
                elif k == 27:
                    sqrt(SD[:, h], VR[:, h])
                elif k == 28:
                    coefficients()
                    for g in (0, 1):
                        normalise(NX, X, g, s_xn[1][0])
                elif k == 29:
                    for g in (2, 3):
                        normalise(NX, X, g, s_xn[1][0])

            for k in range(TILES):
                g, c = divmod(k, GT)
                if k + 1 < TILES:
                    evict_x(k + 1)
                first_row(k)
                for gj in carried(EARLY, g, c):
                    evict_in(*gj)
                for gj in carried(GATE, g, c):
                    conv_sigmoid(*gj)
                if g >= 1:
                    evict_out(g - 1, c)
                for gj in carried(FILL, g, c) + LATE.get(k, []):
                    evict_in(*gj)
                if c == GT - 1:
                    if g >= 1:
                        act.wait_ge(s_out, GT * g)
                    for h in range(HEADS):
                        act.wait_ge(s_post, 2 * g + h + 1)
                        act.activation(YSQ[h], Y[h], ACT.Square).then_inc(s_ysq, 1)
            act.wait_ge(s_out, TILES)
            act.copy(A[:, TOKENS - GW:TOKENS], IN[:, :])
            act.copy(ssq[:, TILES - GT:TILES], OP[:, 0:GT]).then_inc(s_oev, GT)
            act.wait_ge(s_oev, TILES)

            def gate_exponentials(h):
                act.wait_ge(s_ex, h + 1)
                w = tw[:, h * BT * TOPK:(h + 1) * BT * TOPK]
                act.activation(w, w, ACT.Exp).then_inc(s_exd, 1)

            gate_exponentials(0)
            sqrt(SD[:, BT:TILES], ssq[:, BT:TILES])
            normalise_result(0, 1)
            norm(1, 1)
            gate_exponentials(1)

            act.wait_ge(s_et, 1)
            act.wait_ge(s_wup, 16 * 8)

            def fetch_up_weights(q, j):
                n, i, _ = tile(q, j)
                if since(n - 1):
                    act.wait_ge(s_up, n - 1)
                    act.sem_inc(s_apart, 1)
                src = eti[0:1, n:n + 1] if isinstance(n, int) else eti[0:1, bass.ds(n, 1)]
                e = act.value_load(src, min_val=0, max_val=E - 1)
                act.activation(WUB[i % 2][:, :], WU[:, bass.ds(e * HID, HID)], ACT.Copy).then_inc(s_wb, 1)

            def gelu(q, j):
                n, i, _ = tile(q, j)
                act.wait_ge(s_up, n + 1)
                if since(n - 1):
                    act.wait_ge(s_dn, n - 1)
                act.activation(HB[i % 2][:, :], PB[2 + i % 2][:, :], ACT.Gelu).then_inc(s_gl, 1)

            def store(q, j):
                n, i, _ = tile(q, j)
                act.wait_ge(s_ye, n + 1)
                act.sem_inc(s_apart, 1)
                dst = slots_y[n * P:(n + 1) * P, :] if isinstance(n, int) else slots_y[bass.ds(n * P, P), :]
                act.dma_start(dst, YT[i][:, :]).then_inc(s_ys[i], 16)

            def act_step(q, i):
                n = q * RING + i
                if not (isinstance(n, int) and n + 2 >= ST_):
                    fetch_up_weights(q, i + 2)
                if not (isinstance(n, int) and n + 1 >= ST_):
                    gelu(q, i + 1)
                if since(n):
                    store(q, i - 1)

            fetch_up_weights(0, 0)
            fetch_up_weights(0, 1)
            gelu(0, 0)

            def beside(m):
                if m in (5, 16):
                    root_of_row(0)
                if m in (7, 18):
                    coefficients()
                if 7 <= m < 11:
                    normalise(A, A, m - 7, s_res[1][0])
                if 18 <= m < 22:
                    normalise(NX, X, m - 18, s_xn[2][0])
                if 20 <= m < 24:
                    g = m - 20
                    act.wait_ge(s_tr[2][0], g + 1)
                    act.activation(T[:, g * GW:(g + 1) * GW], PB[4 + g % 2][:, :], ACT.Copy).then_inc(s_T[2][0], 1)

            pipeline(act, act_step, beside)
            store(QS - 1, RING - 1)
            def gates(b):
                for g in range(BG):
                    for i in range(2):
                        n = 2 * (b * BG + g) + i + 1
                        act.wait_ge(s_gt, n)
                        act.activation(G[b][i][:, g * GW:(g + 1) * GW], PB[2 + 2 * ((b * BG + g) % 3) + i][:, :], ACT.Sigmoid,
                                       bias=wl("ig_b" if i == 0 else "ag_b")).then_inc(s_gs, 1)
                act.wait_ge(s_gs, n)
                act.activation(G[b][2], G[b][1], ACT.Exp, scale=lru_c[:, 0:1]).then_inc(s_aa, 1)
                act.activation(G[b][3], G[b][1], ACT.Exp, scale=lru_c2[:, 0:1]).then_inc(s_aa, 1)

            def multiplier(b):
                act.wait_ge(s_1a, b + 1)
                act.activation(G[b][3], G[b][3], ACT.Sqrt, scale=-1.0).then_inc(s_mu, 1)

            def evict_h(b):
                for g in range(b * BG, (b + 1) * BG):
                    act.wait_ge(s_ht, g + 1)
                    act.activation(A[:, g * GW:(g + 1) * GW], PB[g % 2][:, :], ACT.Copy).then_inc(s_he, 1)

            def default_rows(b, between=None):
                h = slice(b * BT, (b + 1) * BT)
                sqrt(SD[:, h], DF[:, h])
                if between is not None:
                    between()
                if b == BATCH - 1:
                    act.wait_ge(s_sct, 1)
                    act.activation(sc32[:, :], PB[2][0:TILES, 0:P], ACT.Copy).then_inc(s_sce, 1)
                sqrt(SD[:, h], VR[:, h])
                coefficients()
                for g in range(b * BG, (b + 1) * BG):
                    normalise(A, X, g, s_fin, DS, DB)

            gates(0)
            multiplier(0)
            evict_h(0)
            normalise_result(1, 1)
            norm(2, 1, early_root=0)
            normalise_result(2, 0, rooted=True)
            gates(1)
            default_rows(0, between=lambda: multiplier(1))
            evict_h(1)
            normalise_result(2, 1)
            default_rows(1)
            sqrt(c1[1][:, 1:2], c1[0][:, 1:2])
            sqrt(c1[1][:, 1:2], c1[0][:, 5:6])
            act.wait_ge(s_pd, 1)
            act.activation(hT[:, :], PB[0][:, 0:P], ACT.Copy, scale=wl("g1")).then_inc(s_ad, 1)
            act.wait_ge(s_pd, 2)
            act.copy(qT[:, :], PB[1][:, 0:P]).then_inc(s_ad, 1)
            act.wait_ge(s_pd, 3)
            act.copy(kT[:, :], PB[2][:, 0:P]).then_inc(s_ad, 1)
            act.wait_ge(s_pd, 4)
            act.copy(vv[:, :], PB[3][:, 0:P]).then_inc(s_ad, 1)
            act.wait_ge(s_vd, 3)
            act.activation(SM, SM, ACT.Exp, scale=float(HD) ** -0.5).then_inc(s_ad, 1)
            for i in range(4):
                act.wait_ge(s_pd, 8 + i + 1)
                act.copy(PT[:, i * 512:(i + 1) * 512], PB[i][:, :]).then_inc(s_ad, 1)
            act.wait_ge(s_pd, 14)
            act.copy(OT[:, :], PB[5][:, 0:P]).then_inc(s_ad, 1)
            sqrt(c1[1][:, 1:2], c1[0][:, 5:6])
            act.wait_ge(s_pd, 16)
            act.activation(hT[:, :], PB[0][:, 0:P], ACT.Copy, scale=wl("g2")).then_inc(s_ad, 1)
            act.wait_ge(s_pd, 17)
            for i in range(3):
                act.activation(u1[i][0:FC[i], :], PB[3][0:FC[i], i * P:(i + 1) * P], ACT.Silu).then_inc(s_ad, 1)
            sqrt(c1[1][:, 1:2], c1[0][:, 1:2])

        @block.tensor
        def _(pe):
            def transposes(r, b, groups=range(BG)):
                for g in groups:
                    pe.wait_ge(s_xn[r][b], g + 1)
                    if g >= 2:
                        pe.wait_ge(s_T[r][b], g - 1)
                    elif b == 1 and r == 0:
                        pe.wait_ge(s_T[r][0], g + 3)
                    k = b * BG + g
                    for t in range(k * GT, (k + 1) * GT):
                        i = pe.transpose(PB[k % 2][:, (t % GT) * P:(t % GT + 1) * P], NX[:, t * D:(t + 1) * D], ident[:, :])
                    i.then_inc(s_tr[r][b], 1)

            pe.wait_ge(s_const, N_CONST)
            for b in range(BATCH):
                transposes(0, b)
                pe.wait_ge(s_wm, 16)
                pe.wait_ge(s_T[0][b], BG)
                for t in range(b * BT, (b + 1) * BT):
                    i = pe.matmul(PB[2][:, 2 * t:2 * t + 2], T[:, t * P:(t + 1) * P], wm("win", 640, 642), start=True, stop=True)
            i.then_inc(s_dtp, 1)
            pe.wait_ge(s_sp, 1)

            def project_in(g, j):
                n = block_order.index((g, j))
                if n >= 1:
                    pe.wait_ge(s_ev, n)
                if g == "T":
                    pe.wait_ge(s_xn[1][0], j + 1)
                    for t in range(GT):
                        i = pe.transpose(IN[:, t * P:(t + 1) * P], NX[:, (j * GT + t) * D:(j * GT + t + 1) * D], ident[:, :])
                    i.then_inc(s_in, 1)
                    return
                if g == "logits":
                    pe.wait_ge(s_wl, 16)
                    for t in range(BT):
                        i = pe.matmul(IN[:, E * t:E * t + E], T[:, t * P:(t + 1) * P], wl("gate"), start=True, stop=True)
                    i.then_inc(s_in, 1)
                    return
                c = [512, 256, 384, 0, 128][j]
                pe.matmul(IN[:, :], wm("win", c, c + P), T[:, g * GW:(g + 1) * GW],
                          start=True, stop=True).then_inc(s_in, 1)

            def front(k):
                q, (g, c) = k % 2, divmod(k, GT)
                tok = slice(c * P, (c + 1) * P)
                pe.wait_ge(s_diag, k + 1)
                if k >= 2:
                    pe.wait_ge(s_Bw, k - 1)
                pe.matmul(FR[q][:, 0:256], ones[:, :], diag[q][:, :, :].rearrange("p h t -> p (h t)"),
                          start=True, stop=True).then_inc(s_dec, 1)
                pe.wait_ge(s_xc, 3 * g + 3)
                if k >= 1:
                    pe.wait_ge(s_xt, k)
                for h in range(HEADS):
                    i = pe.transpose(XP[:, h * P:(h + 1) * P], xc[g % 2][h][:, tok], ident[:, :])
                i.then_inc(s_tp, 1)
                pe.wait_ge(s_c0, 16 * (g + 1))
                pe.matmul(FR[q][:, 256 + NS:256 + NS + P], xc[g % 2][2][0:NS, tok], C0[g % 2][:, tok],
                          start=True, stop=True)
                pe.transpose(FR[q][:, 256:256 + NS], xc[g % 2][2][0:NS, tok], ident[0:NS, 0:NS]).then_inc(s_g, 1)

            def back(k):
                q, (g, c) = k % 2, divmod(k, GT)
                tok = slice(c * P, (c + 1) * P)
                pe.wait_ge(s_M, k + 1)
                pe.wait_ge(s_xt, k + 1)
                if g >= 1:
                    pe.wait_ge(s_post, 2 * g)
                pe.wait_ge(s_CE, k + 1)
                pe.wait_ge(s_upd, 2 * k + 2)
                for h in range(HEADS):
                    a, z = h * P, (h + 1) * P
                    pe.matmul(YP[h][:, tok], XT[q][:, a:z], MB[q][:, h, :], start=True, stop=False)
                    pe.matmul(YP[h][:, tok], ST[q][:, a:z], CE[q][:, h, :], start=False, stop=True)
                pe.wait_ge(s_Bw, k + 1)
                for h in range(HEADS):
                    a, z = h * P, (h + 1) * P
                    i = pe.matmul(SP[0:NS, a:z], BW[q][:, h, :], XT[q][:, a:z], start=True, stop=True)
                i.then_inc(s_S, 1)

            def project_out(g, c):
                k = g * GT + c
                tok = slice(c * P, (c + 1) * P)
                pe.wait_ge(s_yf, 2 * g + 2)
                pe.wait_ge(s_ysq, 2 * g + 2)
                if k >= 1:
                    pe.wait_ge(s_oev, k)
                for h in range(HEADS):
                    pe.matmul(OP[:, D:D + 1], YSQ[h][:, tok], ones[:, 0:1], start=(h == 0), stop=(h == 1))
                for h in range(HEADS):
                    i = pe.matmul(OP[:, 0:D], YF[h][:, tok], wm("wout", h * P, (h + 1) * P),
                                  start=(h == 0), stop=(h == 1))
                i.then_inc(s_out, 1)
            for j in range(3):
                project_in(0, j)
            project_in(1, 0)
            front(0)
            project_in(1, 1)
            front(1)
            for k in range(TILES):
                g, c = divmod(k, GT)
                for gj in carried(EARLY, g, c):
                    project_in(*gj)
                back(k)
                if k + 2 < TILES:
                    front(k + 2)
                if g >= 1:
                    project_out(g - 1, c)
                for gj in carried(FILL, g, c) + LATE.get(k, []):
                    project_in(*gj)
            pe.wait_ge(s_ev, BLOCKS)
            pe.wait_ge(s_yf, 2 * GROUPS)
            for t in range(GT):
                for h in range(HEADS):
                    pe.matmul(IN[:, t * D:(t + 1) * D], YF[h][:, t * P:(t + 1) * P], wm("wout", h * P, (h + 1) * P),
                              start=(h == 0), stop=(h == 1))
            pe.wait_ge(s_ysq, 2 * GROUPS)
            pe.wait_ge(s_oev, TILES - GT)
            for t in range(GT):
                for h in range(HEADS):
                    i = pe.matmul(OP[:, t:t + 1], YSQ[h][:, t * P:(t + 1) * P], ones[:, 0:1], start=(h == 0), stop=(h == 1))
            i.then_inc(s_out, GT)
            pe.wait_ge(s_out, TILES)

            pe.wait_ge(s_wl, 16)
            NEC = E * BT

            def gate_logits(h):
                for t in range(BT):
                    if t % GT == 0:
                        pe.wait_ge(s_T[1][h], t // GT + 1)
                    k = h * BT + t
                    i = pe.matmul(PB[2 + h][:, E * t:E * t + E], T[:, k * P:(k + 1) * P], wl("gate"), start=True, stop=True)
                i.then_inc(s_lg, 1)

            def ranks(h):
                pe.wait_ge(s_mk, h + 1)
                mk = MK[:, h * NEC:(h + 1) * NEC]
                pe.matmul(PB[4 + 2 * h][:, 0:NEC], upper[:, :], mk, start=True, stop=True)
                pe.matmul(PB[5 + 2 * h][:, 0:NEC], ones[:, :], mk, start=True, stop=True).then_inc(s_rk, 1)

            ranks(0)
            transposes(1, 1)
            gate_logits(1)
            ranks(1)

            def transpose_slots(q, j):
                n, i, turn = tile(q, j)
                pe.wait_ge(s_xl[i], turn * 16 + 16)
                if since(n - 1):
                    pe.wait_ge(s_xe, 2 * n - 2)
                pe.transpose(PB[i % 2][:, 0:P], XG[i][:, :], ident[:, :]).then_inc(s_xp, 1)

            def project_up(q, j):
                n, i, _ = tile(q, j)
                pe.wait_ge(s_xe, 2 * n + 2)
                pe.wait_ge(s_wb, n + 1)
                if since(n - 1):
                    pe.wait_ge(s_gl, n - 1)
                pe.matmul(PB[2 + i % 2][:, :], biash[:, 0:P], SELB[i][:, :], start=True, stop=False)
                for c in range(HC):
                    b = PB[2 + i % 2][:, c * P:(c + 1) * P]
                    m = pe.matmul(b, WUB[i % 2][:, c * P:(c + 1) * P], XGT[i % 2][:, :],
                                  start=False, stop=(c == HC - 1))
                m.then_inc(s_up, 1)

            def project_down(q, j):
                n, i, _ = tile(q, j)
                src = eti[0:1, n:n + 1] if isinstance(n, int) else eti[0:1, bass.ds(n, 1)]
                e = pe.value_load(src, min_val=0, max_val=E - 1)
                pe.wait_ge(s_gl, n + 1)
                if since(n - 1):
                    pe.wait_ge(s_ye, n - 1)
                b = PB[6 + i % 2][:, 0:D]
                pe.matmul(b, SELB[i][:, 0:P], biash[:, P:P + D], start=True, stop=False)
                for c in range(HC):
                    m = pe.matmul(b, HB[i % 2][:, c * P:(c + 1) * P], WD[:, bass.ds(e * HID + c * D, D)],
                                  start=False, stop=(c == HC - 1))
                m.then_inc(s_dn, 1)

            def pe_step(q, i):
                n = q * RING + i
                if not (isinstance(n, int) and n + 2 >= ST_):
                    transpose_slots(q, i + 2)
                if not (isinstance(n, int) and n + 1 >= ST_):
                    project_up(q, i + 1)
                project_down(q, i)

            pe.wait_ge(s_et, 1)
            pe.wait_ge(s_bh, 1)
            pe.wait_ge(s_wup, 16 * 8)
            transpose_slots(0, 0)
            transpose_slots(0, 1)
            project_up(0, 0)

            def beside(m):
                if 19 <= m < 23:
                    g = m - 19
                    pe.wait_ge(s_xn[2][0], g + 1)
                    if g >= 2:
                        pe.wait_ge(s_T[2][0], g - 1)
                    for t in range(GT):
                        i = pe.transpose(PB[4 + g % 2][:, t * P:(t + 1) * P], NX[:, (g * GT + t) * D:(g * GT + t + 1) * D], ident[:, :])
                    i.then_inc(s_tr[2][0], 1)

            pipeline(pe, pe_step, beside)
            for b in range(BATCH):
                if b == 1:
                    transposes(2, b, range(AHEAD))
                for g in range(BG):
                    pe.wait_ge(s_T[2][b], BG if b == 0 else g + 1)
                    k = b * BG + g
                    if k == 2:
                        pe.wait_ge(s_ye, ST_)
                    if k >= 3:
                        pe.wait_ge(s_gs, 2 * (k - 2))
                    for i, w in enumerate(("ig", "ag")):
                        t0 = (b * BG + g) * GW
                        pe.matmul(PB[2 + 2 * (k % 3) + i][:, :], wl(w), T[:, t0:t0 + GW], start=True, stop=True).then_inc(s_gt, 1)
                    if b == 1 and g == 0:
                        transposes(2, b, range(AHEAD, BG))
                for g in range(BG):
                    k = b * BG + g
                    pe.wait_ge(s_h, k + 1)
                    if g >= 2:
                        pe.wait_ge(s_he, k - 1)
                    for t in range(GT):
                        i = pe.transpose(PB[k % 2][:, t * P:(t + 1) * P], G[b][1][:, (g * GT + t) * P:(g * GT + t + 1) * P], ident[:, :])
                    i.then_inc(s_ht, 1)
            pe.wait_ge(s_sc, 2)
            pe.transpose(PB[2][0:TILES, 0:P], sc[:, :], ident[:, :]).then_inc(s_sct, 1)
            pe.wait_ge(s_vd, 1)
            pe.transpose(PB[0][:, 0:P], HN[:, :], ident[:, :]).then_inc(s_pd, 1)
            pe.wait_ge(s_ad, 1)
            pe.matmul(PB[1][:, 0:P], wl("wqkv", 0, D), hT[:, :], start=True, stop=True).then_inc(s_pd, 1)
            pe.matmul(PB[2][:, 0:P], wl("wqkv", D, 2 * D), hT[:, :], start=True, stop=True).then_inc(s_pd, 1)
            pe.matmul(PB[3][:, 0:P], hT[:, :], wl("wqkv", 2 * D, 3 * D), start=True, stop=True).then_inc(s_pd, 1)
            pe.wait_ge(s_vd, 2)
            pe.wait_ge(s_ad, 4)
            for i in range(4):
                pe.matmul(PB[i][:, :], qT[:, :], kM[:, i * 512:(i + 1) * 512], start=True, stop=True).then_inc(s_pd, 1)
            pe.wait_ge(s_ad, 5)
            for i in range(4):
                for h in range(4):
                    k = 4 * i + h
                    m = pe.transpose(PB[i][:, h * P:(h + 1) * P], SM[:, k * P:(k + 1) * P], ident[:, :])
                m.then_inc(s_pd, 1)
            for h in range(AH):
                pe.wait_ge(s_ad, 6 + h // 4)
                m = pe.matmul(PB[4][:, h * HD:(h + 1) * HD], PT[:, h * P:(h + 1) * P], vv[:, h * HD:(h + 1) * HD],
                              start=True, stop=True)
            m.then_inc(s_pd, 1)
            pe.wait_ge(s_vd, 4)
            pe.transpose(PB[5][:, 0:P], O[:, :], ident[:, :]).then_inc(s_pd, 1)
            pe.wait_ge(s_ad, 10)
            pe.matmul(PB[5][:, 0:D], OT[:, :], wl("wo"), start=True, stop=True).then_inc(s_pd, 1)
            pe.wait_ge(s_vd, 5)
            pe.transpose(PB[0][:, 0:P], HN[:, :], ident[:, :]).then_inc(s_pd, 1)
            pe.wait_ge(s_ad, 11)
            at = [0, 128, 256]
            for i in range(3):
                pe.matmul(PB[3][0:FC[i], i * P:(i + 1) * P], wl("w1", at[i], at[i] + FC[i]), hT[:, :], start=True, stop=True)
            for i in range(3):
                m = pe.matmul(PB[4][0:FC[i], i * P:(i + 1) * P], wl("w2", at[i], at[i] + FC[i]), hT[:, :], start=True, stop=True)
            m.then_inc(s_pd, 1)
            for i in range(3):
                pe.wait_ge(s_vd, 6 + i)
                m = pe.matmul(PB[5][:, 0:D], gg[i][0:FC[i], :], wl("w3", i * D, (i + 1) * D, rows=FC[i]),
                              start=(i == 0), stop=(i == 2))
            m.then_inc(s_pd, 1)


def kernel(**inputs):
    import numpy as np
    import concourse.bacc as bacc
    from concourse.bass_utils import run_bass_kernel_spmd

    f = {k: np.asarray(a) for k, a in inputs.items()}

    def rows(a, n=P):
        return np.broadcast_to(a.reshape(1, -1), (n, a.size))

    def pad(a):
        z = np.zeros((P, a.shape[1]), np.float32)
        z[:a.shape[0]] = a
        return z

    def block_diagonal(w):
        n = w.shape[1]
        z = np.zeros((P, P), np.float32)
        for h in range(w.shape[0]):
            z[h * n:(h + 1) * n, h * n:(h + 1) * n] = w[h]
        return z

    win = f["L0_attn_in_proj_w"].T
    conv_w = f["L0_attn_conv_w"].reshape(3, P, TAPS).transpose(1, 0, 2).reshape(P, 12)
    mixer = {
        "win": win, "wout": f["L0_attn_out_w"].T.reshape(2, P, D).transpose(1, 0, 2).reshape(P, 2 * D),
        "conv_w": conv_w, "conv_b": f["L0_attn_conv_b"].reshape(3, P).T, "rms_w": f["L0_attn_rms_w"].reshape(2, P).T,
        "dt_bias": rows(f["L0_attn_dt_bias"]), "a_log": rows(f["L0_attn_A_log"]), "d_skip": rows(f["L0_attn_D"]),
        "a_param": f["L1_attn_a_param"].reshape(P, 1),
    }
    w3 = f["L1_ffn_W3"].T
    row_expert = np.full((P, 1), -1, np.float32)
    row_chunk = np.zeros((P, HC), np.float32)
    for low in (0, 64):
        for c in range(HC):
            row_expert[low + c * E:low + (c + 1) * E, 0] = np.arange(E)
            row_chunk[low + c * E:low + (c + 1) * E, c] = 1
    down = np.zeros((HC * E, D), np.float32)
    down[:E] = f["L0_ffn_bdown"]
    later = {
        "row_expert": row_expert, "row_chunk": row_chunk, "gate": f["L0_ffn_Wg"], "ig": block_diagonal(f["L1_attn_ig_w"]), "ag": block_diagonal(f["L1_attn_ag_w"]),
        "ig_b": f["L1_attn_ig_b"].reshape(P, 1), "ag_b": f["L1_attn_ag_b"].reshape(P, 1),
        "router": rows(f["L1_ffn_w_router"]), "wqkv": f["L1_ffn_W_qkv"].T, "wo": f["L1_ffn_W_out"].T,
        "g1": f["L1_ffn_g1"].reshape(P, 1), "g2": f["L1_ffn_g2"].reshape(P, 1),
        "w1": f["L1_ffn_W1"].T, "w2": f["L1_ffn_W2"].T,
        "w3": np.concatenate([pad(w3[128 * i:128 * i + n]) for i, n in enumerate(FC)], axis=1),
    }
    arrays = {
        "u": f["L0_attn_u"].reshape(TOKENS, D),
        "mixer_w": np.concatenate([mixer[n] for n, _ in MIXER_COLS], axis=1),
        "later_w": np.concatenate([later[n] for n, _ in LATER_COLS], axis=1),
        "wup": f["L0_ffn_Wup"],
        "wdown": f["L0_ffn_Wdown"].reshape(E, HC, P, D).transpose(0, 2, 1, 3).reshape(E, P, HC * D),
        "biases": np.concatenate([f["L0_ffn_bup"].reshape(E, HC, P).transpose(1, 0, 2).reshape(HC * E, P), down], axis=1),
    }
    arrays = {k: np.ascontiguousarray(a) for k, a in arrays.items()}
    nc = bacc.Bacc("TRN2", target_bir_lowering=False, num_devices=1)
    args = [nc.dram_tensor(k, a.shape, F32, kind="ExternalInput").ap() for k, a in arrays.items()]
    out = nc.dram_tensor("out", (TOKENS, D), F32, kind="ExternalOutput").ap()
    build(nc, *args, out)
    r = run_bass_kernel_spmd(nc, [arrays], core_ids=[0])
    return r.results[0]["out"].reshape(BATCH, SEQ, D)
```
